# Optimizing a Trainium2 kernel written in Bass

```python
import numpy as np
import jax
import jax.numpy as jnp

def _softmax(x, axis=-1):
    return jax.nn.softmax(x, axis=axis)

def _gelu(x):
    return jax.nn.gelu(x, approximate=True)

def _silu(x):
    return jax.nn.silu(x)

def _sigmoid(x):
    return jax.nn.sigmoid(x)

def _layernorm(x, axis=-1, eps=1e-05):
    m = jnp.mean(x, axis=axis, keepdims=True)
    v = jnp.var(x, axis=axis, keepdims=True)
    return (x - m) / jnp.sqrt(v + eps)

def _scatter_add(tgt, idx, src, axis=0):
    return tgt.at[idx].add(src)

def _segment_sum(src, seg, n):
    return jax.ops.segment_sum(src, seg, n)
kernel_name = 'mk_adaln_d1_jaxref_r2_1c199f'

def setup_inputs(seed: int=0):
    np.random.seed(seed)
    _w = jnp.asarray

    def _L0_attn_setup():
        import jax, jax.numpy as jnp
        import numpy as np
        B, S, DM, H, DH = (2, 1024, 512, 16, 64)
        HID = H * DH

        def _xavier(key, shape):
            fan_out, fan_in = shape
            lim = float(np.sqrt(6.0 / (fan_in + fan_out)))
            return jax.random.uniform(key, shape, jnp.float32, -lim, lim)

        def _gla_scan(q, k, v, g):
            qt = jnp.moveaxis(q, 1, 0)
            kt = jnp.moveaxis(k, 1, 0)
            vt = jnp.moveaxis(v, 1, 0)
            gt = jnp.moveaxis(g, 1, 0)

            def step(s, inp):
                qi, ki, vi, gi = inp
                s = jnp.exp(gi)[:, :, None, None] * s + ki[..., :, None] * vi[..., None, :]
                o = jnp.einsum('bhk,bhkv->bhv', qi, s)
                return (s, o)
            s0 = jnp.zeros(q.shape[0:1] + q.shape[2:] + q.shape[-1:], q.dtype)
            _, o = jax.lax.scan(step, s0, (qt, kt, vt, gt))
            return jnp.moveaxis(o, 0, 1)
        key = jax.random.key(seed)
        ks = jax.random.split(key, 8)
        return {'x': jax.random.normal(ks[0], (B, S, DM), jnp.float32), 'Wq': _xavier(ks[1], (HID, DM)), 'Wk': _xavier(ks[2], (HID, DM)), 'Wv': _xavier(ks[3], (HID, DM)), 'Wo': _xavier(ks[4], (DM, HID)), 'Wg': _xavier(ks[5], (HID, DM)), 'Wog': _xavier(ks[6], (HID, DM)), 'Wd': _xavier(ks[7], (H, DM)), 'bd': jnp.full((H,), -2.0, jnp.float32), 'norm_w': jnp.ones((HID,), jnp.float32)}
    _L0_attn_in = _L0_attn_setup()

    def _L0_ffn_setup():
        import jax, jax.numpy as jnp
        import numpy as np
        DIM = 512

        def _reference_tuple_inner(x, W_r, W_k, W_v, mu_r, mu_k):
            B, T, C = x.shape
            x_prev = jnp.concatenate([jnp.zeros((B, 1, C), x.dtype), x[:, :-1, :]], axis=1)
            xr = mu_r * x + (1.0 - mu_r) * x_prev
            xk = mu_k * x + (1.0 - mu_k) * x_prev
            r = jax.nn.sigmoid(jnp.einsum('btc,dc->btd', xr, W_r))
            k = jnp.einsum('btc,dc->btd', xk, W_k)
            k_act = jnp.square(jax.nn.relu(k))
            out = r * jnp.einsum('btc,dc->btd', k_act, W_v)
            new_state = x[:, -1, :]
            return (out, new_state)
        key = jax.random.key(seed)
        ks = jax.random.split(key, 6)
        B, T, C = (8, 1024, DIM)
        x = jax.random.normal(ks[0], (B, T, C), dtype=jnp.float32)
        s = 1.0 / np.sqrt(C)
        W_r = jax.random.uniform(ks[1], (C, C), jnp.float32, -s, s)
        W_k = jax.random.uniform(ks[2], (C, C), jnp.float32, -s, s)
        W_v = jax.random.uniform(ks[3], (C, C), jnp.float32, -s, s)
        mu_r = jax.random.uniform(ks[4], (C,), jnp.float32)
        mu_k = jax.random.uniform(ks[5], (C,), jnp.float32)
        return {'x': x, 'W_r': W_r, 'W_k': W_k, 'W_v': W_v, 'mu_r': mu_r, 'mu_k': mu_k}
    _L0_ffn_in = _L0_ffn_setup()
    _L0_c = _w((lambda *s: np.random.randn(*s).astype(np.float32) * 0.05)(1, 512))
    _L0_wmod = _w((lambda *s: np.random.randn(*s).astype(np.float32) * 0.05)(512, 6 * 512) * 512 ** (-0.5))
    _d = {'L0_attn_x': _L0_attn_in['x'], 'L0_attn_Wq': _L0_attn_in['Wq'], 'L0_attn_Wk': _L0_attn_in['Wk'], 'L0_attn_Wv': _L0_attn_in['Wv'], 'L0_attn_Wo': _L0_attn_in['Wo'], 'L0_attn_Wg': _L0_attn_in['Wg'], 'L0_attn_Wog': _L0_attn_in['Wog'], 'L0_attn_Wd': _L0_attn_in['Wd'], 'L0_attn_bd': _L0_attn_in['bd'], 'L0_attn_norm_w': _L0_attn_in['norm_w'], 'L0_ffn_W_r': _L0_ffn_in['W_r'], 'L0_ffn_W_k': _L0_ffn_in['W_k'], 'L0_ffn_W_v': _L0_ffn_in['W_v'], 'L0_ffn_mu_r': _L0_ffn_in['mu_r'], 'L0_ffn_mu_k': _L0_ffn_in['mu_k'], 'L0_c': _L0_c, 'L0_wmod': _L0_wmod}
    _x0 = _d['L0_attn_x']
    _d['L0_attn_x'] = jax.random.normal(jax.random.fold_in(jax.random.key(seed), 1), (1, 8192, 512), dtype=_x0.dtype)
    del _x0
    return _d

def reference(L0_attn_x, L0_attn_Wq, L0_attn_Wk, L0_attn_Wv, L0_attn_Wo, L0_attn_Wg, L0_attn_Wog, L0_attn_Wd, L0_attn_bd, L0_attn_norm_w, L0_ffn_W_r, L0_ffn_W_k, L0_ffn_W_v, L0_ffn_mu_r, L0_ffn_mu_k, L0_c, L0_wmod):

    def _L0_attn_ref(x, Wq, Wk, Wv, Wo, Wg, Wog, Wd, bd, norm_w):
        import jax, jax.numpy as jnp
        import numpy as np
        B, S, DM, H, DH = (2, 1024, 512, 16, 64)
        HID = H * DH

        def _xavier(key, shape):
            fan_out, fan_in = shape
            lim = float(np.sqrt(6.0 / (fan_in + fan_out)))
            return jax.random.uniform(key, shape, jnp.float32, -lim, lim)

        def _gla_scan(q, k, v, g):
            qt = jnp.moveaxis(q, 1, 0)
            kt = jnp.moveaxis(k, 1, 0)
            vt = jnp.moveaxis(v, 1, 0)
            gt = jnp.moveaxis(g, 1, 0)

            def step(s, inp):
                qi, ki, vi, gi = inp
                s = jnp.exp(gi)[:, :, None, None] * s + ki[..., :, None] * vi[..., None, :]
                o = jnp.einsum('bhk,bhkv->bhv', qi, s)
                return (s, o)
            s0 = jnp.zeros(q.shape[0:1] + q.shape[2:] + q.shape[-1:], q.dtype)
            _, o = jax.lax.scan(step, s0, (qt, kt, vt, gt))
            return jnp.moveaxis(o, 0, 1)
        b, s, _ = x.shape
        q = (x @ Wq.T).reshape(b, s, H, DH)
        k = (x @ Wk.T).reshape(b, s, H, DH)
        v = (x @ Wv.T).reshape(b, s, H, DH)
        log_decay = -jax.nn.softplus(x @ Wd.T + bd)
        gate = jax.nn.sigmoid((x @ Wg.T).reshape(b, s, H, DH))
        k_gated = k * gate
        out = _gla_scan(q, k_gated, v, log_decay)
        out = out.reshape(b, s, HID)
        eps = jnp.finfo(out.dtype).eps
        out = out * jax.lax.rsqrt(jnp.mean(out * out, -1, keepdims=True) + eps) * norm_w
        out = out * jax.nn.sigmoid(x @ Wog.T)
        return out @ Wo.T

    def _L0_ffn_ref(x, W_r, W_k, W_v, mu_r, mu_k):
        import jax, jax.numpy as jnp
        import numpy as np
        DIM = 512

        def _reference_tuple_inner(x, W_r, W_k, W_v, mu_r, mu_k):
            B, T, C = x.shape
            x_prev = jnp.concatenate([jnp.zeros((B, 1, C), x.dtype), x[:, :-1, :]], axis=1)
            xr = mu_r * x + (1.0 - mu_r) * x_prev
            xk = mu_k * x + (1.0 - mu_k) * x_prev
            r = jax.nn.sigmoid(jnp.einsum('btc,dc->btd', xr, W_r))
            k = jnp.einsum('btc,dc->btd', xk, W_k)
            k_act = jnp.square(jax.nn.relu(k))
            out = r * jnp.einsum('btc,dc->btd', k_act, W_v)
            new_state = x[:, -1, :]
            return (out, new_state)
        return _reference_tuple_inner(x, W_r, W_k, W_v, mu_r, mu_k)[0]
    x = L0_attn_x
    mod = (_silu(L0_c) @ L0_wmod).reshape(L0_c.shape[0], 6, 1, -1)
    sa, ca, ga, sb, cb, gb = (mod[:, 0], mod[:, 1], mod[:, 2], mod[:, 3], mod[:, 4], mod[:, 5])
    ga = (2 * (ga >= 0) - 1) * jnp.maximum(jnp.abs(ga), 0.25)
    gb = (2 * (gb >= 0) - 1) * jnp.maximum(jnp.abs(gb), 0.25)
    h = _layernorm(x, axis=-1) * (1 + ca) + sa
    x = x + ga * _L0_attn_ref(h, L0_attn_Wq, L0_attn_Wk, L0_attn_Wv, L0_attn_Wo, L0_attn_Wg, L0_attn_Wog, L0_attn_Wd, L0_attn_bd, L0_attn_norm_w)
    h = _layernorm(x, axis=-1) * (1 + cb) + sb
    x = x + gb * _L0_ffn_ref(h, L0_ffn_W_r, L0_ffn_W_k, L0_ffn_W_v, L0_ffn_mu_r, L0_ffn_mu_k)
    return x

_drawn_inputs = setup_inputs


def setup_inputs(seed=0):
    import zlib

    import numpy as np

    out = dict(_drawn_inputs(seed))
    spreads = {'L0_attn_bd': (-2.0, 0.547), 'L0_attn_norm_w': (1.0, 0.2)}
    factors = {'L0_ffn_W_r': 8.0,
     'L0_ffn_W_k': 3.076,
     'L0_ffn_W_v': 2.798,
     'L0_ffn_mu_r': 8.0,
     'L0_ffn_mu_k': 5.085}
    for name, (base, spread) in spreads.items():
        noise = np.random.default_rng([zlib.crc32(name.encode()), seed]).standard_normal(out[name].shape)
        drawn = base * np.exp(spread * noise) if base else spread * noise
        out[name] = jnp.asarray(drawn.astype(out[name].dtype))
    for name, factor in factors.items():
        out[name] = (out[name] * factor).astype(out[name].dtype)
    return out
```

```python
from contextlib import ExitStack

import concourse.bass as bass
from concourse import mybir

F32 = mybir.dt.float32
F32R = mybir.dt.float32r
BF16 = mybir.dt.bfloat16
ALU = mybir.AluOpType
ACT = mybir.ActivationFunctionType

P = 128
DM = 512
HID = 1024
H = 16
DH = HID // H
TOK = 8192
CH = 128
NC = 2
T = NC * CH
NT = TOK // T
KD = DM // P
NP = HID // P
LN_EPS = 1e-5
RMS_EPS = 1.1920928955078125e-07
SA, CA, GA, SB, CB, GB = range(6)


def hold(eng, sem, value):
    if isinstance(value, int) and value <= 0:
        return
    eng.wait_ge(sem, value)


def signals(nc, ctx, prefix, names):
    return {n: ctx.enter_context(nc.semaphore(f"{prefix}_{n}")) for n in names.split()}


def three_passes(nc, out, w_hi, w_lo, x_hi, x_lo, first, last):
    nc.tensor.matmul(out, w_hi, x_hi, start=first, stop=False)
    nc.tensor.matmul(out, w_hi, x_lo, start=False, stop=False)
    return nc.tensor.matmul(out, w_lo, x_hi, start=False, stop=last)


def prepare_constants(nc, t, small, wmod, wd):
    with ExitStack() as ctx:
        stage = [ctx.enter_context(nc.sbuf_tensor(f"mod_stage{n}", [P, KD, DM], F32)) for n in range(3)]
        wd_rows = ctx.enter_context(nc.sbuf_tensor("wd_rows", [H, DM], F32))
        vec_rows = ctx.enter_context(nc.sbuf_tensor("vec_rows", [2 * KD + NP, P], F32))
        c_col = ctx.enter_context(nc.sbuf_tensor("c_col", [P, KD], F32))
        silu = ctx.enter_context(nc.sbuf_tensor("silu", [P, 3, KD], F32))
        sign = ctx.enter_context(nc.sbuf_tensor("sign", [P, 4, KD], F32))
        mod_ps = ctx.enter_context(nc.psum_tensor("mod_ps", [P, 512], F32))
        wd_ps = ctx.enter_context(nc.psum_tensor("wd_ps", [P, 512], F32))
        s = signals(nc, ctx, "c", "small stage used filled masks exp silu mod wd wd_hi mu dve")
        stage_sem = [ctx.enter_context(nc.semaphore(f"c_stage{n}")) for n in range(3)]
        block = ctx.enter_context(nc.Block())

        @block.sync
        def _(sp):
            sp.dma_start(c_col[:, :], small["c"].rearrange("a (p t) -> (a p) t", t=KD)).then_inc(s["small"], 16)
            sp.dma_start(wd_rows[:, :], wd).then_inc(s["small"], 16)
            for name, r0, n in (("mu_r", 0, KD), ("mu_k", KD, KD), ("norm_w", 2 * KD, NP)):
                sp.dma_start(vec_rows[r0:r0 + n, :], small[name].rearrange("(t p) -> t p", p=P)).then_inc(s["small"], 16)
            sp.dma_start(t["bd"][:, :], small["bd"].rearrange("(h a) -> h a", a=1)).then_inc(s["small"], 16)
            wv = wmod.rearrange("(p t) (v n) -> v p t n", t=KD, v=6)
            for v in range(6):
                if v >= 3:
                    sp.wait_ge(s["used"], v - 2)
                sp.dma_start(stage[v % 3][:, :, :], wv[v]).then_inc(stage_sem[v % 3], 16)
            sp.wait_ge(s["small"], 16 * 6)

        @block.gpsimd
        def _(pool):
            pool.wait_ge(s["filled"], 1)
            one = t["ones"][:, :]
            nc.gpsimd.affine_select(out=t["ident"][:, :], in_=one, compare_op=ALU.is_equal, fill=0.0, base=0,
                                    pattern=[[-1, P]], channel_multiplier=1)
            nc.gpsimd.affine_select(out=t["upto"][:, :], in_=one, compare_op=ALU.is_ge, fill=0.0, base=0,
                                    pattern=[[1, P]], channel_multiplier=-1)
            nc.gpsimd.affine_select(out=t["after"][:, :], in_=one, compare_op=ALU.is_gt, fill=0.0, base=0,
                                    pattern=[[-1, P]], channel_multiplier=1).then_inc(s["masks"], 1)

        @block.scalar
        def _(act):
            act.wait_ge(s["small"], 16 * 6)
            nc.scalar.activation(silu[:, 0, :], c_col[:, :], ACT.Exp, scale=-1.0).then_inc(s["exp"], 1)

        @block.vector
        def _(dve):
            nc.vector.memset(t["ones"][:, :], 1.0).then_inc(s["filled"], 1)
            nc.vector.memset(t["minus_half"][:, :], -0.5)
            nc.vector.memset(t["zeros"][:, :], 0.0)
            dve.wait_ge(s["exp"], 1)
            nc.vector.tensor_scalar(silu[:, 1, :], silu[:, 0, :], 1.0, None, ALU.add).then_inc(s["dve"], 1)
            dve.wait_ge(s["dve"], 1)
            nc.vector.reciprocal(silu[:, 2, :], silu[:, 1, :]).then_inc(s["dve"], 1)
            dve.wait_ge(s["dve"], 2)
            nc.vector.tensor_tensor(t["silu_c"][:, :], c_col[:, :], silu[:, 2, :], ALU.mult).then_inc(s["silu"], 1)
            dve.wait_ge(s["masks"], 1)
            nc.vector.tensor_copy(t["after_r"][:, :], t["after"][:, :])
            dve.wait_ge(s["wd"], 1)
            wd_t = wd_ps[:, 0:KD * H].rearrange("p (k h) -> p k h", k=KD)
            nc.vector.tensor_copy(t["wd_hi"][:, :, :], wd_t).then_inc(s["wd_hi"], 1)
            dve.wait_ge(s["wd_hi"], 1)
            nc.vector.tensor_tensor(t["wd_lo"][:, :, :], wd_t, t["wd_hi"][:, :, :].bitcast(F32), ALU.subtract)
            vecs = wd_ps[:, KD * H:KD * H + 2 * KD + NP]
            nc.vector.tensor_copy(t["mu"][:, :, :], vecs[:, 0:2 * KD].rearrange("p (m k) -> p m k", m=2)).then_inc(s["mu"], 1)
            nc.vector.tensor_copy(t["norm_w"][:, :], vecs[:, 2 * KD:])
            dve.wait_ge(s["mod"], 6)
            nc.vector.tensor_copy(t["mod"][:, :, :], mod_ps[:, 0:6 * KD].rearrange("p (v k) -> p v k", v=6)).then_inc(s["dve"], 1)
            dve.wait_ge(s["dve"], 3)
            n = 3
            for v, scale in ((CA, "ca1"), (CB, "cb1")):
                nc.vector.tensor_scalar(t[scale][:, :], t["mod"][:, v, :], 1.0, None, ALU.add)
            for v, gate in ((GA, "ga"), (GB, "gb")):
                g = t["mod"][:, v, :]
                nc.vector.tensor_scalar(sign[:, 0, :], g, 0.0, 2.0, ALU.is_ge, ALU.mult)
                nc.vector.scalar_tensor_tensor(out=sign[:, 1, :], in0=g, scalar=-1.0, in1=g, op0=ALU.mult,
                                               op1=ALU.max).then_inc(s["dve"], 1)
                dve.wait_ge(s["dve"], n + 1)
                nc.vector.tensor_scalar(sign[:, 2, :], sign[:, 1, :], 0.25, None, ALU.max)
                nc.vector.tensor_scalar(sign[:, 3, :], sign[:, 0, :], -1.0, None, ALU.add).then_inc(s["dve"], 1)
                dve.wait_ge(s["dve"], n + 2)
                nc.vector.tensor_tensor(t[gate][:, :], sign[:, 2, :], sign[:, 3, :], ALU.mult).then_inc(s["dve"], 1)
                dve.wait_ge(s["dve"], n + 3)
                n += 3
            dve.wait_ge(s["mu"], 1)
            nc.vector.tensor_scalar(t["one_minus_mu"][:, :, :], t["mu"][:, :, :], -1.0, 1.0, ALU.mult, ALU.add)

        @block.tensor
        def _(pe):
            pe.wait_ge(s["masks"], 1)
            pe.wait_ge(s["small"], 16 * 6)
            for k in range(KD):
                last = nc.tensor.transpose(wd_ps[:, k * H:(k + 1) * H], wd_rows[:, k * P:(k + 1) * P],
                                           t["ident"][0:H, 0:H])
            NV = 2 * KD + NP
            last = nc.tensor.transpose(wd_ps[:, KD * H:KD * H + NV], vec_rows[:, :], t["ident"][0:NV, 0:NV])
            last.then_inc(s["wd"], 1)
            pe.wait_ge(s["silu"], 1)
            for v in range(6):
                pe.wait_ge(stage_sem[v % 3], 16 * (v // 3 + 1))
                for b in range(KD):
                    for k in range(KD):
                        last = nc.tensor.matmul(mod_ps[:, v * KD + b:v * KD + b + 1],
                                                stage[v % 3][:, k, b * P:(b + 1) * P],
                                                t["silu_c"][:, k:k + 1], start=(k == 0), stop=(k == KD - 1))
                last.then_inc(s["mod"], 1)
                if v < 3:
                    pe.wait_ge(s["mod"], v + 1)
                    pe.sem_inc(s["used"], 1)


def prepare_weights(nc, ident, jobs, name):
    with ExitStack() as ctx:
        stage = [ctx.enter_context(nc.sbuf_tensor(f"{name}_stage{n}", [P, 4, 512], F32)) for n in range(2)]
        scaled = ctx.enter_context(nc.sbuf_tensor(f"{name}_scaled", [P, 4, 512], F32))
        bank = [ctx.enter_context(nc.psum_tensor(f"{name}_ps{n}", [P, 512], F32)) for n in range(4)]
        s = signals(nc, ctx, name, "turned hi lo scaled")
        loaded = [ctx.enter_context(nc.semaphore(f"{name}_loaded{n}")) for n in range(2)]
        block = ctx.enter_context(nc.Block())
        scaled_before = [sum(1 for _, r, _ in jobs[:n] if r is not None) for n in range(len(jobs) + 1)]

        @block.sync
        def _(sp):
            for n, (rows, _, _) in enumerate(jobs):
                if n >= 2:
                    sp.wait_ge(s["turned"], 4 * (n - 1))
                    hold(sp, s["scaled"], scaled_before[n - 1])
                sp.dma_start(stage[n % 2][:, :, :], rows).then_inc(loaded[n % 2], 16)

        @block.tensor
        def _(pe):
            for n, (_, row_scale, cols) in enumerate(jobs):
                if row_scale is None:
                    pe.wait_ge(loaded[n % 2], 16 * (n // 2 + 1))
                    src = stage[n % 2]
                else:
                    pe.wait_ge(s["scaled"], scaled_before[n + 1])
                    src = scaled
                for k in range(4):
                    m = 4 * n + k
                    if m >= 4:
                        pe.wait_ge(s["lo"], m - 3)
                    for r in range(4):
                        last = nc.tensor.transpose(bank[m % 4][:, r * P:(r + 1) * P], src[:, r, k * P:(k + 1) * P],
                                                   ident[:, :])
                    last.then_inc(s["turned"], 1)

        @block.gpsimd
        def _(pool):
            for n, (_, row_scale, _) in enumerate(jobs):
                if row_scale is not None:
                    pool.wait_ge(loaded[n % 2], 16 * (n // 2 + 1))
                    hold(pool, s["turned"], 4 * n)
                    for r in range(4):
                        last = nc.gpsimd.tensor_scalar(scaled[:, r, :], stage[n % 2][:, r, :], row_scale[:, r:r + 1],
                                                       1.0, ALU.mult, ALU.mult)
                    last.then_inc(s["scaled"], 1)

        @block.scalar
        def _(act):
            for n, (_, _, cols) in enumerate(jobs):
                for k, (hi, _, col_scale) in enumerate(cols):
                    m = 4 * n + k
                    act.wait_ge(s["turned"], m + 1)
                    if col_scale is None:
                        nc.scalar.copy(hi, bank[m % 4][:, :]).then_inc(s["hi"], 1)
                    else:
                        nc.scalar.activation(hi, bank[m % 4][:, :], ACT.Copy, scale=col_scale).then_inc(s["hi"], 1)

        @block.vector
        def _(dve):
            for n, (_, _, cols) in enumerate(jobs):
                for k, (hi, lo, col_scale) in enumerate(cols):
                    m = 4 * n + k
                    dve.wait_ge(s["hi"], m + 1)
                    if col_scale is None:
                        nc.vector.tensor_tensor(lo, bank[m % 4][:, :], hi.bitcast(F32), ALU.subtract).then_inc(s["lo"], 1)
                    else:
                        nc.vector.scalar_tensor_tensor(out=lo, in0=bank[m % 4][:, :], scalar=col_scale,
                                                       in1=hi.bitcast(F32), op0=ALU.mult,
                                                       op1=ALU.subtract).then_inc(s["lo"], 1)


KINDS = "gqk"
USES = [(kind, b) for b in range(4) for kind in KINDS] + [("v", 0), ("v", 1)]
USES += [(kind, b) for b in range(4, NP) for kind in KINDS] + [("v", 2), ("v", 3)]
BY_ACT = [u for u in USES if u[0] != "k"]
NU, NA = len(USES), len(BY_ACT)


def attention_pass(nc, t, W, x_v, o_v):
    with ExitStack() as ctx:
        def sb(name, shape, dt=F32):
            return ctx.enter_context(nc.sbuf_tensor(name, shape, dt))

        def ps(name, shape):
            return ctx.enter_context(nc.psum_tensor(name, shape, F32))

        x = sb("x", [P, NC, DM])
        hT = sb("hT", [P, KD, T])
        h_hi = sb("h_hi", [P, KD, T], F32R)
        h_lo = sb("h_lo", [P, KD, T], F32R)
        q = sb("q", [P, NP, T])
        kg = sb("kg", [P, NP, T])
        kpad = sb("kpad", [P, 2, T])
        v = sb("v", [P, NC, HID])
        o = sb("o", [P, 2, NC, P])
        decay = sb("decay", [P, 4, CH])
        prob = sb("prob", [P, 4, CH])
        r_hi = sb("r_hi", [P, NC, 2, CH], F32R)
        r_lo = sb("r_lo", [P, NC, 2, CH], F32R)
        state = sb("state", [P, NP, P])
        mid = sb("mid", [P, P])
        kw = sb("kw", [P, NC, P])
        inter = sb("inter", [P, NC, P])
        gate = sb("gate", [P, 3, T])
        stats = sb("stats", [P, NC, 6])
        mv = sb("mv", [P, NC, 2])
        var_eps = sb("var_eps", [P, NC])
        rstd = sb("rstd", [P, NC])
        zt = sb("zt", [H, 5, T])
        g_raw = sb("g_raw", [P, NC * H])
        g_hi = sb("g_hi", [P, NC * H], F32R)
        g_lo = sb("g_lo", [P, NC * H], F32R)
        w_new = sb("w_new", [P, 3, NC * H])
        w_cur = sb("w_cur", [P, 3, NC, H])

        tick = sb("tick", [P, 2])

        psA = ps("psA", [P, 4, CH])
        psS = ps("psS", [P, 4, CH])
        psK = ps("psK", [P, 4, P])
        psO = ps("psO", [P, 4, P])
        psJ = [ps(f"psJ{n}", [P, 512]) for n in range(2)]
        psT = ps("psT", [P, KD, T])
        psZ = psT[0:H, 0, :]
        psG = psT[:, 1, 0:NC * H]
        psC = psT[:, 1, NC * H:4 * NC * H]

        s = signals(nc, ctx, "a", "x stats mv var_eps rstd xn xT hT h_hi h_lo z zb softin e1 l soft gT g_turned g_raw cum w_new g_hi g cur "
                 "proj by_act k gate1 gate2 r a e mask kpad score prob kT kw inc mid state pv gla inter o zero")
        store = [ctx.enter_context(nc.semaphore(f"a_store{n}")) for n in range(2)]
        block = ctx.enter_context(nc.Block())

        def evacuated(eng, i, u):
            if u < 0:
                i, u = i - 1, u + NU
                if isinstance(i, int) and i < 0:
                    return
            kind, b = USES[u]
            if kind == "k":
                hold(eng, s["k"], NP * i + b + 1)
            else:
                hold(eng, s["by_act"], NA * i + BY_ACT.index(USES[u]) + 1)

        def proj_done(i, use):
            return NU * i + USES.index(use) + 1

        def act_done(i, use):
            return NA * i + BY_ACT.index(use) + 1

        def sp_tile(sp, i, gla, proj, prep):
            j = i - 1
            if prep:
                hold(sp, s["xT"], KD * (i + 1))
                sp.dma_start(x[:, :, :], x_v[i + 1]).then_inc(s["x"], 16)
            if gla:
                for p in range(NP):
                    sp.wait_ge(s["o"], NP * j + p + 1)
                    sp.dma_start(o_v[j, :, :, p * P:(p + 1) * P], o[:, p % 2, :, :]).then_inc(store[p % 2], 16)

        @block.sync
        def _(sp):
            sp.dma_start(x[:, :, :], x_v[0]).then_inc(s["x"], 16)
            sp_tile(sp, 0, False, True, True)
            sp_tile(sp, 1, True, True, True)
            with sp.Fori(2, NT - 1) as i:
                sp_tile(sp, i, True, True, True)
            sp_tile(sp, NT - 1, True, True, False)
            sp_tile(sp, NT, True, False, False)
            for n in range(2):
                sp.wait_ge(store[n], 16 * NP // 2 * NT)

        def project(i, kind, b, pe):
            u = USES.index((kind, b))
            bank = psJ[u % 2]
            if u == 0:
                pe.wait_ge(s["h_lo"], i + 1)
            evacuated(pe, i, u - 2)
            for k in range(KD):
                if kind == "v":
                    c, half = b % 2, b // 2
                    hh, hl = (a[:, k, c * CH:(c + 1) * CH] for a in (h_hi, h_lo))
                    wh, wl = (a[:, k, half * 512:(half + 1) * 512] for a in W["v"])
                    last = three_passes(nc, bank[:, :], hh, hl, wh, wl, k == 0, k == KD - 1)
                else:
                    wh, wl = (a[:, k, b * P:(b + 1) * P] for a in W[kind])
                    last = three_passes(nc, bank[:, 0:T], wh, wl, h_hi[:, k, :], h_lo[:, k, :], k == 0, k == KD - 1)
            last.then_inc(s["proj"], 1)

        def turn_x(pe, n):
            pe.wait_ge(s["xn"], NC * (n + 1))
            hold(pe, s["hT"], KD * n)
            hold(pe, s["w_new"], n)
            for k in range(KD):
                for c in range(NC):
                    last = nc.tensor.transpose(psT[:, k, c * CH:(c + 1) * CH], x[:, c, k * P:(k + 1) * P],
                                               t["ident"][:, :])
                last.then_inc(s["xT"], 1)

        def pe_tile(pe, i, gla, proj, prep):
            j = i - 1
            for p in range(NP):
                n = NP * j + p
                if gla:
                    pe.wait_ge(s["r"], n + 1)
                    hold(pe, s["e"], n)
                    nc.tensor.matmul(psA[:, :, :], t["after_r"][:, :], r_hi[:, :, :, :], start=True, stop=False)
                    nc.tensor.matmul(psA[:, :, :], t["after_r"][:, :], r_lo[:, :, :, :], start=False,
                                     stop=True).then_inc(s["a"], 1)
                    pe.wait_ge(s["kpad"], n + 1)
                    hold(pe, s["prob"], n)
                    for c in range(NC):
                        for h in range(2):
                            last = nc.tensor.matmul(psS[:, 2 * c + h, :], kpad[:, h, c * CH:(c + 1) * CH],
                                                    q[:, p, c * CH:(c + 1) * CH], start=True, stop=True)
                    last.then_inc(s["score"], 1)
                    hold(pe, s["mid"], n)
                    hold(pe, s["state"], n)
                    for c in range(NC):
                        last = nc.tensor.transpose(psK[:, c, :], kg[:, p, c * CH:(c + 1) * CH], t["ident"][:, :])
                    last.then_inc(s["kT"], 1)
                if p == 0 and gla:
                    project(j, "v", 2, pe)
                if p > 0 and proj:
                    project(i, "g", p - 1, pe)
                if gla:
                    pe.wait_ge(s["kw"], n + 1)
                    pe.wait_ge(s["by_act"], act_done(j, ("v", 1 + 2 * (p // 4))) if p else act_done(j, ("v", 1)))
                    for c in range(NC):
                        last = nc.tensor.matmul(psK[:, 2 + c, :], kw[:, c, :], v[:, c, p * P:(p + 1) * P],
                                                start=True, stop=True)
                    last.then_inc(s["inc"], 1)
                    pe.wait_ge(s["prob"], n + 1)
                    hold(pe, s["o"], n)
                    for c in range(NC):
                        for h in range(2):
                            nc.tensor.matmul(psO[:, c, h * DH:(h + 1) * DH], prob[:, 2 * c + h, :],
                                             v[:, c, p * P + h * DH:p * P + (h + 1) * DH], start=True, stop=True)
                    nc.tensor.matmul(psO[:, 2, :], q[:, p, 0:CH], state[:, p, :], start=True,
                                     stop=True).then_inc(s["pv"], 1)
                if p == 0 and gla:
                    project(j, "v", 3, pe)
                if p > 0 and proj:
                    project(i, "q", p - 1, pe)
                    if p == 4:
                        pe.wait_ge(s["gT"], i + 1)
                    project(i, "k", p - 1, pe)
                if gla:
                    pe.wait_ge(s["mid"], n + 1)
                    nc.tensor.matmul(psO[:, 3, :], q[:, p, CH:T], mid[:, :], start=True, stop=True).then_inc(s["gla"], 1)
                if p == 1 and proj:
                    for k in range(KD):
                        last = three_passes(nc, psZ, t["wd_hi"][:, k, :], t["wd_lo"][:, k, :], h_hi[:, k, :],
                                            h_lo[:, k, :], k == 0, k == KD - 1)
                    last.then_inc(s["z"], 1)
                if p == 4 and proj:
                    for c in range(NC):
                        last = nc.tensor.transpose(psG[:, c * H:(c + 1) * H], zt[:, 4, c * CH:(c + 1) * CH],
                                                   t["ident"][0:H, 0:H])
                    last.then_inc(s["g_turned"], 1)
                if p == 5 and proj:
                    pe.wait_ge(s["g_raw"], i + 1)
                    for n3, m in enumerate(("upto", "after", "ones")):
                        last = nc.tensor.matmul(psC[:, n3 * NC * H:(n3 + 1) * NC * H], t[m][:, :], g_raw[:, :],
                                                start=True, stop=True)
                    last.then_inc(s["cum"], 1)
                if p == 4 and proj:
                    project(i, "v", 0, pe)
                    project(i, "v", 1, pe)
                if p == 6 and prep:
                    turn_x(pe, i + 1)
            if proj:
                for kind in KINDS:
                    project(i, kind, NP - 1, pe)

        @block.tensor
        def _(pe):
            turn_x(pe, 0)
            pe_tile(pe, 0, False, True, True)
            pe_tile(pe, 1, True, True, True)
            with pe.Fori(2, NT - 1) as i:
                pe_tile(pe, i, True, True, True)
            pe_tile(pe, NT - 1, True, True, False)
            pe_tile(pe, NT, True, False, False)

        def affine_h(act, n):
            hold(act, s["h_lo"], n)
            for k in range(KD):
                act.wait_ge(s["xT"], KD * n + 2 * (k // 2) + 2)
                nc.scalar.activation(hT[:, k, :], psT[:, k, :], ACT.Identity, bias=t["mod"][:, SA, k:k + 1],
                                     scale=t["ca1"][:, k:k + 1]).then_inc(s["hT"], 1)

        def copy_v(act, i, b):
            c, half = b % 2, b // 2
            act.wait_ge(s["proj"], proj_done(i, ("v", b)))
            hold(act, s["gla"], NP * (i - 1) + 4 * (half + 1))
            nc.scalar.copy(v[:, c, half * 512:(half + 1) * 512],
                           psJ[USES.index(("v", b)) % 2][:, :]).then_inc(s["by_act"], 1)

        def copy_qg(act, i, b):
            act.wait_ge(s["proj"], proj_done(i, ("g", b)))
            hold(act, s["gate2"], NP * i + b)
            nc.scalar.activation(gate[:, 0, :], psJ[USES.index(("g", b)) % 2][:, 0:T], ACT.Exp,
                                 scale=-1.0).then_inc(s["by_act"], 1)
            act.wait_ge(s["proj"], proj_done(i, ("q", b)))
            hold(act, s["gla"], NP * (i - 1) + b + 1)
            nc.scalar.copy(q[:, b, :], psJ[USES.index(("q", b)) % 2][:, 0:T]).then_inc(s["by_act"], 1)

        def pad_k(act, i, p):
            n = NP * i + p
            hold(act, s["k"], n + 1)
            hold(act, s["score"], n)
            nc.scalar.copy(kpad[0:DH, 0, :], kg[0:DH, p, :])
            nc.scalar.copy(kpad[DH:P, 1, :], kg[DH:P, p, :]).then_inc(s["kpad"], 1)

        def act_tile(act, i, gla, proj, prep):
            j = i - 1
            for p in range(NP):
                n = NP * j + p
                if gla:
                    act.wait_ge(s["a"], n + 1)
                    hold(act, s["prob"], n)
                    nc.scalar.activation(decay[:, :, :], psA[:, :, :], ACT.Exp).then_inc(s["e"], 1)
                    if p + 1 < NP:
                        pad_k(act, j, p + 1)
                    elif proj:
                        pad_k(act, i, 0)
                if p == 0 and gla:
                    copy_v(act, j, 2)
                    copy_v(act, j, 3)
                if p > 0 and proj:
                    copy_qg(act, i, p - 1)
                if p == 2 and proj:
                    act.wait_ge(s["softin"], i + 1)
                    nc.scalar.activation(zt[:, 2, :], zt[:, 1, :], ACT.Exp).then_inc(s["e1"], 1)
                    act.wait_ge(s["e1"], i + 1)
                    nc.scalar.activation(zt[:, 3, :], zt[:, 2, :], ACT.Ln, bias=1.0).then_inc(s["l"], 1)
                if p == 4 and proj:
                    copy_v(act, i, 0)
                    copy_v(act, i, 1)
                if p == 6 and proj:
                    act.wait_ge(s["cum"], i + 1)
                    hold(act, s["cur"], i)
                    nc.scalar.activation(w_new[:, :, :], psC.rearrange("p (a b) -> p a b", a=3),
                                         ACT.Exp).then_inc(s["w_new"], 1)
                if p == 6 and prep:
                    affine_h(act, i + 1)
            if proj:
                copy_qg(act, i, NP - 1)
                if not gla:
                    pad_k(act, i, 0)

        @block.scalar
        def _(act):
            nc.scalar.preload_act_table_set("natural_log_exp_and_others")
            affine_h(act, 0)
            act.wait_ge(s["zero"], 1)
            act_tile(act, 0, False, True, True)
            act_tile(act, 1, True, True, True)
            with act.Fori(2, NT - 1) as i:
                act_tile(act, i, True, True, True)
            act_tile(act, NT - 1, True, True, False)
            act_tile(act, NT, True, False, False)

        def norm_stats(dve, n):
            dve.wait_ge(s["x"], 16 * (n + 1))
            for c in range(NC):
                last = nc.vector.bn_stats(stats[:, c, :], x[:, c, :])
            last.then_inc(s["stats"], 1)
            dve.wait_ge(s["stats"], n + 1)
            nc.vector.memset(tick[:, 0:1], 0.0)
            for c in range(NC):
                last = nc.vector.bn_aggr(mv[:, c, :], stats[:, c, :])
            last.then_inc(s["mv"], 1)
            dve.wait_ge(s["mv"], n + 1)
            nc.vector.tensor_scalar(var_eps[:, :], mv[:, :, 1], LN_EPS, None, ALU.add).then_inc(s["var_eps"], 1)

        def norm_x(dve, n):
            dve.wait_ge(s["rstd"], n + 1)
            for c in range(NC):
                nc.vector.tensor_scalar(x[:, c, :], x[:, c, :], mv[:, c, 0:1], rstd[:, c:c + 1], ALU.subtract,
                                        ALU.mult).then_inc(s["xn"], 1)

        def split_h(dve, i):
            dve.wait_ge(s["hT"], KD * (i + 1))
            hold(dve, s["proj"], NU * i)
            nc.vector.tensor_copy(h_hi[:, :, :], hT[:, :, :]).then_inc(s["h_hi"], 1)
            dve.wait_ge(s["h_hi"], i + 1)
            nc.vector.tensor_tensor(h_lo[:, :, :], hT[:, :, :], h_hi[:, :, :].bitcast(F32),
                                    ALU.subtract).then_inc(s["h_lo"], 1)

        def gate_start(dve, i, b):
            dve.wait_ge(s["by_act"], act_done(i, ("g", b)))
            nc.vector.tensor_scalar(gate[:, 1, :], gate[:, 0, :], 1.0, None, ALU.add).then_inc(s["gate1"], 1)
            dve.wait_ge(s["gate1"], NP * i + b + 1)
            nc.vector.reciprocal(gate[:, 2, :], gate[:, 1, :]).then_inc(s["gate2"], 1)

        def gate_end(dve, i, b):
            dve.wait_ge(s["gate2"], NP * i + b + 1)
            dve.wait_ge(s["proj"], proj_done(i, ("k", b)))
            hold(dve, s["gla"], NP * (i - 1) + b + 1)
            nc.vector.tensor_tensor(kg[:, b, :], psJ[USES.index(("k", b)) % 2][:, 0:T], gate[:, 2, :],
                                    ALU.mult).then_inc(s["k"], 1)

        def dve_tile(dve, i, gla, proj, prep):
            j = i - 1
            for p in range(NP):
                n = NP * j + p
                if gla:
                    if p == 0:
                        dve.wait_ge(s["cur"], i)
                    dve.wait_ge(s["kT"], n + 1)
                    hold(dve, s["inc"], n)
                    nc.vector.tensor_tensor(
                        kw[:, :, :].rearrange("p c (h d) -> p c h d", h=2),
                        psK[:, 0:2, :].rearrange("p c (h d) -> p c h d", h=2),
                        w_cur[:, 1, :, 2 * p:2 * p + 2].unsqueeze(3).to_broadcast([P, NC, 2, DH]),
                        ALU.mult).then_inc(s["kw"], 1)
                    dve.wait_ge(s["mask"], n + 1)
                    dve.wait_ge(s["score"], n + 1)
                    hold(dve, s["pv"], n)
                    nc.vector.tensor_tensor(prob[:, :, :], decay[:, :, :], psS[:, :, :], ALU.mult).then_inc(s["prob"], 1)
                    dve.wait_ge(s["inc"], n + 1)
                    hold(dve, s["gla"], n)
                    for h in range(2):
                        r = slice(h * DH, (h + 1) * DH)
                        last = nc.vector.scalar_tensor_tensor(
                            out=mid[r, r], in0=state[r, p, r], scalar=w_cur[r, 2, 0, 2 * p + h:2 * p + h + 1],
                            in1=psK[r, 2, r], op0=ALU.mult, op1=ALU.add)
                    last.then_inc(s["mid"], 1)
                if p > 0 and proj:
                    gate_start(dve, i, p - 1)
                if gla:
                    dve.wait_ge(s["mid"], n + 1)
                    dve.wait_ge(s["pv"], n + 1)
                    for h in range(2):
                        r = slice(h * DH, (h + 1) * DH)
                        last = nc.vector.scalar_tensor_tensor(
                            out=state[r, p, r], in0=mid[r, r], scalar=w_cur[r, 2, 1, 2 * p + h:2 * p + h + 1],
                            in1=psK[r, 3, r], op0=ALU.mult, op1=ALU.add)
                    last.then_inc(s["state"], 1)
                if p == 0 and proj:
                    split_h(dve, i)
                if p == 2 and proj:
                    dve.wait_ge(s["z"], i + 1)
                    nc.vector.tensor_scalar(zt[:, 0, :], psZ, t["bd"][:, 0:1], None, ALU.add).then_inc(s["zb"], 1)
                    dve.wait_ge(s["zb"], i + 1)
                    nc.vector.scalar_tensor_tensor(out=zt[:, 1, :], in0=zt[:, 0, :], scalar=-1.0, in1=zt[:, 0, :],
                                                   op0=ALU.mult, op1=ALU.min).then_inc(s["softin"], 1)
                if p == 3 and proj:
                    dve.wait_ge(s["l"], i + 1)
                    nc.vector.scalar_tensor_tensor(out=zt[:, 1, :], in0=zt[:, 0, :], scalar=0.0, in1=zt[:, 3, :],
                                                   op0=ALU.max, op1=ALU.add).then_inc(s["soft"], 1)
                    dve.wait_ge(s["soft"], i + 1)
                    nc.vector.tensor_scalar(zt[:, 4, :], zt[:, 1, :], -1.0, None, ALU.mult).then_inc(s["gT"], 1)
                if p == 5 and proj:
                    dve.wait_ge(s["g_turned"], i + 1)
                    nc.vector.tensor_copy(g_raw[:, :], psG).then_inc(s["g_raw"], 1)
                if p == 7 and proj:
                    hold(dve, s["r"], NP * i if gla else 0)
                    dve.wait_ge(s["g_raw"], i + 1)
                    nc.vector.tensor_copy(g_hi[:, :], g_raw[:, :]).then_inc(s["g_hi"], 1)
                    dve.wait_ge(s["g_hi"], i + 1)
                    nc.vector.tensor_tensor(g_lo[:, :], g_raw[:, :], g_hi[:, :].bitcast(F32),
                                            ALU.subtract).then_inc(s["g"], 1)
                if p == 4 and prep:
                    norm_stats(dve, i + 1)
                if p == 5 and prep:
                    norm_x(dve, i + 1)
                if p > 0 and proj:
                    gate_end(dve, i, p - 1)
                if gla:
                    dve.wait_ge(s["gla"], n + 1)
                    nc.vector.tensor_tensor(
                        inter[:, :, :].rearrange("p c (h d) -> p c h d", h=2),
                        psO[:, 2:4, :].rearrange("p c (h d) -> p c h d", h=2),
                        w_cur[:, 0, :, 2 * p:2 * p + 2].unsqueeze(3).to_broadcast([P, NC, 2, DH]),
                        ALU.mult).then_inc(s["inter"], 1)
                    dve.wait_ge(s["inter"], n + 1)
                    hold(dve, store[p % 2], 16 * (NP // 2 * j + p // 2))
                    nc.vector.tensor_tensor(o[:, p % 2, :, :], inter[:, :, :], psO[:, 0:2, :], ALU.add).then_inc(s["o"], 1)
            if proj:
                dve.wait_ge(s["w_new"], i + 1)
                nc.vector.tensor_copy(w_cur[:, :, :, :].rearrange("p a c h -> p (a c h)"),
                                      w_new[:, :, :].rearrange("p a b -> p (a b)")).then_inc(s["cur"], 1)
                gate_start(dve, i, NP - 1)
                gate_end(dve, i, NP - 1)

        @block.vector
        def _(dve):
            nc.vector.memset(state[:, :, :], 0.0)
            nc.vector.memset(mid[:, :], 0.0)
            nc.vector.memset(kpad[:, :, :], 0.0).then_inc(s["zero"], 1)
            dve.wait_ge(s["zero"], 1)
            norm_stats(dve, 0)
            norm_x(dve, 0)
            dve_tile(dve, 0, False, True, True)
            dve_tile(dve, 1, True, True, True)
            with dve.Fori(2, NT - 1) as i:
                dve_tile(dve, i, True, True, True)
            dve_tile(dve, NT - 1, True, True, False)
            dve_tile(dve, NT, True, False, False)

        def rsqrt(pool, n):
            pool.wait_ge(s["var_eps"], n + 1)
            nc.gpsimd.tensor_tensor(rstd[:, :], var_eps[:, :], t["minus_half"][:, 0:NC], ALU.pow).then_inc(s["rstd"], 1)

        def spread_g(pool, i, p):
            if p == 0:
                pool.wait_ge(s["g"], i + 1)
            hold(pool, s["a"], NP * i + p)
            for dst, g in ((r_hi, g_hi), (r_lo, g_lo)):
                gg = g[:, :].bitcast(F32).rearrange("p (c h) -> p c h", c=NC)[:, :, 2 * p:2 * p + 2]
                last = nc.gpsimd.tensor_tensor(dst[:, :, :, :], gg.unsqueeze(3).to_broadcast([P, NC, 2, CH]),
                                               t["upto"][:, :].unsqueeze(1).unsqueeze(1).to_broadcast([P, NC, 2, CH]),
                                               ALU.mult)
            last.then_inc(s["r"], 1)

        def pool_tile(pool, i, gla, proj, prep):
            j = i - 1
            for p in range(NP):
                if gla:
                    pool.wait_ge(s["e"], NP * j + p + 1)
                    nc.gpsimd.tensor_tensor(tick[:, 1:2], t["zeros"][:, :], t["zeros"][:, :],
                                            ALU.mult)
                    nc.gpsimd.affine_select(out=decay[:, :, :], in_=decay[:, :, :], compare_op=ALU.is_ge, fill=0.0,
                                            base=0, pattern=[[0, 4], [1, CH]], channel_multiplier=-1).then_inc(s["mask"], 1)
                    if p + 1 < NP:
                        spread_g(pool, j, p + 1)
                    elif proj:
                        spread_g(pool, i, 0)
                if p == 4 and prep:
                    rsqrt(pool, i + 1)
            if proj and not gla:
                spread_g(pool, i, 0)

        @block.gpsimd
        def _(pool):
            rsqrt(pool, 0)
            pool_tile(pool, 0, False, True, True)
            pool_tile(pool, 1, True, True, True)
            with pool.Fori(2, NT - 1) as i:
                pool_tile(pool, i, True, True, True)
            pool_tile(pool, NT - 1, True, True, False)
            pool_tile(pool, NT, True, False, False)


def output_pass(nc, t, W, x_v, o_v, out_v):
    with ExitStack() as ctx:
        def sb(name, shape, dt=F32):
            return ctx.enter_context(nc.sbuf_tensor(name, shape, dt))

        def ps(name, shape):
            return ctx.enter_context(nc.psum_tensor(name, shape, F32))

        xn = sb("xn", [P, NC, DM])
        hT = sb("hT2", [P, KD, T])
        h_hi = sb("h_hi2", [P, KD, T], F32R)
        h_lo = sb("h_lo2", [P, KD, T], F32R)
        o = sb("o_rows", [P, NC, HID])
        og = sb("og", [P, 2, 512])
        z_hi = sb("z_hi", [P, NP, T], F32R)
        z_lo = sb("z_lo", [P, NP, T], F32R)
        x1 = sb("x1", [P, NC, DM])
        x1_old = sb("x1_old", [P, NC, DM])
        x2n = sb("x2n", [P, NC, DM])
        h2 = sb("h2", [P, KD, T + 1])
        mix = sb("mix", [P, KD, T])
        prev = sb("prev", [P, KD, T])
        ra_hi = sb("ra_hi", [P, KD, T], F32R)
        ra_lo = sb("ra_lo", [P, KD, T], F32R)
        xk_hi = sb("xk_hi", [P, KD, T], F32R)
        xk_lo = sb("xk_lo", [P, KD, T], F32R)
        r = sb("r_gate", [P, NC, DM])
        relu = sb("relu", [P, 2, T])
        junk = sb("junk", [P, HID], BF16)
        ss = sb("ss", [P, NC])
        small = sb("small", [P, 10])
        stats = sb("stats2", [P, 2, NC, 6])
        mv = sb("mv2", [P, 2, NC, 2])
        var_eps = sb("var_eps2", [P, 3, NC])
        rstd = sb("rstd2", [P, 3, NC])

        tick = sb("tick2", [P, 1])

        psT = ps("psT2", [P, KD, T])
        psG = [ps(f"psG{n}", [P, 512]) for n in range(2)]
        psR = [ps(f"psR{n}", [P, 512]) for n in range(2)]
        psW = [ps(f"psW{n}", [P, 512]) for n in range(2)]
        psZ = psG + psR

        s = signals(nc, ctx, "b", "xa xb ol st1 mv1 ve1 rstd1 xn xT hT h_hi h_lo og sg sq ve3 rstd3 z tz zh zl wo x1 "
                 "st2 mv2 ve2 rstd2 xn2 xT2 h2 prev mixr xr_hi xr prevk mixk xk_hi xk last rr rs kt relu k2 ka_hi ka "
                 "kv fin1 fin keep store zero")
        block = ctx.enter_context(nc.Block())

        def sp_tile(sp, i, att, ffn, prep):
            j = i - 1
            if prep:
                sp.wait_ge(s["xT"], KD * (i + 1))
                sp.dma_start(xn[:, :, :], x_v[i + 1]).then_inc(s["xa"], 16)
            if att:
                hold(sp, s["keep"], i)
                sp.dma_start(x1[:, :, :], x_v[i]).then_inc(s["xb"], 16)
            if prep:
                sp.wait_ge(s["tz"], 4 * (i + 1))
                sp.dma_start(o[:, :, :], o_v[i + 1]).then_inc(s["ol"], 16)
            if ffn:
                for c in range(NC):
                    sp.wait_ge(s["fin"], NC * j + c + 1)
                    sp.dma_start(out_v[j, :, c, :], r[:, c, :]).then_inc(s["store"], 16)

        @block.sync
        def _(sp):
            sp.dma_start(xn[:, :, :], x_v[0]).then_inc(s["xa"], 16)
            sp.dma_start(o[:, :, :], o_v[0]).then_inc(s["ol"], 16)
            sp_tile(sp, 0, True, False, True)
            sp_tile(sp, 1, True, True, True)
            with sp.Fori(2, NT - 1) as i:
                sp_tile(sp, i, True, True, True)
            sp_tile(sp, NT - 1, True, True, False)
            sp_tile(sp, NT, False, True, False)
            sp.wait_ge(s["store"], 16 * NC * NT)

        def turn(pe, src, sem):
            for k in range(KD):
                for c in range(NC):
                    last = nc.tensor.transpose(psT[:, k, c * CH:(c + 1) * CH], src[:, c, k * P:(k + 1) * P],
                                               t["ident"][:, :])
                last.then_inc(sem, 1)

        def rows_product(bank, a_hi, a_lo, w, c, half, blocks, ready=()):
            for k in range(blocks):
                for at, eng, sem, value in ready:
                    if at == k:
                        eng.wait_ge(sem, value)
                ah, al = (a[:, k, c * CH:(c + 1) * CH] for a in (a_hi, a_lo))
                wh, wl = (a[:, k, half * 512:(half + 1) * 512] for a in w)
                last = three_passes(nc, bank[:, :], ah, al, wh, wl, k == 0, k == blocks - 1)
            return last

        def pe_tile(pe, i, att, ffn, prep):
            j = i - 1
            if att:
                pe.wait_ge(s["h_lo"], i + 1)
                for n in range(4):
                    if n < 2:
                        hold(pe, s["zl"], 4 * i)
                    else:
                        pe.wait_ge(s["sg"], 4 * i + n - 1)
                    rows_product(psG[n % 2], h_hi, h_lo, W["og"], n // 2, n % 2, KD).then_inc(s["og"], 1)
            if ffn:
                pe.wait_ge(s["xn2"], NC * (j + 1))
                hold(pe, s["hT"], KD * (i + 1 if att else i))
                hold(pe, s["h2"], KD * j)
                turn(pe, x2n, s["xT2"])
            if att:
                for n in range(4):
                    c, half = n // 2, n % 2
                    pe.wait_ge(s["z"], 4 * i + n + 1)
                    if n == 0:
                        pe.wait_ge(s["sg"], 4 * (i + 1))
                    if n == 2:
                        hold(pe, s["fin1"], NC * j)
                    for b in range(4):
                        last = nc.tensor.transpose(psZ[n][:, b * CH:(b + 1) * CH],
                                                   o[:, c, (4 * half + b) * P:(4 * half + b + 1) * P], t["ident"][:, :])
                    last.then_inc(s["tz"], 1)
                hold(pe, s["relu"], KD * j)
                for c in range(NC):
                    ready = [(4 * half, pe, s["zl"], 4 * i + 2 * c + half + 1) for half in range(2)]
                    rows_product(psW[c], z_hi, z_lo, W["o"], c, 0, NP, ready).then_inc(s["wo"], 1)
            if ffn:
                pe.wait_ge(s["xr"], j + 1)
                if att:
                    pe.wait_ge(s["zl"], 4 * (i + 1))
                hold(pe, s["fin1"], NC * j)
                for c in range(NC):
                    rows_product(psR[c], ra_hi, ra_lo, W["r"], c, 0, KD).then_inc(s["rr"], 1)
            if prep:
                pe.wait_ge(s["xn"], NC * (i + 2))
                hold(pe, s["h2"], KD * (j + 1) if ffn else 0)
                turn(pe, xn, s["xT"])
            if ffn:
                pe.wait_ge(s["xk"], j + 1)
                for n in range(KD):
                    if n < 2:
                        pe.wait_ge(s["x1"], NC * (i + 1) if att else NC * i)
                        hold(pe, s["relu"], KD * j)
                    else:
                        pe.wait_ge(s["relu"], KD * j + n - 1)
                    for k in range(KD):
                        wh, wl = (a[:, k, n * P:(n + 1) * P] for a in W["k2"])
                        last = three_passes(nc, psW[n % 2][:, 0:T], wh, wl, xk_hi[:, k, :], xk_lo[:, k, :], k == 0,
                                            k == KD - 1)
                    last.then_inc(s["kt"], 1)
                pe.wait_ge(s["rs"], NC * (j + 1))
                for c in range(NC):
                    ready = [(k, pe, s["ka"], KD * j + k + 1) for k in range(KD)]
                    rows_product(psR[c], ra_hi, ra_lo, W["v2"], c, 0, KD, ready if c == 0 else ()).then_inc(s["kv"], 1)

        @block.tensor
        def _(pe):
            pe.wait_ge(s["xn"], NC)
            turn(pe, xn, s["xT"])
            pe_tile(pe, 0, True, False, True)
            pe_tile(pe, 1, True, True, True)
            with pe.Fori(2, NT - 1) as i:
                pe_tile(pe, i, True, True, True)
            pe_tile(pe, NT - 1, True, True, False)
            pe_tile(pe, NT, False, True, False)

        def affine_h(act, n):
            hold(act, s["h_lo"], n)
            for k in range(KD):
                act.wait_ge(s["xT"], KD * n + 2 * (k // 2) + 2)
                nc.scalar.activation(hT[:, k, :], psT[:, k, :], ACT.Identity, bias=t["mod"][:, SA, k:k + 1],
                                     scale=t["ca1"][:, k:k + 1]).then_inc(s["hT"], 1)

        def act_tile(act, i, att, ffn, prep):
            j = i - 1

            def copy_z(n):
                c, half = n // 2, n % 2
                act.wait_ge(s["tz"], 4 * i + n + 1)
                nc.scalar.copy(z_hi[:, 4 * half:4 * half + 4, c * CH:(c + 1) * CH],
                               psZ[n][:, :].rearrange("p (b t) -> p b t", b=4)).then_inc(s["zh"], 1)

            if att:
                act.wait_ge(s["ol"], 16 * (i + 1))
                hold(act, s["ve3"], i)
                for c in range(NC):
                    hold(act, s["sq"], NC * i + c)
                    nc.scalar.activation(junk[:, :], o[:, c, :], ACT.Square, accum_out=ss[:, c:c + 1]).then_inc(s["sq"], 1)
                for n in range(4):
                    act.wait_ge(s["og"], 4 * i + n + 1)
                    hold(act, s["z"], 4 * i + n - 1 if n else 4 * i)
                    nc.scalar.activation(og[:, n % 2, :], psG[n % 2][:, :], ACT.Sigmoid).then_inc(s["sg"], 1)
                hold(act, s["wo"], NC * i)
                copy_z(0)
                copy_z(1)
            if ffn:
                hold(act, s["last"], j + 1)
                for k in range(KD):
                    act.wait_ge(s["xT2"], KD * j + 2 * (k // 2) + 2)
                    nc.scalar.activation(h2[:, k, 1:T + 1], psT[:, k, :], ACT.Identity, bias=t["mod"][:, SB, k:k + 1],
                                         scale=t["cb1"][:, k:k + 1]).then_inc(s["h2"], 1)
            if att:
                copy_z(2)
                copy_z(3)
            if ffn:
                hold(act, s["store"], 16 * NC * j)
                for c in range(NC):
                    act.wait_ge(s["rr"], NC * j + c + 1)
                    nc.scalar.activation(r[:, c, :], psR[c][:, :], ACT.Sigmoid).then_inc(s["rs"], 1)
            if prep:
                affine_h(act, i + 1)
            if ffn:
                for n in range(KD):
                    act.wait_ge(s["kt"], KD * j + n + 1)
                    hold(act, s["ka"], KD * j + n)
                    nc.scalar.activation(relu[:, 0, :], psW[n % 2][:, 0:T], ACT.Relu).then_inc(s["relu"], 1)
                    act.wait_ge(s["relu"], KD * j + n + 1)
                    nc.scalar.activation(relu[:, 1, :], relu[:, 0, :], ACT.Square).then_inc(s["k2"], 1)

        @block.scalar
        def _(act):
            affine_h(act, 0)
            act.wait_ge(s["zero"], 1)
            act_tile(act, 0, True, False, True)
            act_tile(act, 1, True, True, True)
            with act.Fori(2, NT - 1) as i:
                act_tile(act, i, True, True, True)
            act_tile(act, NT - 1, True, True, False)
            act_tile(act, NT, False, True, False)

        def row_stats(dve, which, src, n, st, m, ve):
            for c in range(NC):
                last = nc.vector.bn_stats(stats[:, which, c, :], src[:, c, :])
            last.then_inc(st, 1)
            dve.wait_ge(st, n + 1)
            nc.vector.memset(tick[:, 0:1], 0.0)
            for c in range(NC):
                last = nc.vector.bn_aggr(mv[:, which, c, :], stats[:, which, c, :])
            last.then_inc(m, 1)
            dve.wait_ge(m, n + 1)
            nc.vector.tensor_scalar(var_eps[:, which, :], mv[:, which, :, 1], LN_EPS, None, ALU.add).then_inc(ve, 1)

        def split_h(dve, n):
            dve.wait_ge(s["hT"], KD * (n + 1))
            hold(dve, s["og"], 4 * n)
            nc.vector.tensor_copy(h_hi[:, :, :], hT[:, :, :]).then_inc(s["h_hi"], 1)
            dve.wait_ge(s["h_hi"], n + 1)
            nc.vector.tensor_tensor(h_lo[:, :, :], hT[:, :, :], h_hi[:, :, :].bitcast(F32),
                                    ALU.subtract).then_inc(s["h_lo"], 1)

        def norm_first(dve, n):
            dve.wait_ge(s["rstd1"], n + 1)
            for c in range(NC):
                nc.vector.tensor_scalar(xn[:, c, :], xn[:, c, :], mv[:, 0, c, 0:1], rstd[:, 0, c:c + 1], ALU.subtract,
                                        ALU.mult).then_inc(s["xn"], 1)

        def norm_second(dve, n):
            dve.wait_ge(s["rstd2"], n + 1)
            hold(dve, s["xT2"], KD * n)
            for c in range(NC):
                nc.vector.tensor_scalar(x2n[:, c, :], x1[:, c, :], mv[:, 1, c, 0:1], rstd[:, 1, c:c + 1],
                                        ALU.subtract, ALU.mult).then_inc(s["xn2"], 1)

        def shift_mix(dve, j, m, hi, lo, s_prev, s_mix, s_hi, s_lo):
            for k in range(KD):
                last = nc.vector.tensor_scalar(prev[:, k, :], h2[:, k, 0:T], t["one_minus_mu"][:, m, k:k + 1], None,
                                               ALU.mult)
            last.then_inc(s_prev, 1)
            dve.wait_ge(s_prev, j + 1)
            for k in range(KD):
                last = nc.vector.scalar_tensor_tensor(out=mix[:, k, :], in0=h2[:, k, 1:T + 1],
                                                      scalar=t["mu"][:, m, k:k + 1], in1=prev[:, k, :],
                                                      op0=ALU.mult, op1=ALU.add)
            last.then_inc(s_mix, 1)
            dve.wait_ge(s_mix, j + 1)
            nc.vector.tensor_copy(hi[:, :, :], mix[:, :, :]).then_inc(s_hi, 1)
            dve.wait_ge(s_hi, j + 1)
            nc.vector.tensor_tensor(lo[:, :, :], mix[:, :, :], hi[:, :, :].bitcast(F32), ALU.subtract).then_inc(s_lo, 1)

        def dve_tile(dve, i, att, ffn, prep):
            j = i - 1
            if prep:
                dve.wait_ge(s["xa"], 16 * (i + 2))
                row_stats(dve, 0, xn, i + 1, s["st1"], s["mv1"], s["ve1"])
            if att:
                dve.wait_ge(s["sq"], NC * (i + 1))
                nc.vector.tensor_scalar(var_eps[:, 2, :], ss[:, :], 1.0 / HID, RMS_EPS, ALU.mult,
                                        ALU.add).then_inc(s["ve3"], 1)
                for n in range(4):
                    c, half = n // 2, n % 2
                    dve.wait_ge(s["sg"], 4 * i + n + 1)
                    rows = o[:, c, half * 512:(half + 1) * 512]
                    nc.vector.tensor_tensor(rows, rows, og[:, n % 2, :], ALU.mult).then_inc(s["z"], 1)
                hold(dve, s["wo"], NC * i)
                for n in range(4):
                    c, half = n // 2, n % 2
                    dve.wait_ge(s["zh"], 4 * i + n + 1)
                    d = (slice(None), slice(4 * half, 4 * half + 4), slice(c * CH, (c + 1) * CH))
                    nc.vector.tensor_tensor(z_lo[d], psZ[n][:, :].rearrange("p (b t) -> p b t", b=4),
                                            z_hi[d].bitcast(F32), ALU.subtract).then_inc(s["zl"], 1)
            if ffn:
                dve.wait_ge(s["h2"], KD * (j + 1))
                hold(dve, s["kv"], NC * j)
                shift_mix(dve, j, 0, ra_hi, ra_lo, s["prev"], s["mixr"], s["xr_hi"], s["xr"])
                hold(dve, s["kt"], KD * j)
                dve.wait_ge(s["xr"], j + 1)
                shift_mix(dve, j, 1, xk_hi, xk_lo, s["prevk"], s["mixk"], s["xk_hi"], s["xk"])
                dve.wait_ge(s["xk"], j + 1)
                nc.vector.tensor_copy(h2[:, :, 0:1], h2[:, :, T:T + 1]).then_inc(s["last"], 1)
            if prep:
                norm_first(dve, i + 1)
            if att:
                dve.wait_ge(s["rstd3"], i + 1)
                dve.wait_ge(s["xb"], 16 * (i + 1))
                for c in range(NC):
                    dve.wait_ge(s["wo"], NC * i + c + 1)
                    nc.vector.scalar_tensor_tensor(out=x1[:, c, :], in0=psW[c][:, :], scalar=rstd[:, 2, c:c + 1],
                                                   in1=x1[:, c, :], op0=ALU.mult, op1=ALU.add).then_inc(s["x1"], 1)
                dve.wait_ge(s["x1"], NC * (i + 1))
                row_stats(dve, 1, x1, i, s["st2"], s["mv2"], s["ve2"])
            if ffn:
                dve.wait_ge(s["rr"], NC * (j + 1))
                for n in range(KD):
                    if prep and n == 0:
                        split_h(dve, i + 1)
                    if att and n == 0:
                        norm_second(dve, i)
                    dve.wait_ge(s["k2"], KD * j + n + 1)
                    nc.vector.tensor_copy(ra_hi[:, n, :], relu[:, 1, :]).then_inc(s["ka_hi"], 1)
                    dve.wait_ge(s["ka_hi"], KD * j + n + 1)
                    nc.vector.tensor_tensor(ra_lo[:, n, :], relu[:, 1, :], ra_hi[:, n, :].bitcast(F32),
                                            ALU.subtract).then_inc(s["ka"], 1)
                for c in range(NC):
                    dve.wait_ge(s["kv"], NC * j + c + 1)
                    nc.vector.tensor_tensor(r[:, c, :], psR[c][:, :], r[:, c, :], ALU.mult).then_inc(s["fin1"], 1)
                    dve.wait_ge(s["fin1"], NC * j + c + 1)
                    nc.vector.tensor_tensor(r[:, c, :], x1_old[:, c, :], r[:, c, :], ALU.add).then_inc(s["fin"], 1)
            else:
                split_h(dve, i + 1)
                norm_second(dve, i)
            if att:
                hold(dve, s["fin"], NC * i)
                nc.vector.tensor_copy(x1_old[:, :, :], x1[:, :, :]).then_inc(s["keep"], 1)

        @block.vector
        def _(dve):
            nc.vector.memset(h2[:, :, 0:1], 0.0).then_inc(s["zero"], 1)
            dve.wait_ge(s["zero"], 1)
            nc.vector.tensor_copy(small[:, 0:4], t["minus_half"][:, :]).then_inc(s["last"], 1)
            dve.wait_ge(s["xa"], 16)
            row_stats(dve, 0, xn, 0, s["st1"], s["mv1"], s["ve1"])
            norm_first(dve, 0)
            split_h(dve, 0)
            dve_tile(dve, 0, True, False, True)
            dve_tile(dve, 1, True, True, True)
            with dve.Fori(2, NT - 1) as i:
                dve_tile(dve, i, True, True, True)
            dve_tile(dve, NT - 1, True, True, False)
            dve_tile(dve, NT, False, True, False)

        def rsqrt(pool, which, n, ready, done):
            pool.wait_ge(ready, n + 1)
            nc.gpsimd.tensor_tensor(rstd[:, which, :], var_eps[:, which, :], t["minus_half"][:, 0:NC],
                                    ALU.pow).then_inc(done, 1)

        def pool_tile(pool, i, att, ffn, prep):
            if prep:
                rsqrt(pool, 0, i + 1, s["ve1"], s["rstd1"])
            if att:
                rsqrt(pool, 2, i, s["ve3"], s["rstd3"])
                rsqrt(pool, 1, i, s["ve2"], s["rstd2"])

        @block.gpsimd
        def _(pool):
            rsqrt(pool, 0, 0, s["ve1"], s["rstd1"])
            pool_tile(pool, 0, True, False, True)
            pool_tile(pool, 1, True, True, True)
            with pool.Fori(2, NT - 1) as i:
                pool_tile(pool, i, True, True, True)
            pool_tile(pool, NT - 1, True, True, False)


def adaln_gla_block(nc, x, wq, wk, wv, wo, wg, wog, wd, bd, norm_w, w_r, w_k, w_v, mu_r, mu_k, c, wmod, out):
    o_rows = nc.dram_tensor("o_rows_dram", (TOK, HID), F32).ap()
    x_v = x.rearrange("a (i c p) d -> (a i) p c d", c=NC, p=CH)
    out_v = out.rearrange("a (i c p) d -> (a i) p c d", c=NC, p=CH)
    o_v = o_rows.rearrange("(i c p) d -> i p c d", c=NC, p=CH)
    with ExitStack() as ctx:
        t = {}
        for name, shape, dt in (
            ("ones", [P, P], F32), ("ident", [P, P], F32), ("upto", [P, P], F32), ("after", [P, P], F32),
            ("after_r", [P, P], F32R), ("zeros", [P, 1], F32), ("minus_half", [P, 4], F32), ("bd", [H, 1], F32),
            ("mu", [P, 2, KD], F32), ("one_minus_mu", [P, 2, KD], F32), ("norm_w", [P, NP], F32),
            ("silu_c", [P, KD], F32), ("mod", [P, 6, KD], F32), ("ca1", [P, KD], F32), ("cb1", [P, KD], F32),
            ("ga", [P, KD], F32), ("gb", [P, KD], F32), ("wd_hi", [P, KD, H], F32R), ("wd_lo", [P, KD, H], F32R),
        ):
            t[name] = ctx.enter_context(nc.sbuf_tensor(f"c_{name}", shape, dt))
        prepare_constants(nc, t, {"c": c, "bd": bd, "mu_r": mu_r, "mu_k": mu_k, "norm_w": norm_w}, wmod, wd)

        def pair(ctx2, name, blocks, width):
            return [ctx2.enter_context(nc.sbuf_tensor(f"w_{name}_{part}", [P, blocks, width], F32R))
                    for part in ("hi", "lo")]

        def rows(w, n):
            return w.rearrange("(n r p) d -> n p r d", r=4, p=P)[n]

        with ExitStack() as first:
            W = {name: pair(first, name, KD, HID) for name in "qgkv"}
            jobs = []
            for name, w in (("q", wq), ("g", wg), ("k", wk), ("v", wv)):
                for n in range(2):
                    cols = [(*(a[:, k, n * 512:(n + 1) * 512] for a in W[name]), None) for k in range(KD)]
                    jobs.append((rows(w, n), None, cols))
            prepare_weights(nc, t["ident"], jobs, "p")
            attention_pass(nc, t, W, x_v, o_v)
        with ExitStack() as second:
            W = {"og": pair(second, "og", KD, HID), "o": pair(second, "o", NP, DM)}
            for name in ("r", "k2", "v2"):
                W[name] = pair(second, name, KD, DM)
            jobs = []
            for n in range(2):
                cols = [(*(a[:, k, n * 512:(n + 1) * 512] for a in W["og"]), None) for k in range(KD)]
                jobs.append((rows(wog, n), None, cols))
            for n in range(2):
                cols = [(*(a[:, 4 * n + k, :] for a in W["o"]), t["norm_w"][:, 4 * n + k:4 * n + k + 1])
                        for k in range(4)]
                jobs.append((wo.rearrange("(r p) (n d) -> n p r d", p=P, n=2)[n], t["ga"], cols))
            for name, w, scale in (("r", w_r, None), ("k2", w_k, None), ("v2", w_v, t["gb"])):
                cols = [(*(a[:, k, :] for a in W[name]), None) for k in range(KD)]
                jobs.append((rows(w, 0), scale, cols))
            prepare_weights(nc, t["ident"], jobs, "s")
            output_pass(nc, t, W, x_v, o_v, out_v)


_INS = ["L0_attn_x", "L0_attn_Wq", "L0_attn_Wk", "L0_attn_Wv", "L0_attn_Wo", "L0_attn_Wg", "L0_attn_Wog", "L0_attn_Wd",
        "L0_attn_bd", "L0_attn_norm_w", "L0_ffn_W_r", "L0_ffn_W_k", "L0_ffn_W_v", "L0_ffn_mu_r", "L0_ffn_mu_k", "L0_c",
        "L0_wmod"]


def kernel(**inputs):
    import numpy as _np
    import concourse.bacc as _bacc
    from concourse import mybir as _mybir
    from concourse.bass_utils import run_bass_kernel_spmd as _run

    nc = _bacc.Bacc("TRN2", target_bir_lowering=False, num_devices=1)
    arrays, args = {}, []
    for name in _INS:
        a = _np.ascontiguousarray(inputs[name])
        arrays[f"in_{name}_dram"] = a
        args.append(nc.dram_tensor(f"in_{name}_dram", a.shape, _mybir.dt.from_np(a.dtype), kind="ExternalInput").ap())
    out = nc.dram_tensor("out_0_dram", (1, TOK, DM), _mybir.dt.float32, kind="ExternalOutput").ap()
    adaln_gla_block(nc, *args, out)
    r = _run(nc, [arrays], core_ids=[0])
    return r.results[0]["out_0_dram"]
```

```python
from contextlib import ExitStack

import concourse.bass as bass
from concourse import mybir

F32 = mybir.dt.float32
F32R = mybir.dt.float32r
BF16 = mybir.dt.bfloat16
ALU = mybir.AluOpType
ACT = mybir.ActivationFunctionType

P = 128
DM = 512
HID = 1024
H = 16
DH = HID // H
TOK = 8192
CH = 128
NC = 2
T = NC * CH
NT = TOK // T
KD = DM // P
NP = HID // P
LN_EPS = 1e-5
RMS_EPS = 1.1920928955078125e-07
SA, CA, GA, SB, CB, GB = range(6)


def hold(eng, sem, value):
    if isinstance(value, int) and value <= 0:
        return
    eng.wait_ge(sem, value)


def signals(nc, ctx, prefix, names):
    return {n: ctx.enter_context(nc.semaphore(f"{prefix}_{n}")) for n in names.split()}


def three_passes(nc, out, w_hi, w_lo, x_hi, x_lo, first, last):
    nc.tensor.matmul(out, w_hi, x_hi, start=first, stop=False)
    nc.tensor.matmul(out, w_hi, x_lo, start=False, stop=False)
    return nc.tensor.matmul(out, w_lo, x_hi, start=False, stop=last)


def prepare(nc, t, jobs, name, first=None):
    NS, NB = 4, 4
    is_mod = [len(job) == 2 for job in jobs]
    scales = [not m and job[1] is not None for m, job in zip(is_mod, jobs)]
    before = lambda flags, n: sum(flags[:n])
    banks_before = lambda n: 4 * (n - before(is_mod, n))
    with ExitStack() as ctx:
        stage = [ctx.enter_context(nc.sbuf_tensor(f"{name}_stage{n}", [P, 4, 512], F32)) for n in range(NS)]
        scaled = ctx.enter_context(nc.sbuf_tensor(f"{name}_scaled", [P, 4, 512], F32))
        sign = ctx.enter_context(nc.sbuf_tensor(f"{name}_sign", [P, 4, KD], F32))
        bank = [ctx.enter_context(nc.psum_tensor(f"{name}_ps{n}", [P, 512], F32)) for n in range(NB)]
        mod_ps = [ctx.enter_context(nc.psum_tensor(f"{name}_mod{n}", [P, 512], F32)) for n in range(2)]
        s = signals(nc, ctx, name, "turned hi lo scaled read mod mod_out gate step "
                    "small filled masks exp one silu wd wd_hi mu")
        loaded = [ctx.enter_context(nc.semaphore(f"{name}_loaded{n}")) for n in range(NS)]
        if first:
            NV = 2 * KD + NP
            wd_rows = ctx.enter_context(nc.sbuf_tensor("wd_rows", [H, DM], F32))
            vec_rows = ctx.enter_context(nc.sbuf_tensor("vec_rows", [NV, P], F32))
            c_col = ctx.enter_context(nc.sbuf_tensor("c_col", [P, KD], F32))
            silu = ctx.enter_context(nc.sbuf_tensor("silu", [P, 3, KD], F32))
            wd_ps = ctx.enter_context(nc.psum_tensor("wd_ps", [P, 512], F32))
        block = ctx.enter_context(nc.Block())

        @block.sync
        def _(sp):
            for n, job in enumerate(jobs):
                if n >= NS:
                    m = n - NS
                    if scales[m]:
                        sp.wait_ge(s["scaled"], before(scales, m + 1))
                    else:
                        sp.wait_ge(s["read"], m + 1)
                sp.dma_start(stage[n % NS][:, :, :], job[0]).then_inc(loaded[n % NS], 16)
                if n == 0 and first:
                    sp.dma_start(c_col[:, :], first["c"].rearrange("a (p t) -> (a p) t", t=KD)).then_inc(s["small"], 16)
                    sp.dma_start(wd_rows[:, :], first["wd"]).then_inc(s["small"], 16)
                    for vec, r0, rows in (("mu_r", 0, KD), ("mu_k", KD, KD), ("norm_w", 2 * KD, NP)):
                        sp.dma_start(vec_rows[r0:r0 + rows, :],
                                     first[vec].rearrange("(t p) -> t p", p=P)).then_inc(s["small"], 16)
                    sp.dma_start(t["bd"][:, :], first["bd"].rearrange("(h a) -> h a", a=1)).then_inc(s["small"], 16)

        @block.tensor
        def _(pe):
            if first:
                pe.wait_ge(s["masks"], 1)
            for n, job in enumerate(jobs):
                if scales[n]:
                    pe.wait_ge(s["scaled"], before(scales, n + 1))
                else:
                    pe.wait_ge(loaded[n % NS], 16 * (n // NS + 1))
                if is_mod[n]:
                    m = before(is_mod, n)
                    hold(pe, s["mod_out"], m - 1)
                    if first:
                        pe.wait_ge(s["silu"], 1)
                    for b in range(KD):
                        for k in range(KD):
                            last = nc.tensor.matmul(mod_ps[m % 2][:, b:b + 1], stage[n % NS][:, k, b * P:(b + 1) * P],
                                                    t["silu_c"][:, k:k + 1], start=(k == 0), stop=(k == KD - 1))
                    last.then_inc(s["read"], 1)
                    continue
                src = scaled if scales[n] else stage[n % NS]
                for k in range(4):
                    m = banks_before(n) + k
                    hold(pe, s["lo"], m - NB + 1)
                    for r in range(4):
                        last = nc.tensor.transpose(bank[m % NB][:, r * P:(r + 1) * P], src[:, r, k * P:(k + 1) * P],
                                                   t["ident"][:, :])
                    if k < 3:
                        last.then_inc(s["turned"], 1)
                last.then_inc(s["read"], 1)
                if n == 1 and first:
                    pe.wait_ge(s["small"], 16 * 6)
                    for k in range(KD):
                        nc.tensor.transpose(wd_ps[:, k * H:(k + 1) * H], wd_rows[:, k * P:(k + 1) * P],
                                            t["ident"][0:H, 0:H])
                    nc.tensor.transpose(wd_ps[:, KD * H:KD * H + NV], vec_rows[:, :],
                                        t["ident"][0:NV, 0:NV]).then_inc(s["wd"], 1)

        def bank_ready(eng, n, k):
            if k < 3:
                eng.wait_ge(s["turned"], 3 * (n - before(is_mod, n)) + k + 1)
            else:
                eng.wait_ge(s["read"], n + 1)

        @block.gpsimd
        def _(pool):
            if first:
                pool.wait_ge(s["filled"], 1)
                one = t["ones"][:, :]
                nc.gpsimd.affine_select(out=t["ident"][:, :], in_=one, compare_op=ALU.is_equal, fill=0.0, base=0,
                                        pattern=[[-1, P]], channel_multiplier=1)
                nc.gpsimd.affine_select(out=t["upto"][:, :], in_=one, compare_op=ALU.is_ge, fill=0.0, base=0,
                                        pattern=[[1, P]], channel_multiplier=-1)
                nc.gpsimd.affine_select(out=t["after"][:, :], in_=one, compare_op=ALU.is_gt, fill=0.0, base=0,
                                        pattern=[[-1, P]], channel_multiplier=1).then_inc(s["masks"], 1)
            for n, job in enumerate(jobs):
                if scales[n]:
                    if before(scales, n) == 0:
                        pool.wait_ge(s["gate"], sum(1 for m, q in zip(is_mod, jobs) if m and q[1] in (GA, GB)))
                    pool.wait_ge(loaded[n % NS], 16 * (n // NS + 1))
                    earlier = [m for m in range(n) if scales[m]]
                    if earlier:
                        pool.wait_ge(s["read"], earlier[-1] + 1)
                    for r in range(4):
                        last = nc.gpsimd.tensor_scalar(scaled[:, r, :], stage[n % NS][:, r, :], job[1][:, r:r + 1],
                                                       1.0, ALU.mult, ALU.mult)
                    last.then_inc(s["scaled"], 1)

        @block.scalar
        def _(act):
            if first:
                nc.scalar.preload_act_table_set("natural_log_exp_and_others")
                act.wait_ge(s["small"], 16 * 6)
                nc.scalar.activation(silu[:, 0, :], c_col[:, :], ACT.Exp, scale=-1.0).then_inc(s["exp"], 1)
            for n, job in enumerate(jobs):
                if is_mod[n]:
                    continue
                for k, (hi, _, col_scale) in enumerate(job[2]):
                    m = banks_before(n) + k
                    bank_ready(act, n, k)
                    if col_scale is None:
                        nc.scalar.copy(hi, bank[m % NB][:, :]).then_inc(s["hi"], 1)
                    else:
                        nc.scalar.activation(hi, bank[m % NB][:, :], ACT.Copy, scale=col_scale).then_inc(s["hi"], 1)

        @block.vector
        def _(dve):
            if first:
                nc.vector.memset(t["ones"][:, :], 1.0).then_inc(s["filled"], 1)
                nc.vector.memset(t["minus_half"][:, :], -0.5)
                nc.vector.memset(t["zeros"][:, :], 0.0)
                dve.wait_ge(s["exp"], 1)
                nc.vector.tensor_scalar(silu[:, 1, :], silu[:, 0, :], 1.0, None, ALU.add).then_inc(s["one"], 1)
                dve.wait_ge(s["one"], 1)
                nc.vector.reciprocal(silu[:, 2, :], silu[:, 1, :]).then_inc(s["one"], 1)
                dve.wait_ge(s["one"], 2)
                nc.vector.tensor_tensor(t["silu_c"][:, :], c_col[:, :], silu[:, 2, :], ALU.mult).then_inc(s["silu"], 1)
                dve.wait_ge(s["masks"], 1)
                nc.vector.tensor_copy(t["after_r"][:, :], t["after"][:, :])
            steps = 0
            for n, job in enumerate(jobs):
                if is_mod[n]:
                    v, m = job[1], before(is_mod, n)
                    dve.wait_ge(s["read"], n + 1)
                    nc.vector.tensor_copy(t["mod"][:, v, :], mod_ps[m % 2][:, 0:KD]).then_inc(s["mod_out"], 1)
                    dve.wait_ge(s["mod_out"], m + 1)
                    g = t["mod"][:, v, :]
                    if v in (CA, CB):
                        nc.vector.tensor_scalar(t["ca1" if v == CA else "cb1"][:, :], g, 1.0, None, ALU.add)
                    if v in (GA, GB):
                        nc.vector.tensor_scalar(sign[:, 0, :], g, 0.0, 2.0, ALU.is_ge, ALU.mult)
                        nc.vector.scalar_tensor_tensor(out=sign[:, 1, :], in0=g, scalar=-1.0, in1=g, op0=ALU.mult,
                                                       op1=ALU.max).then_inc(s["step"], 1)
                        dve.wait_ge(s["step"], steps + 1)
                        nc.vector.tensor_scalar(sign[:, 2, :], sign[:, 1, :], 0.25, None, ALU.max)
                        nc.vector.tensor_scalar(sign[:, 3, :], sign[:, 0, :], -1.0, None, ALU.add).then_inc(s["step"], 1)
                        dve.wait_ge(s["step"], steps + 2)
                        steps += 2
                        nc.vector.tensor_tensor(t["ga" if v == GA else "gb"][:, :], sign[:, 2, :], sign[:, 3, :],
                                                ALU.mult).then_inc(s["gate"], 1)
                        dve.wait_ge(s["gate"], steps // 2)
                    continue
                for k, (hi, lo, col_scale) in enumerate(job[2]):
                    m = banks_before(n) + k
                    dve.wait_ge(s["hi"], m + 1)
                    if col_scale is None:
                        nc.vector.tensor_tensor(lo, bank[m % NB][:, :], hi.bitcast(F32),
                                                ALU.subtract).then_inc(s["lo"], 1)
                    else:
                        nc.vector.scalar_tensor_tensor(out=lo, in0=bank[m % NB][:, :], scalar=col_scale,
                                                       in1=hi.bitcast(F32), op0=ALU.mult,
                                                       op1=ALU.subtract).then_inc(s["lo"], 1)
                if n == 1 and first:
                    dve.wait_ge(s["wd"], 1)
                    wd_t = wd_ps[:, 0:KD * H].rearrange("p (k h) -> p k h", k=KD)
                    nc.vector.tensor_copy(t["wd_hi"][:, :, :], wd_t).then_inc(s["wd_hi"], 1)
                    dve.wait_ge(s["wd_hi"], 1)
                    nc.vector.tensor_tensor(t["wd_lo"][:, :, :], wd_t, t["wd_hi"][:, :, :].bitcast(F32), ALU.subtract)
                    vecs = wd_ps[:, KD * H:KD * H + NV]
                    nc.vector.tensor_copy(t["mu"][:, :, :],
                                          vecs[:, 0:2 * KD].rearrange("p (m k) -> p m k", m=2)).then_inc(s["mu"], 1)
                    nc.vector.tensor_copy(t["norm_w"][:, :], vecs[:, 2 * KD:])
                    dve.wait_ge(s["mu"], 1)
                    nc.vector.tensor_scalar(t["one_minus_mu"][:, :, :], t["mu"][:, :, :], -1.0, 1.0, ALU.mult, ALU.add)


KINDS = "gqk"
USES = [(kind, b) for b in range(4) for kind in KINDS] + [("v", 0), ("v", 1)]
USES += [(kind, b) for b in range(4, NP) for kind in KINDS] + [("v", 2), ("v", 3)]
BY_ACT = [u for u in USES if u[0] != "k"]
NU, NA = len(USES), len(BY_ACT)


def attention_pass(nc, t, W, x_v, o_v):
    with ExitStack() as ctx:
        def sb(name, shape, dt=F32):
            return ctx.enter_context(nc.sbuf_tensor(name, shape, dt))

        def ps(name, shape):
            return ctx.enter_context(nc.psum_tensor(name, shape, F32))

        x = sb("x", [P, NC, DM])
        hT = sb("hT", [P, KD, T])
        h_hi = sb("h_hi", [P, KD, T], F32R)
        h_lo = sb("h_lo", [P, KD, T], F32R)
        q = sb("q", [P, NP, T])
        kg = sb("kg", [P, NP, T])
        kpad = sb("kpad", [P, 2, T])
        v = sb("v", [P, NC, HID])
        o = sb("o", [P, 2, NC, P])
        decay = sb("decay", [P, 4, CH])
        prob = sb("prob", [P, 4, CH])
        r_hi = sb("r_hi", [P, NC, 2, CH], F32R)
        r_lo = sb("r_lo", [P, NC, 2, CH], F32R)
        state = sb("state", [P, NP, P])
        mid = sb("mid", [P, P])
        kw = sb("kw", [P, NC, P])
        inter = sb("inter", [P, NC, P])
        gate = sb("gate", [P, 3, T])
        stats = sb("stats", [P, NC, 6])
        mv = sb("mv", [P, NC, 2])
        var_eps = sb("var_eps", [P, NC])
        rstd = sb("rstd", [P, NC])
        zt = sb("zt", [H, 5, T])
        g_raw = sb("g_raw", [P, NC * H])
        g_hi = sb("g_hi", [P, NC * H], F32R)
        g_lo = sb("g_lo", [P, NC * H], F32R)
        w_new = sb("w_new", [P, 3, NC * H])
        w_cur = sb("w_cur", [P, 3, NC, H])

        tick = sb("tick", [P, 2])

        psA = ps("psA", [P, 4, CH])
        psS = ps("psS", [P, 4, CH])
        psK = ps("psK", [P, 4, P])
        psO = ps("psO", [P, 4, P])
        psJ = [ps(f"psJ{n}", [P, 512]) for n in range(2)]
        psT = ps("psT", [P, KD, T])
        psZ = psT[0:H, 0, :]
        psG = psT[:, 1, 0:NC * H]
        psC = psT[:, 1, NC * H:4 * NC * H]

        s = signals(nc, ctx, "a", "x stats mv var_eps rstd xn xT hT h_hi h_lo z zb softin e1 l soft gT g_turned g_raw cum w_new g_hi g cur "
                 "proj by_act k gate1 gate2 r a e mask kpad score prob kT kw inc mid state pv gla inter o zero")
        store = [ctx.enter_context(nc.semaphore(f"a_store{n}")) for n in range(2)]
        block = ctx.enter_context(nc.Block())

        def evacuated(eng, i, u):
            if u < 0:
                i, u = i - 1, u + NU
                if isinstance(i, int) and i < 0:
                    return
            kind, b = USES[u]
            if kind == "k":
                hold(eng, s["k"], NP * i + b + 1)
            else:
                hold(eng, s["by_act"], NA * i + BY_ACT.index(USES[u]) + 1)

        def proj_done(i, use):
            return NU * i + USES.index(use) + 1

        def act_done(i, use):
            return NA * i + BY_ACT.index(use) + 1

        def sp_tile(sp, i, gla, proj, prep):
            j = i - 1
            if prep:
                hold(sp, s["xT"], KD * (i + 1))
                sp.dma_start(x[:, :, :], x_v[i + 1]).then_inc(s["x"], 16)
            if gla:
                for p in range(NP):
                    sp.wait_ge(s["o"], NP * j + p + 1)
                    sp.dma_start(o_v[j, :, :, p * P:(p + 1) * P], o[:, p % 2, :, :]).then_inc(store[p % 2], 16)

        @block.sync
        def _(sp):
            sp.dma_start(x[:, :, :], x_v[0]).then_inc(s["x"], 16)
            sp_tile(sp, 0, False, True, True)
            sp_tile(sp, 1, True, True, True)
            with sp.Fori(2, NT - 1) as i:
                sp_tile(sp, i, True, True, True)
            sp_tile(sp, NT - 1, True, True, False)
            sp_tile(sp, NT, True, False, False)
            for n in range(2):
                sp.wait_ge(store[n], 16 * NP // 2 * NT)

        def project(i, kind, b, pe):
            u = USES.index((kind, b))
            bank = psJ[u % 2]
            if u == 0:
                pe.wait_ge(s["h_lo"], i + 1)
            evacuated(pe, i, u - 2)
            for k in range(KD):
                if kind == "v":
                    c, half = b % 2, b // 2
                    hh, hl = (a[:, k, c * CH:(c + 1) * CH] for a in (h_hi, h_lo))
                    wh, wl = (a[:, k, half * 512:(half + 1) * 512] for a in W["v"])
                    last = three_passes(nc, bank[:, :], hh, hl, wh, wl, k == 0, k == KD - 1)
                else:
                    wh, wl = (a[:, k, b * P:(b + 1) * P] for a in W[kind])
                    last = three_passes(nc, bank[:, 0:T], wh, wl, h_hi[:, k, :], h_lo[:, k, :], k == 0, k == KD - 1)
            last.then_inc(s["proj"], 1)

        def turn_x(pe, n):
            pe.wait_ge(s["xn"], NC * (n + 1))
            hold(pe, s["hT"], KD * n)
            hold(pe, s["w_new"], n)
            for k in range(KD):
                for c in range(NC):
                    last = nc.tensor.transpose(psT[:, k, c * CH:(c + 1) * CH], x[:, c, k * P:(k + 1) * P],
                                               t["ident"][:, :])
                last.then_inc(s["xT"], 1)

        def pe_tile(pe, i, gla, proj, prep):
            j = i - 1
            for p in range(NP):
                n = NP * j + p
                if gla:
                    pe.wait_ge(s["r"], n + 1)
                    hold(pe, s["e"], n)
                    nc.tensor.matmul(psA[:, :, :], t["after_r"][:, :], r_hi[:, :, :, :], start=True, stop=False)
                    nc.tensor.matmul(psA[:, :, :], t["after_r"][:, :], r_lo[:, :, :, :], start=False,
                                     stop=True).then_inc(s["a"], 1)
                    pe.wait_ge(s["kpad"], n + 1)
                    hold(pe, s["prob"], n)
                    for c in range(NC):
                        for h in range(2):
                            last = nc.tensor.matmul(psS[:, 2 * c + h, :], kpad[:, h, c * CH:(c + 1) * CH],
                                                    q[:, p, c * CH:(c + 1) * CH], start=True, stop=True)
                    last.then_inc(s["score"], 1)
                    hold(pe, s["mid"], n)
                    hold(pe, s["state"], n)
                    for c in range(NC):
                        last = nc.tensor.transpose(psK[:, c, :], kg[:, p, c * CH:(c + 1) * CH], t["ident"][:, :])
                    last.then_inc(s["kT"], 1)
                if p == 0 and gla:
                    project(j, "v", 2, pe)
                if p > 0 and proj:
                    project(i, "g", p - 1, pe)
                if gla:
                    pe.wait_ge(s["kw"], n + 1)
                    pe.wait_ge(s["by_act"], act_done(j, ("v", 1 + 2 * (p // 4))) if p else act_done(j, ("v", 1)))
                    for c in range(NC):
                        last = nc.tensor.matmul(psK[:, 2 + c, :], kw[:, c, :], v[:, c, p * P:(p + 1) * P],
                                                start=True, stop=True)
                    last.then_inc(s["inc"], 1)
                    pe.wait_ge(s["prob"], n + 1)
                    hold(pe, s["o"], n)
                    for c in range(NC):
                        for h in range(2):
                            nc.tensor.matmul(psO[:, c, h * DH:(h + 1) * DH], prob[:, 2 * c + h, :],
                                             v[:, c, p * P + h * DH:p * P + (h + 1) * DH], start=True, stop=True)
                    nc.tensor.matmul(psO[:, 2, :], q[:, p, 0:CH], state[:, p, :], start=True,
                                     stop=True).then_inc(s["pv"], 1)
                if p == 0 and gla:
                    project(j, "v", 3, pe)
                if p > 0 and proj:
                    project(i, "q", p - 1, pe)
                    if p == 4:
                        pe.wait_ge(s["gT"], i + 1)
                    project(i, "k", p - 1, pe)
                if gla:
                    pe.wait_ge(s["mid"], n + 1)
                    nc.tensor.matmul(psO[:, 3, :], q[:, p, CH:T], mid[:, :], start=True, stop=True).then_inc(s["gla"], 1)
                if p == 1 and proj:
                    for k in range(KD):
                        last = three_passes(nc, psZ, t["wd_hi"][:, k, :], t["wd_lo"][:, k, :], h_hi[:, k, :],
                                            h_lo[:, k, :], k == 0, k == KD - 1)
                    last.then_inc(s["z"], 1)
                if p == 4 and proj:
                    for c in range(NC):
                        last = nc.tensor.transpose(psG[:, c * H:(c + 1) * H], zt[:, 4, c * CH:(c + 1) * CH],
                                                   t["ident"][0:H, 0:H])
                    last.then_inc(s["g_turned"], 1)
                if p == 5 and proj:
                    pe.wait_ge(s["g_raw"], i + 1)
                    for n3, m in enumerate(("upto", "after", "ones")):
                        last = nc.tensor.matmul(psC[:, n3 * NC * H:(n3 + 1) * NC * H], t[m][:, :], g_raw[:, :],
                                                start=True, stop=True)
                    last.then_inc(s["cum"], 1)
                if p == 4 and proj:
                    project(i, "v", 0, pe)
                    project(i, "v", 1, pe)
                if p == 6 and prep:
                    turn_x(pe, i + 1)
            if proj:
                for kind in KINDS:
                    project(i, kind, NP - 1, pe)

        @block.tensor
        def _(pe):
            turn_x(pe, 0)
            pe_tile(pe, 0, False, True, True)
            pe_tile(pe, 1, True, True, True)
            with pe.Fori(2, NT - 1) as i:
                pe_tile(pe, i, True, True, True)
            pe_tile(pe, NT - 1, True, True, False)
            pe_tile(pe, NT, True, False, False)

        def affine_h(act, n):
            hold(act, s["h_lo"], n)
            for k in range(KD):
                act.wait_ge(s["xT"], KD * n + 2 * (k // 2) + 2)
                nc.scalar.activation(hT[:, k, :], psT[:, k, :], ACT.Identity, bias=t["mod"][:, SA, k:k + 1],
                                     scale=t["ca1"][:, k:k + 1]).then_inc(s["hT"], 1)

        def copy_v(act, i, b):
            c, half = b % 2, b // 2
            act.wait_ge(s["proj"], proj_done(i, ("v", b)))
            hold(act, s["gla"], NP * (i - 1) + 4 * (half + 1))
            nc.scalar.copy(v[:, c, half * 512:(half + 1) * 512],
                           psJ[USES.index(("v", b)) % 2][:, :]).then_inc(s["by_act"], 1)

        def copy_qg(act, i, b):
            act.wait_ge(s["proj"], proj_done(i, ("g", b)))
            hold(act, s["gate2"], NP * i + b)
            nc.scalar.activation(gate[:, 0, :], psJ[USES.index(("g", b)) % 2][:, 0:T], ACT.Exp,
                                 scale=-1.0).then_inc(s["by_act"], 1)
            act.wait_ge(s["proj"], proj_done(i, ("q", b)))
            hold(act, s["gla"], NP * (i - 1) + b + 1)
            nc.scalar.copy(q[:, b, :], psJ[USES.index(("q", b)) % 2][:, 0:T]).then_inc(s["by_act"], 1)

        def pad_k(act, i, p):
            n = NP * i + p
            hold(act, s["k"], n + 1)
            hold(act, s["score"], n)
            nc.scalar.copy(kpad[0:DH, 0, :], kg[0:DH, p, :])
            nc.scalar.copy(kpad[DH:P, 1, :], kg[DH:P, p, :]).then_inc(s["kpad"], 1)

        def act_tile(act, i, gla, proj, prep):
            j = i - 1
            for p in range(NP):
                n = NP * j + p
                if gla:
                    act.wait_ge(s["a"], n + 1)
                    hold(act, s["prob"], n)
                    nc.scalar.activation(decay[:, :, :], psA[:, :, :], ACT.Exp).then_inc(s["e"], 1)
                    if p + 1 < NP:
                        pad_k(act, j, p + 1)
                    elif proj:
                        pad_k(act, i, 0)
                if p == 0 and gla:
                    copy_v(act, j, 2)
                    copy_v(act, j, 3)
                if p > 0 and proj:
                    copy_qg(act, i, p - 1)
                if p == 2 and proj:
                    act.wait_ge(s["softin"], i + 1)
                    nc.scalar.activation(zt[:, 2, :], zt[:, 1, :], ACT.Exp).then_inc(s["e1"], 1)
                    act.wait_ge(s["e1"], i + 1)
                    nc.scalar.activation(zt[:, 3, :], zt[:, 2, :], ACT.Ln, bias=1.0).then_inc(s["l"], 1)
                if p == 4 and proj:
                    copy_v(act, i, 0)
                    copy_v(act, i, 1)
                if p == 6 and proj:
                    act.wait_ge(s["cum"], i + 1)
                    hold(act, s["cur"], i)
                    nc.scalar.activation(w_new[:, :, :], psC.rearrange("p (a b) -> p a b", a=3),
                                         ACT.Exp).then_inc(s["w_new"], 1)
                if p == 6 and prep:
                    affine_h(act, i + 1)
            if proj:
                copy_qg(act, i, NP - 1)
                if not gla:
                    pad_k(act, i, 0)

        @block.scalar
        def _(act):
            affine_h(act, 0)
            act.wait_ge(s["zero"], 1)
            act_tile(act, 0, False, True, True)
            act_tile(act, 1, True, True, True)
            with act.Fori(2, NT - 1) as i:
                act_tile(act, i, True, True, True)
            act_tile(act, NT - 1, True, True, False)
            act_tile(act, NT, True, False, False)

        def norm_stats(dve, n):
            dve.wait_ge(s["x"], 16 * (n + 1))
            for c in range(NC):
                last = nc.vector.bn_stats(stats[:, c, :], x[:, c, :])
            last.then_inc(s["stats"], 1)
            dve.wait_ge(s["stats"], n + 1)
            nc.vector.memset(tick[:, 0:1], 0.0)
            for c in range(NC):
                last = nc.vector.bn_aggr(mv[:, c, :], stats[:, c, :])
            last.then_inc(s["mv"], 1)
            dve.wait_ge(s["mv"], n + 1)
            nc.vector.tensor_scalar(var_eps[:, :], mv[:, :, 1], LN_EPS, None, ALU.add).then_inc(s["var_eps"], 1)

        def norm_x(dve, n):
            dve.wait_ge(s["rstd"], n + 1)
            for c in range(NC):
                nc.vector.tensor_scalar(x[:, c, :], x[:, c, :], mv[:, c, 0:1], rstd[:, c:c + 1], ALU.subtract,
                                        ALU.mult).then_inc(s["xn"], 1)

        def split_h(dve, i):
            dve.wait_ge(s["hT"], KD * (i + 1))
            hold(dve, s["proj"], NU * i)
            nc.vector.tensor_copy(h_hi[:, :, :], hT[:, :, :]).then_inc(s["h_hi"], 1)
            dve.wait_ge(s["h_hi"], i + 1)
            nc.vector.tensor_tensor(h_lo[:, :, :], hT[:, :, :], h_hi[:, :, :].bitcast(F32),
                                    ALU.subtract).then_inc(s["h_lo"], 1)

        def gate_start(dve, i, b):
            dve.wait_ge(s["by_act"], act_done(i, ("g", b)))
            nc.vector.tensor_scalar(gate[:, 1, :], gate[:, 0, :], 1.0, None, ALU.add).then_inc(s["gate1"], 1)
            dve.wait_ge(s["gate1"], NP * i + b + 1)
            nc.vector.reciprocal(gate[:, 2, :], gate[:, 1, :]).then_inc(s["gate2"], 1)

        def gate_end(dve, i, b):
            dve.wait_ge(s["gate2"], NP * i + b + 1)
            dve.wait_ge(s["proj"], proj_done(i, ("k", b)))
            hold(dve, s["gla"], NP * (i - 1) + b + 1)
            nc.vector.tensor_tensor(kg[:, b, :], psJ[USES.index(("k", b)) % 2][:, 0:T], gate[:, 2, :],
                                    ALU.mult).then_inc(s["k"], 1)

        def dve_tile(dve, i, gla, proj, prep):
            j = i - 1
            for p in range(NP):
                n = NP * j + p
                if gla:
                    if p == 0:
                        dve.wait_ge(s["cur"], i)
                    dve.wait_ge(s["kT"], n + 1)
                    hold(dve, s["inc"], n)
                    nc.vector.tensor_tensor(
                        kw[:, :, :].rearrange("p c (h d) -> p c h d", h=2),
                        psK[:, 0:2, :].rearrange("p c (h d) -> p c h d", h=2),
                        w_cur[:, 1, :, 2 * p:2 * p + 2].unsqueeze(3).to_broadcast([P, NC, 2, DH]),
                        ALU.mult).then_inc(s["kw"], 1)
                    dve.wait_ge(s["mask"], n + 1)
                    dve.wait_ge(s["score"], n + 1)
                    hold(dve, s["pv"], n)
                    nc.vector.tensor_tensor(prob[:, :, :], decay[:, :, :], psS[:, :, :], ALU.mult).then_inc(s["prob"], 1)
                    dve.wait_ge(s["inc"], n + 1)
                    hold(dve, s["gla"], n)
                    for h in range(2):
                        r = slice(h * DH, (h + 1) * DH)
                        last = nc.vector.scalar_tensor_tensor(
                            out=mid[r, r], in0=state[r, p, r], scalar=w_cur[r, 2, 0, 2 * p + h:2 * p + h + 1],
                            in1=psK[r, 2, r], op0=ALU.mult, op1=ALU.add)
                    last.then_inc(s["mid"], 1)
                if p > 0 and proj:
                    gate_start(dve, i, p - 1)
                if gla:
                    dve.wait_ge(s["mid"], n + 1)
                    dve.wait_ge(s["pv"], n + 1)
                    for h in range(2):
                        r = slice(h * DH, (h + 1) * DH)
                        last = nc.vector.scalar_tensor_tensor(
                            out=state[r, p, r], in0=mid[r, r], scalar=w_cur[r, 2, 1, 2 * p + h:2 * p + h + 1],
                            in1=psK[r, 3, r], op0=ALU.mult, op1=ALU.add)
                    last.then_inc(s["state"], 1)
                if p == 0 and proj:
                    split_h(dve, i)
                if p == 2 and proj:
                    dve.wait_ge(s["z"], i + 1)
                    nc.vector.tensor_scalar(zt[:, 0, :], psZ, t["bd"][:, 0:1], None, ALU.add).then_inc(s["zb"], 1)
                    dve.wait_ge(s["zb"], i + 1)
                    nc.vector.scalar_tensor_tensor(out=zt[:, 1, :], in0=zt[:, 0, :], scalar=-1.0, in1=zt[:, 0, :],
                                                   op0=ALU.mult, op1=ALU.min).then_inc(s["softin"], 1)
                if p == 3 and proj:
                    dve.wait_ge(s["l"], i + 1)
                    nc.vector.scalar_tensor_tensor(out=zt[:, 1, :], in0=zt[:, 0, :], scalar=0.0, in1=zt[:, 3, :],
                                                   op0=ALU.max, op1=ALU.add).then_inc(s["soft"], 1)
                    dve.wait_ge(s["soft"], i + 1)
                    nc.vector.tensor_scalar(zt[:, 4, :], zt[:, 1, :], -1.0, None, ALU.mult).then_inc(s["gT"], 1)
                if p == 5 and proj:
                    dve.wait_ge(s["g_turned"], i + 1)
                    nc.vector.tensor_copy(g_raw[:, :], psG).then_inc(s["g_raw"], 1)
                if p == 7 and proj:
                    hold(dve, s["r"], NP * i if gla else 0)
                    dve.wait_ge(s["g_raw"], i + 1)
                    nc.vector.tensor_copy(g_hi[:, :], g_raw[:, :]).then_inc(s["g_hi"], 1)
                    dve.wait_ge(s["g_hi"], i + 1)
                    nc.vector.tensor_tensor(g_lo[:, :], g_raw[:, :], g_hi[:, :].bitcast(F32),
                                            ALU.subtract).then_inc(s["g"], 1)
                if p == 4 and prep:
                    norm_stats(dve, i + 1)
                if p == 5 and prep:
                    norm_x(dve, i + 1)
                if p > 0 and proj:
                    gate_end(dve, i, p - 1)
                if gla:
                    dve.wait_ge(s["gla"], n + 1)
                    nc.vector.tensor_tensor(
                        inter[:, :, :].rearrange("p c (h d) -> p c h d", h=2),
                        psO[:, 2:4, :].rearrange("p c (h d) -> p c h d", h=2),
                        w_cur[:, 0, :, 2 * p:2 * p + 2].unsqueeze(3).to_broadcast([P, NC, 2, DH]),
                        ALU.mult).then_inc(s["inter"], 1)
                    dve.wait_ge(s["inter"], n + 1)
                    hold(dve, store[p % 2], 16 * (NP // 2 * j + p // 2))
                    nc.vector.tensor_tensor(o[:, p % 2, :, :], inter[:, :, :], psO[:, 0:2, :], ALU.add).then_inc(s["o"], 1)
            if proj:
                dve.wait_ge(s["w_new"], i + 1)
                nc.vector.tensor_copy(w_cur[:, :, :, :].rearrange("p a c h -> p (a c h)"),
                                      w_new[:, :, :].rearrange("p a b -> p (a b)")).then_inc(s["cur"], 1)
                gate_start(dve, i, NP - 1)
                gate_end(dve, i, NP - 1)

        @block.vector
        def _(dve):
            nc.vector.memset(state[:, :, :], 0.0)
            nc.vector.memset(mid[:, :], 0.0)
            nc.vector.memset(kpad[:, :, :], 0.0).then_inc(s["zero"], 1)
            dve.wait_ge(s["zero"], 1)
            norm_stats(dve, 0)
            norm_x(dve, 0)
            dve_tile(dve, 0, False, True, True)
            dve_tile(dve, 1, True, True, True)
            with dve.Fori(2, NT - 1) as i:
                dve_tile(dve, i, True, True, True)
            dve_tile(dve, NT - 1, True, True, False)
            dve_tile(dve, NT, True, False, False)

        def rsqrt(pool, n):
            pool.wait_ge(s["var_eps"], n + 1)
            nc.gpsimd.tensor_tensor(rstd[:, :], var_eps[:, :], t["minus_half"][:, 0:NC], ALU.pow).then_inc(s["rstd"], 1)

        def spread_g(pool, i, p):
            if p == 0:
                pool.wait_ge(s["g"], i + 1)
            hold(pool, s["a"], NP * i + p)
            for dst, g in ((r_hi, g_hi), (r_lo, g_lo)):
                gg = g[:, :].bitcast(F32).rearrange("p (c h) -> p c h", c=NC)[:, :, 2 * p:2 * p + 2]
                last = nc.gpsimd.tensor_tensor(dst[:, :, :, :], gg.unsqueeze(3).to_broadcast([P, NC, 2, CH]),
                                               t["upto"][:, :].unsqueeze(1).unsqueeze(1).to_broadcast([P, NC, 2, CH]),
                                               ALU.mult)
            last.then_inc(s["r"], 1)

        def pool_tile(pool, i, gla, proj, prep):
            j = i - 1
            for p in range(NP):
                if gla:
                    pool.wait_ge(s["e"], NP * j + p + 1)
                    nc.gpsimd.tensor_tensor(tick[:, 1:2], t["zeros"][:, :], t["zeros"][:, :],
                                            ALU.mult)
                    nc.gpsimd.affine_select(out=decay[:, :, :], in_=decay[:, :, :], compare_op=ALU.is_ge, fill=0.0,
                                            base=0, pattern=[[0, 4], [1, CH]], channel_multiplier=-1).then_inc(s["mask"], 1)
                    if p + 1 < NP:
                        spread_g(pool, j, p + 1)
                    elif proj:
                        spread_g(pool, i, 0)
                if p == 4 and prep:
                    rsqrt(pool, i + 1)
            if proj and not gla:
                spread_g(pool, i, 0)

        @block.gpsimd
        def _(pool):
            rsqrt(pool, 0)
            pool_tile(pool, 0, False, True, True)
            pool_tile(pool, 1, True, True, True)
            with pool.Fori(2, NT - 1) as i:
                pool_tile(pool, i, True, True, True)
            pool_tile(pool, NT - 1, True, True, False)
            pool_tile(pool, NT, True, False, False)


def output_pass(nc, t, W, x_v, o_v, out_v):
    with ExitStack() as ctx:
        def sb(name, shape, dt=F32):
            return ctx.enter_context(nc.sbuf_tensor(name, shape, dt))

        def ps(name, shape):
            return ctx.enter_context(nc.psum_tensor(name, shape, F32))

        xn = sb("xn", [P, NC, DM])
        hT = sb("hT2", [P, KD, T])
        h_hi = sb("h_hi2", [P, KD, T], F32R)
        h_lo = sb("h_lo2", [P, KD, T], F32R)
        o = sb("o_rows", [P, NC, HID])
        og = sb("og", [P, 2, 512])
        z_hi = sb("z_hi", [P, NP, T], F32R)
        z_lo = sb("z_lo", [P, NP, T], F32R)
        x1 = sb("x1", [P, NC, DM])
        x1_old = sb("x1_old", [P, NC, DM])
        x2n = sb("x2n", [P, NC, DM])
        h2 = sb("h2", [P, KD, T + 1])
        mix = sb("mix", [P, KD, T])
        prev = sb("prev", [P, KD, T])
        ra_hi = sb("ra_hi", [P, KD, T], F32R)
        ra_lo = sb("ra_lo", [P, KD, T], F32R)
        xk_hi = sb("xk_hi", [P, KD, T], F32R)
        xk_lo = sb("xk_lo", [P, KD, T], F32R)
        r = sb("r_gate", [P, NC, DM])
        relu = sb("relu", [P, 2, 2, T])
        ss = sb("ss", [P, NC])
        stats = sb("stats2", [P, 2, NC, 6])
        mv = sb("mv2", [P, 2, NC, 2])
        var_eps = sb("var_eps2", [P, 3, NC])
        rstd = sb("rstd2", [P, 3, NC])

        tick = sb("tick2", [P, 1])

        psT = ps("psT2", [P, KD, T])
        psG = [ps(f"psG{n}", [P, 512]) for n in range(2)]
        psR = [ps(f"psR{n}", [P, 512]) for n in range(2)]
        psW = [ps(f"psW{n}", [P, 512]) for n in range(2)]
        psZ = psG + psR
        psK = psW + psG

        s = signals(nc, ctx, "b", "xa xb ol st1 mv1 ve1 rstd1 xn xT hT h_hi h_lo og sg sq ve3 rstd3 z tz zh zl wo x1 "
                 "st2 mv2 ve2 rstd2 xn2 xT2 h2 prev mixr xr_hi xr prevk mixk xk_hi xk last rr rs kt relu k2 ka_hi ka "
                 "kv fin1 fin keep store zero")
        block = ctx.enter_context(nc.Block())

        def sp_tile(sp, i, att, ffn, prep):
            j = i - 1
            if prep:
                sp.wait_ge(s["xT"], KD * (i + 1))
                sp.dma_start(xn[:, :, :], x_v[i + 1]).then_inc(s["xa"], 16)
            if att:
                hold(sp, s["keep"], i)
                sp.dma_start(x1[:, :, :], x_v[i]).then_inc(s["xb"], 16)
            if prep:
                sp.wait_ge(s["tz"], 4 * (i + 1))
                sp.dma_start(o[:, :, :], o_v[i + 1]).then_inc(s["ol"], 16)
            if ffn:
                for c in range(NC):
                    sp.wait_ge(s["fin"], NC * j + c + 1)
                    sp.dma_start(out_v[j, :, c, :], r[:, c, :]).then_inc(s["store"], 16)

        @block.sync
        def _(sp):
            sp.dma_start(xn[:, :, :], x_v[0]).then_inc(s["xa"], 16)
            sp.dma_start(o[:, :, :], o_v[0]).then_inc(s["ol"], 16)
            sp_tile(sp, 0, True, False, True)
            sp_tile(sp, 1, True, True, True)
            with sp.Fori(2, NT - 1) as i:
                sp_tile(sp, i, True, True, True)
            sp_tile(sp, NT - 1, True, True, False)
            sp_tile(sp, NT, False, True, False)
            sp.wait_ge(s["store"], 16 * NC * NT)

        def turn(pe, src, sem):
            for k in range(KD):
                for c in range(NC):
                    last = nc.tensor.transpose(psT[:, k, c * CH:(c + 1) * CH], src[:, c, k * P:(k + 1) * P],
                                               t["ident"][:, :])
                last.then_inc(sem, 1)

        def rows_product(bank, a_hi, a_lo, w, c, half, blocks, ready=()):
            for k in range(blocks):
                for at, eng, sem, value in ready:
                    if at == k:
                        eng.wait_ge(sem, value)
                ah, al = (a[:, k, c * CH:(c + 1) * CH] for a in (a_hi, a_lo))
                wh, wl = (a[:, k, half * 512:(half + 1) * 512] for a in w)
                last = three_passes(nc, bank[:, :], ah, al, wh, wl, k == 0, k == blocks - 1)
            return last

        def pe_tile(pe, i, att, ffn, prep):
            j = i - 1
            if att:
                pe.wait_ge(s["h_lo"], i + 1)
                for n in range(4):
                    if n < 2:
                        hold(pe, s["relu"], KD * (i - 1))
                    else:
                        pe.wait_ge(s["sg"], 4 * i + n - 1)
                    rows_product(psG[n % 2], h_hi, h_lo, W["og"], n // 2, n % 2, KD).then_inc(s["og"], 1)
            if ffn:
                pe.wait_ge(s["xn2"], NC * (j + 1))
                hold(pe, s["hT"], KD * (i + 1 if att else i))
                hold(pe, s["h2"], KD * j)
                turn(pe, x2n, s["xT2"])
            if att:
                for n in range(4):
                    c, half = n // 2, n % 2
                    pe.wait_ge(s["z"], 4 * i + n + 1)
                    if n == 0:
                        pe.wait_ge(s["sg"], 4 * (i + 1))
                    if n == 2:
                        hold(pe, s["fin1"], NC * j)
                    for b in range(4):
                        last = nc.tensor.transpose(psZ[n][:, b * CH:(b + 1) * CH],
                                                   o[:, c, (4 * half + b) * P:(4 * half + b + 1) * P], t["ident"][:, :])
                    last.then_inc(s["tz"], 1)
                hold(pe, s["relu"], KD * j)
                for c in range(NC):
                    ready = [(4 * half, pe, s["zl"], 4 * i + 2 * c + half + 1) for half in range(2)]
                    rows_product(psW[c], z_hi, z_lo, W["o"], c, 0, NP, ready).then_inc(s["wo"], 1)
            if ffn:
                pe.wait_ge(s["xr"], j + 1)
                if att:
                    pe.wait_ge(s["zl"], 4 * (i + 1))
                hold(pe, s["fin1"], NC * j)
                for c in range(NC):
                    rows_product(psR[c], ra_hi, ra_lo, W["r"], c, 0, KD).then_inc(s["rr"], 1)
            if prep:
                pe.wait_ge(s["xn"], NC * (i + 2))
                hold(pe, s["h2"], KD * (j + 1) if ffn else 0)
                turn(pe, xn, s["xT"])
            if ffn:
                pe.wait_ge(s["xk"], j + 1)
                pe.wait_ge(s["x1"], NC * (i + 1) if att else NC * i)
                hold(pe, s["relu"], KD * j)
                for n in range(KD):
                    for k in range(KD):
                        wh, wl = (a[:, k, n * P:(n + 1) * P] for a in W["k2"])
                        last = three_passes(nc, psK[n][:, 0:T], wh, wl, xk_hi[:, k, :], xk_lo[:, k, :], k == 0,
                                            k == KD - 1)
                    last.then_inc(s["kt"], 1)
                pe.wait_ge(s["rs"], NC * (j + 1))
                for c in range(NC):
                    ready = [(k, pe, s["ka"], KD * j + k + 1) for k in range(KD)]
                    rows_product(psR[c], ra_hi, ra_lo, W["v2"], c, 0, KD, ready if c == 0 else ()).then_inc(s["kv"], 1)

        @block.tensor
        def _(pe):
            pe.wait_ge(s["xn"], NC)
            turn(pe, xn, s["xT"])
            pe_tile(pe, 0, True, False, True)
            pe_tile(pe, 1, True, True, True)
            with pe.Fori(2, NT - 1) as i:
                pe_tile(pe, i, True, True, True)
            pe_tile(pe, NT - 1, True, True, False)
            pe_tile(pe, NT, False, True, False)

        def affine_h(act, n, blocks):
            hold(act, s["h_lo"], n)
            for k in blocks:
                act.wait_ge(s["xT"], KD * n + 2 * (k // 2) + 2)
                nc.scalar.activation(hT[:, k, :], psT[:, k, :], ACT.Identity, bias=t["mod"][:, SA, k:k + 1],
                                     scale=t["ca1"][:, k:k + 1]).then_inc(s["hT"], 1)

        def act_tile(act, i, att, ffn, prep):
            j = i - 1

            def copy_z(n):
                c, half = n // 2, n % 2
                act.wait_ge(s["tz"], 4 * i + n + 1)
                nc.scalar.copy(z_hi[:, 4 * half:4 * half + 4, c * CH:(c + 1) * CH],
                               psZ[n][:, :].rearrange("p (b t) -> p b t", b=4)).then_inc(s["zh"], 1)

            if att:
                act.wait_ge(s["ol"], 16 * (i + 1))
                hold(act, s["ve3"], i)
                hold(act, s["z"], 4 * i)
                for c in range(NC):
                    hold(act, s["sq"], NC * i + c)
                    nc.scalar.activation(og[:, :, :], o[:, c, :].rearrange("p (b d) -> p b d", b=2), ACT.Square,
                                         accum_out=ss[:, c:c + 1]).then_inc(s["sq"], 1)
                act.wait_ge(s["sq"], NC * (i + 1))
                for n in range(4):
                    act.wait_ge(s["og"], 4 * i + n + 1)
                    if n > 1:
                        act.wait_ge(s["z"], 4 * i + n - 1)
                    nc.scalar.activation(og[:, n % 2, :], psG[n % 2][:, :], ACT.Sigmoid).then_inc(s["sg"], 1)
                hold(act, s["wo"], NC * i)
                copy_z(0)
                copy_z(1)
            if ffn:
                hold(act, s["last"], j + 1)
                for k in range(KD):
                    act.wait_ge(s["xT2"], KD * j + 2 * (k // 2) + 2)
                    nc.scalar.activation(h2[:, k, 1:T + 1], psT[:, k, :], ACT.Identity, bias=t["mod"][:, SB, k:k + 1],
                                         scale=t["cb1"][:, k:k + 1]).then_inc(s["h2"], 1)
            if att:
                copy_z(2)
                copy_z(3)
            if ffn:
                hold(act, s["store"], 16 * NC * j)
                for c in range(NC):
                    act.wait_ge(s["rr"], NC * j + c + 1)
                    nc.scalar.activation(r[:, c, :], psR[c][:, :], ACT.Sigmoid).then_inc(s["rs"], 1)
            if prep:
                affine_h(act, i + 1, (0, 1) if ffn else range(KD))
            if ffn:
                for n in range(KD):
                    act.wait_ge(s["kt"], KD * j + n + 1)
                    hold(act, s["ka"], KD * j + n - 1 if n else KD * j)
                    nc.scalar.activation(relu[:, n % 2, 0, :], psK[n][:, 0:T], ACT.Relu).then_inc(s["relu"], 1)
                    act.wait_ge(s["relu"], KD * j + n + 1)
                    nc.scalar.activation(relu[:, n % 2, 1, :], relu[:, n % 2, 0, :], ACT.Square).then_inc(s["k2"], 1)
                    if prep and n in (1, 2):
                        affine_h(act, i + 1, (n + 1,))

        @block.scalar
        def _(act):
            affine_h(act, 0, range(KD))
            act.wait_ge(s["zero"], 1)
            act_tile(act, 0, True, False, True)
            act_tile(act, 1, True, True, True)
            with act.Fori(2, NT - 1) as i:
                act_tile(act, i, True, True, True)
            act_tile(act, NT - 1, True, True, False)
            act_tile(act, NT, False, True, False)

        def row_stats(dve, which, src, n, st, m, ve):
            for c in range(NC):
                last = nc.vector.bn_stats(stats[:, which, c, :], src[:, c, :])
            last.then_inc(st, 1)
            dve.wait_ge(st, n + 1)
            nc.vector.memset(tick[:, 0:1], 0.0)
            for c in range(NC):
                last = nc.vector.bn_aggr(mv[:, which, c, :], stats[:, which, c, :])
            last.then_inc(m, 1)
            dve.wait_ge(m, n + 1)
            nc.vector.tensor_scalar(var_eps[:, which, :], mv[:, which, :, 1], LN_EPS, None, ALU.add).then_inc(ve, 1)

        def split_h(dve, n):
            dve.wait_ge(s["hT"], KD * (n + 1))
            hold(dve, s["og"], 4 * n)
            nc.vector.tensor_copy(h_hi[:, :, :], hT[:, :, :]).then_inc(s["h_hi"], 1)
            dve.wait_ge(s["h_hi"], n + 1)
            nc.vector.tensor_tensor(h_lo[:, :, :], hT[:, :, :], h_hi[:, :, :].bitcast(F32),
                                    ALU.subtract).then_inc(s["h_lo"], 1)

        def norm_first(dve, n):
            dve.wait_ge(s["rstd1"], n + 1)
            for c in range(NC):
                nc.vector.tensor_scalar(xn[:, c, :], xn[:, c, :], mv[:, 0, c, 0:1], rstd[:, 0, c:c + 1], ALU.subtract,
                                        ALU.mult).then_inc(s["xn"], 1)

        def norm_second(dve, n):
            dve.wait_ge(s["rstd2"], n + 1)
            hold(dve, s["xT2"], KD * n)
            for c in range(NC):
                nc.vector.tensor_scalar(x2n[:, c, :], x1[:, c, :], mv[:, 1, c, 0:1], rstd[:, 1, c:c + 1],
                                        ALU.subtract, ALU.mult).then_inc(s["xn2"], 1)

        def shift_mix(dve, j, m, hi, lo, s_prev, s_mix, s_hi, s_lo):
            for k in range(KD):
                last = nc.vector.tensor_scalar(prev[:, k, :], h2[:, k, 0:T], t["one_minus_mu"][:, m, k:k + 1], None,
                                               ALU.mult)
            last.then_inc(s_prev, 1)
            dve.wait_ge(s_prev, j + 1)
            for k in range(KD):
                last = nc.vector.scalar_tensor_tensor(out=mix[:, k, :], in0=h2[:, k, 1:T + 1],
                                                      scalar=t["mu"][:, m, k:k + 1], in1=prev[:, k, :],
                                                      op0=ALU.mult, op1=ALU.add)
            last.then_inc(s_mix, 1)
            dve.wait_ge(s_mix, j + 1)
            nc.vector.tensor_copy(hi[:, :, :], mix[:, :, :]).then_inc(s_hi, 1)
            dve.wait_ge(s_hi, j + 1)
            nc.vector.tensor_tensor(lo[:, :, :], mix[:, :, :], hi[:, :, :].bitcast(F32), ALU.subtract).then_inc(s_lo, 1)

        def dve_tile(dve, i, att, ffn, prep):
            j = i - 1
            if prep:
                dve.wait_ge(s["xa"], 16 * (i + 2))
                row_stats(dve, 0, xn, i + 1, s["st1"], s["mv1"], s["ve1"])
            if att:
                dve.wait_ge(s["sq"], NC * (i + 1))
                nc.vector.tensor_scalar(var_eps[:, 2, :], ss[:, :], 1.0 / HID, RMS_EPS, ALU.mult,
                                        ALU.add).then_inc(s["ve3"], 1)
                for n in range(4):
                    c, half = n // 2, n % 2
                    dve.wait_ge(s["sg"], 4 * i + n + 1)
                    rows = o[:, c, half * 512:(half + 1) * 512]
                    nc.vector.tensor_tensor(rows, rows, og[:, n % 2, :], ALU.mult).then_inc(s["z"], 1)
                hold(dve, s["wo"], NC * i)
                for n in range(4):
                    c, half = n // 2, n % 2
                    dve.wait_ge(s["zh"], 4 * i + n + 1)
                    d = (slice(None), slice(4 * half, 4 * half + 4), slice(c * CH, (c + 1) * CH))
                    nc.vector.tensor_tensor(z_lo[d], psZ[n][:, :].rearrange("p (b t) -> p b t", b=4),
                                            z_hi[d].bitcast(F32), ALU.subtract).then_inc(s["zl"], 1)
            if ffn:
                dve.wait_ge(s["h2"], KD * (j + 1))
                hold(dve, s["kv"], NC * j)
                shift_mix(dve, j, 0, ra_hi, ra_lo, s["prev"], s["mixr"], s["xr_hi"], s["xr"])
                hold(dve, s["kt"], KD * j)
                dve.wait_ge(s["xr"], j + 1)
                shift_mix(dve, j, 1, xk_hi, xk_lo, s["prevk"], s["mixk"], s["xk_hi"], s["xk"])
                dve.wait_ge(s["xk"], j + 1)
                nc.vector.tensor_copy(h2[:, :, 0:1], h2[:, :, T:T + 1]).then_inc(s["last"], 1)
            if prep:
                norm_first(dve, i + 1)
            if att:
                dve.wait_ge(s["rstd3"], i + 1)
                dve.wait_ge(s["xb"], 16 * (i + 1))
                for c in range(NC):
                    dve.wait_ge(s["wo"], NC * i + c + 1)
                    nc.vector.scalar_tensor_tensor(out=x1[:, c, :], in0=psW[c][:, :], scalar=rstd[:, 2, c:c + 1],
                                                   in1=x1[:, c, :], op0=ALU.mult, op1=ALU.add).then_inc(s["x1"], 1)
                dve.wait_ge(s["x1"], NC * (i + 1))
                row_stats(dve, 1, x1, i, s["st2"], s["mv2"], s["ve2"])
            if ffn:
                dve.wait_ge(s["rr"], NC * (j + 1))
                for n in range(KD):
                    dve.wait_ge(s["k2"], KD * j + n + 1)
                    nc.vector.tensor_copy(ra_hi[:, n, :], relu[:, n % 2, 1, :]).then_inc(s["ka_hi"], 1)
                    dve.wait_ge(s["ka_hi"], KD * j + n + 1)
                    nc.vector.tensor_tensor(ra_lo[:, n, :], relu[:, n % 2, 1, :], ra_hi[:, n, :].bitcast(F32),
                                            ALU.subtract).then_inc(s["ka"], 1)
            if prep:
                split_h(dve, i + 1)
            if att:
                norm_second(dve, i)
            if ffn:
                for c in range(NC):
                    dve.wait_ge(s["kv"], NC * j + c + 1)
                    nc.vector.tensor_tensor(r[:, c, :], psR[c][:, :], r[:, c, :], ALU.mult).then_inc(s["fin1"], 1)
                    dve.wait_ge(s["fin1"], NC * j + c + 1)
                    nc.vector.tensor_tensor(r[:, c, :], x1_old[:, c, :], r[:, c, :], ALU.add).then_inc(s["fin"], 1)
            if att:
                hold(dve, s["fin"], NC * i)
                nc.vector.tensor_copy(x1_old[:, :, :], x1[:, :, :]).then_inc(s["keep"], 1)

        @block.vector
        def _(dve):
            nc.vector.memset(h2[:, :, 0:1], 0.0).then_inc(s["zero"], 1)
            dve.wait_ge(s["zero"], 1)
            nc.vector.memset(tick[:, 0:1], 0.0).then_inc(s["last"], 1)
            dve.wait_ge(s["xa"], 16)
            row_stats(dve, 0, xn, 0, s["st1"], s["mv1"], s["ve1"])
            norm_first(dve, 0)
            split_h(dve, 0)
            dve_tile(dve, 0, True, False, True)
            dve_tile(dve, 1, True, True, True)
            with dve.Fori(2, NT - 1) as i:
                dve_tile(dve, i, True, True, True)
            dve_tile(dve, NT - 1, True, True, False)
            dve_tile(dve, NT, False, True, False)

        def rsqrt(pool, which, n, ready, done):
            pool.wait_ge(ready, n + 1)
            nc.gpsimd.tensor_tensor(rstd[:, which, :], var_eps[:, which, :], t["minus_half"][:, 0:NC],
                                    ALU.pow).then_inc(done, 1)

        def pool_tile(pool, i, att, ffn, prep):
            if prep:
                rsqrt(pool, 0, i + 1, s["ve1"], s["rstd1"])
            if att:
                rsqrt(pool, 2, i, s["ve3"], s["rstd3"])
                rsqrt(pool, 1, i, s["ve2"], s["rstd2"])

        @block.gpsimd
        def _(pool):
            rsqrt(pool, 0, 0, s["ve1"], s["rstd1"])
            pool_tile(pool, 0, True, False, True)
            pool_tile(pool, 1, True, True, True)
            with pool.Fori(2, NT - 1) as i:
                pool_tile(pool, i, True, True, True)
            pool_tile(pool, NT - 1, True, True, False)


def adaln_gla_block(nc, x, wq, wk, wv, wo, wg, wog, wd, bd, norm_w, w_r, w_k, w_v, mu_r, mu_k, c, wmod, out):
    o_rows = nc.dram_tensor("o_rows_dram", (TOK, HID), F32).ap()
    x_v = x.rearrange("a (i c p) d -> (a i) p c d", c=NC, p=CH)
    out_v = out.rearrange("a (i c p) d -> (a i) p c d", c=NC, p=CH)
    o_v = o_rows.rearrange("(i c p) d -> i p c d", c=NC, p=CH)
    with ExitStack() as ctx:
        t = {}
        for name, shape, dt in (
            ("ones", [P, P], F32), ("ident", [P, P], F32), ("upto", [P, P], F32), ("after", [P, P], F32),
            ("after_r", [P, P], F32R), ("zeros", [P, 1], F32), ("minus_half", [P, 4], F32), ("bd", [H, 1], F32),
            ("mu", [P, 2, KD], F32), ("one_minus_mu", [P, 2, KD], F32), ("norm_w", [P, NP], F32),
            ("silu_c", [P, KD], F32), ("mod", [P, 6, KD], F32), ("ca1", [P, KD], F32), ("cb1", [P, KD], F32),
            ("ga", [P, KD], F32), ("gb", [P, KD], F32), ("wd_hi", [P, KD, H], F32R), ("wd_lo", [P, KD, H], F32R),
        ):
            t[name] = ctx.enter_context(nc.sbuf_tensor(f"c_{name}", shape, dt))
        small = {"c": c, "wd": wd, "bd": bd, "mu_r": mu_r, "mu_k": mu_k, "norm_w": norm_w}
        wmod_v = wmod.rearrange("(p t) (v n) -> v p t n", t=KD, v=6)

        def pair(ctx2, name, blocks, width):
            return [ctx2.enter_context(nc.sbuf_tensor(f"w_{name}_{part}", [P, blocks, width], F32R))
                    for part in ("hi", "lo")]

        def rows(w, n):
            return w.rearrange("(n r p) d -> n p r d", r=4, p=P)[n]

        with ExitStack() as first:
            W = {name: pair(first, name, KD, HID) for name in "qgkv"}
            jobs = []
            for name, w in (("q", wq), ("g", wg), ("k", wk), ("v", wv)):
                for n in range(2):
                    cols = [(*(a[:, k, n * 512:(n + 1) * 512] for a in W[name]), None) for k in range(KD)]
                    jobs.append((rows(w, n), None, cols))
            jobs += [(wmod_v[v], v) for v in (SA, CA)]
            prepare(nc, t, jobs, "p", small)
            attention_pass(nc, t, W, x_v, o_v)
        with ExitStack() as second:
            W = {"og": pair(second, "og", KD, HID), "o": pair(second, "o", NP, DM)}
            for name in ("r", "k2", "v2"):
                W[name] = pair(second, name, KD, DM)
            jobs = [(wmod_v[v], v) for v in (GA, GB)]
            for n in range(2):
                cols = [(*(a[:, k, n * 512:(n + 1) * 512] for a in W["og"]), None) for k in range(KD)]
                jobs.append((rows(wog, n), None, cols))
            for n in range(2):
                cols = [(*(a[:, 4 * n + k, :] for a in W["o"]), t["norm_w"][:, 4 * n + k:4 * n + k + 1])
                        for k in range(4)]
                jobs.append((wo.rearrange("(r p) (n d) -> n p r d", p=P, n=2)[n], t["ga"], cols))
            for name, w, scale in (("r", w_r, None), ("k2", w_k, None), ("v2", w_v, t["gb"])):
                cols = [(*(a[:, k, :] for a in W[name]), None) for k in range(KD)]
                jobs.append((rows(w, 0), scale, cols))
            jobs += [(wmod_v[v], v) for v in (SB, CB)]
            prepare(nc, t, jobs, "s")
            output_pass(nc, t, W, x_v, o_v, out_v)


_INS = ["L0_attn_x", "L0_attn_Wq", "L0_attn_Wk", "L0_attn_Wv", "L0_attn_Wo", "L0_attn_Wg", "L0_attn_Wog", "L0_attn_Wd",
        "L0_attn_bd", "L0_attn_norm_w", "L0_ffn_W_r", "L0_ffn_W_k", "L0_ffn_W_v", "L0_ffn_mu_r", "L0_ffn_mu_k", "L0_c",
        "L0_wmod"]


def kernel(**inputs):
    import numpy as _np
    import concourse.bacc as _bacc
    from concourse import mybir as _mybir
    from concourse.bass_utils import run_bass_kernel_spmd as _run

    nc = _bacc.Bacc("TRN2", target_bir_lowering=False, num_devices=1)
    arrays, args = {}, []
    for name in _INS:
        a = _np.ascontiguousarray(inputs[name])
        arrays[f"in_{name}_dram"] = a
        args.append(nc.dram_tensor(f"in_{name}_dram", a.shape, _mybir.dt.from_np(a.dtype), kind="ExternalInput").ap())
    out = nc.dram_tensor("out_0_dram", (1, TOK, DM), _mybir.dt.float32, kind="ExternalOutput").ap()
    adaln_gla_block(nc, *args, out)
    r = _run(nc, [arrays], core_ids=[0])
    return r.results[0]["out_0_dram"]
```

```python
from contextlib import ExitStack

import concourse.bass as bass
from concourse import mybir

F32 = mybir.dt.float32
F32R = mybir.dt.float32r
ALU = mybir.AluOpType
ACT = mybir.ActivationFunctionType

P = 128
DM = 512
HID = 1024
H = 16
DH = HID // H
TOK = 8192
CH = 128
NC = 2
T = NC * CH
NT = TOK // T
KD = DM // P
NP = HID // P
LN_EPS = 1e-5
RMS_EPS = 1.1920928955078125e-07
SA, CA, GA, SB, CB, GB = range(6)


def hold(eng, sem, value):
    if isinstance(value, int) and value <= 0:
        return
    eng.wait_ge(sem, value)


def signals(nc, ctx, prefix, names):
    return {n: ctx.enter_context(nc.semaphore(f"{prefix}_{n}")) for n in names.split()}


def three_passes(nc, out, w_hi, w_lo, x_hi, x_lo, first, last):
    nc.tensor.matmul(out, w_hi, x_hi, start=first, stop=False)
    nc.tensor.matmul(out, w_hi, x_lo, start=False, stop=False)
    return nc.tensor.matmul(out, w_lo, x_hi, start=False, stop=last)


def norm_parts(nc, ctx, name, sets):
    n = {"s": signals(nc, ctx, name, "x stats mv var_eps rstd xn")}
    for part, shape in (("x", [P, NC, DM]), ("stats", [P, sets, NC, 6]), ("mv", [P, sets, NC, 2]),
                        ("var_eps", [P, sets, NC]), ("rstd", [P, sets, NC])):
        n[part] = ctx.enter_context(nc.sbuf_tensor(f"{name}_norm_{part}", shape, F32))
    return n


def prepare(nc, t, jobs, name, norm, x_first, first=None):
    NS, NB = 4, 4
    is_mod = [len(job) == 2 for job in jobs]
    scales = [not m and job[1] is not None for m, job in zip(is_mod, jobs)]
    before = lambda flags, n: sum(flags[:n])
    banks_before = lambda n: 4 * (n - before(is_mod, n))
    with ExitStack() as ctx:
        stage = [ctx.enter_context(nc.sbuf_tensor(f"{name}_stage{n}", [P, 4, 512], F32)) for n in range(NS)]
        scaled = ctx.enter_context(nc.sbuf_tensor(f"{name}_scaled", [P, 4, 512], F32))
        sign = ctx.enter_context(nc.sbuf_tensor(f"{name}_sign", [P, 4, KD], F32))
        sums = ctx.enter_context(nc.sbuf_tensor(f"{name}_sums", [P, 2, 512], F32))
        bank = [ctx.enter_context(nc.psum_tensor(f"{name}_ps{n}", [P, 512], F32)) for n in range(NB)]
        mod_ps = [ctx.enter_context(nc.psum_tensor(f"{name}_mod{n}", [P, 512], F32)) for n in range(2)]
        s = signals(nc, ctx, name, "turned hi lo scaled read sum mod_out gate step "
                    "small filled masks exp one silu wd wd_hi mu")
        loaded = [ctx.enter_context(nc.semaphore(f"{name}_loaded{n}")) for n in range(NS)]
        if first:
            NV = 2 * KD + NP
            wd_rows = ctx.enter_context(nc.sbuf_tensor("wd_rows", [H, DM], F32))
            vec_rows = ctx.enter_context(nc.sbuf_tensor("vec_rows", [NV, P], F32))
            c_col = ctx.enter_context(nc.sbuf_tensor("c_col", [P, KD], F32))
            silu = ctx.enter_context(nc.sbuf_tensor("silu", [P, 3, KD], F32))
            wd_ps = ctx.enter_context(nc.psum_tensor("wd_ps", [P, 512], F32))
        block = ctx.enter_context(nc.Block())

        @block.sync
        def _(sp):
            for n, job in enumerate(jobs):
                if n >= NS:
                    m = n - NS
                    if scales[m]:
                        sp.wait_ge(s["scaled"], before(scales, m + 1))
                    else:
                        sp.wait_ge(s["read"], m + 1)
                sp.dma_start(stage[n % NS][:, :, :], job[0]).then_inc(loaded[n % NS], 16)
                if n == 1:
                    sp.dma_start(norm["x"][:, :, :], x_first).then_inc(norm["s"]["x"], 16)
                if n == 0 and first:
                    sp.dma_start(c_col[:, :], first["c"].rearrange("a (p t) -> (a p) t", t=KD)).then_inc(s["small"], 16)
                    sp.dma_start(wd_rows[:, :], first["wd"]).then_inc(s["small"], 16)
                    for vec, r0, rows in (("mu_r", 0, KD), ("mu_k", KD, KD), ("norm_w", 2 * KD, NP)):
                        sp.dma_start(vec_rows[r0:r0 + rows, :],
                                     first[vec].rearrange("(t p) -> t p", p=P)).then_inc(s["small"], 16)
                    sp.dma_start(t["bd"][:, :], first["bd"].rearrange("(h a) -> h a", a=1)).then_inc(s["small"], 16)

        @block.tensor
        def _(pe):
            if first:
                pe.wait_ge(s["masks"], 1)
            for n, job in enumerate(jobs):
                if is_mod[n]:
                    m = before(is_mod, n)
                    pe.wait_ge(s["sum"], KD * (m + 1))
                    hold(pe, s["mod_out"], m - 1)
                    for b in range(KD):
                        last = nc.tensor.matmul(mod_ps[m % 2][:, b:b + 1], sums[:, m % 2, b * P:(b + 1) * P],
                                                t["ones"][:, 0:1], start=True, stop=True)
                    last.then_inc(s["read"], 1)
                    continue
                if scales[n]:
                    pe.wait_ge(s["scaled"], before(scales, n + 1))
                else:
                    pe.wait_ge(loaded[n % NS], 16 * (n // NS + 1))
                src = scaled if scales[n] else stage[n % NS]
                for k in range(4):
                    m = banks_before(n) + k
                    hold(pe, s["lo"], m - NB + 1)
                    for r in range(4):
                        last = nc.tensor.transpose(bank[m % NB][:, r * P:(r + 1) * P], src[:, r, k * P:(k + 1) * P],
                                                   t["ident"][:, :])
                    if k < 3:
                        last.then_inc(s["turned"], 1)
                last.then_inc(s["read"], 1)
                if n == 1 and first:
                    pe.wait_ge(s["small"], 16 * 6)
                    for k in range(KD):
                        nc.tensor.transpose(wd_ps[:, k * H:(k + 1) * H], wd_rows[:, k * P:(k + 1) * P],
                                            t["ident"][0:H, 0:H])
                    nc.tensor.transpose(wd_ps[:, KD * H:KD * H + NV], vec_rows[:, :],
                                        t["ident"][0:NV, 0:NV]).then_inc(s["wd"], 1)

        def bank_ready(eng, n, k):
            if k < 3:
                eng.wait_ge(s["turned"], 3 * (n - before(is_mod, n)) + k + 1)
            else:
                eng.wait_ge(s["read"], n + 1)

        @block.gpsimd
        def _(pool):
            if first:
                pool.wait_ge(s["filled"], 1)
                one = t["ones"][:, :]
                nc.gpsimd.affine_select(out=t["ident"][:, :], in_=one, compare_op=ALU.is_equal, fill=0.0, base=0,
                                        pattern=[[-1, P]], channel_multiplier=1)
                nc.gpsimd.affine_select(out=t["upto"][:, :], in_=one, compare_op=ALU.is_ge, fill=0.0, base=0,
                                        pattern=[[1, P]], channel_multiplier=-1)
                nc.gpsimd.affine_select(out=t["after"][:, :], in_=one, compare_op=ALU.is_gt, fill=0.0, base=0,
                                        pattern=[[-1, P]], channel_multiplier=1).then_inc(s["masks"], 1)
            pool.wait_ge(norm["s"]["var_eps"], 1)
            nc.gpsimd.tensor_tensor(norm["rstd"][:, 0, :], norm["var_eps"][:, 0, :], t["minus_half"][:, 0:NC],
                                    ALU.pow).then_inc(norm["s"]["rstd"], 1)
            for n, job in enumerate(jobs):
                if scales[n]:
                    if before(scales, n) == 0:
                        pool.wait_ge(s["gate"], sum(1 for m, q in zip(is_mod, jobs) if m and q[1] in (GA, GB)))
                    pool.wait_ge(loaded[n % NS], 16 * (n // NS + 1))
                    earlier = [m for m in range(n) if scales[m]]
                    if earlier:
                        pool.wait_ge(s["read"], earlier[-1] + 1)
                    for r in range(4):
                        last = nc.gpsimd.tensor_scalar(scaled[:, r, :], stage[n % NS][:, r, :], job[1][:, r:r + 1],
                                                       1.0, ALU.mult, ALU.mult)
                    last.then_inc(s["scaled"], 1)

        @block.scalar
        def _(act):
            if first:
                nc.scalar.preload_act_table_set("natural_log_exp_and_others")
                act.wait_ge(s["small"], 16 * 6)
                nc.scalar.activation(silu[:, 0, :], c_col[:, :], ACT.Exp, scale=-1.0).then_inc(s["exp"], 1)
            for n, job in enumerate(jobs):
                if is_mod[n]:
                    continue
                for k, (hi, _, col_scale) in enumerate(job[2]):
                    m = banks_before(n) + k
                    bank_ready(act, n, k)
                    if col_scale is None:
                        nc.scalar.copy(hi, bank[m % NB][:, :]).then_inc(s["hi"], 1)
                    else:
                        nc.scalar.activation(hi, bank[m % NB][:, :], ACT.Copy, scale=col_scale).then_inc(s["hi"], 1)

        @block.vector
        def _(dve):
            if first:
                nc.vector.memset(t["ones"][:, :], 1.0).then_inc(s["filled"], 1)
                nc.vector.memset(t["minus_half"][:, :], -0.5)
                nc.vector.memset(t["zeros"][:, :], 0.0)
                dve.wait_ge(s["exp"], 1)
                nc.vector.tensor_scalar(silu[:, 1, :], silu[:, 0, :], 1.0, None, ALU.add).then_inc(s["one"], 1)
                dve.wait_ge(s["one"], 1)
                nc.vector.reciprocal(silu[:, 2, :], silu[:, 1, :]).then_inc(s["one"], 1)
                dve.wait_ge(s["one"], 2)
                nc.vector.tensor_tensor(t["silu_c"][:, :], c_col[:, :], silu[:, 2, :], ALU.mult).then_inc(s["silu"], 1)
                dve.wait_ge(s["masks"], 1)
                nc.vector.tensor_copy(t["after_r"][:, :], t["after"][:, :])

            def finish_mod(n):
                v, m = jobs[n][1], before(is_mod, n)
                gates = sum(1 for mod, job in zip(is_mod[:n], jobs) if mod and job[1] in (GA, GB))
                dve.wait_ge(s["read"], n + 1)
                nc.vector.tensor_copy(t["mod"][:, v, :], mod_ps[m % 2][:, 0:KD]).then_inc(s["mod_out"], 1)
                dve.wait_ge(s["mod_out"], m + 1)
                g = t["mod"][:, v, :]
                if v in (CA, CB):
                    nc.vector.tensor_scalar(t["ca1" if v == CA else "cb1"][:, :], g, 1.0, None, ALU.add)
                if v in (GA, GB):
                    nc.vector.tensor_scalar(sign[:, 0, :], g, 0.0, 2.0, ALU.is_ge, ALU.mult)
                    nc.vector.scalar_tensor_tensor(out=sign[:, 1, :], in0=g, scalar=-1.0, in1=g, op0=ALU.mult,
                                                   op1=ALU.max).then_inc(s["step"], 1)
                    dve.wait_ge(s["step"], 2 * gates + 1)
                    nc.vector.tensor_scalar(sign[:, 2, :], sign[:, 1, :], 0.25, None, ALU.max)
                    nc.vector.tensor_scalar(sign[:, 3, :], sign[:, 0, :], -1.0, None, ALU.add).then_inc(s["step"], 1)
                    dve.wait_ge(s["step"], 2 * gates + 2)
                    nc.vector.tensor_tensor(t["ga" if v == GA else "gb"][:, :], sign[:, 2, :], sign[:, 3, :],
                                            ALU.mult).then_inc(s["gate"], 1)
                    dve.wait_ge(s["gate"], gates + 1)

            unfinished = None
            for n, job in enumerate(jobs):
                if n == 2:
                    dve.wait_ge(norm["s"]["x"], 16)
                    for c in range(NC):
                        last = nc.vector.bn_stats(norm["stats"][:, 0, c, :], norm["x"][:, c, :])
                    last.then_inc(norm["s"]["stats"], 1)
                    dve.wait_ge(norm["s"]["stats"], 1)
                    for c in range(NC):
                        last = nc.vector.bn_aggr(norm["mv"][:, 0, c, :], norm["stats"][:, 0, c, :])
                    last.then_inc(norm["s"]["mv"], 1)
                    dve.wait_ge(norm["s"]["mv"], 1)
                    nc.vector.tensor_scalar(norm["var_eps"][:, 0, :], norm["mv"][:, 0, :, 1], LN_EPS, None,
                                            ALU.add).then_inc(norm["s"]["var_eps"], 1)
                if n == 4:
                    dve.wait_ge(norm["s"]["rstd"], 1)
                    for c in range(NC):
                        nc.vector.tensor_scalar(norm["x"][:, c, :], norm["x"][:, c, :], norm["mv"][:, 0, c, 0:1],
                                                norm["rstd"][:, 0, c:c + 1], ALU.subtract,
                                                ALU.mult).then_inc(norm["s"]["xn"], 1)
                if is_mod[n]:
                    m = before(is_mod, n)
                    dve.wait_ge(loaded[n % NS], 16 * (n // NS + 1))
                    for k in range(KD):
                        rows, weight = stage[n % NS][:, k, :], t["silu_c"][:, k:k + 1]
                        if k == 0:
                            if first:
                                dve.wait_ge(s["silu"], 1)
                            nc.vector.tensor_scalar(sums[:, m % 2, :], rows, weight, None, ALU.mult).then_inc(s["sum"], 1)
                        else:
                            dve.wait_ge(s["sum"], KD * m + k)
                            nc.vector.scalar_tensor_tensor(out=sums[:, m % 2, :], in0=rows, scalar=weight, in1=sums[:, m % 2, :],
                                                           op0=ALU.mult, op1=ALU.add).then_inc(s["sum"], 1)
                    if unfinished is not None:
                        finish_mod(unfinished)
                    unfinished = n
                    continue
                if unfinished is not None:
                    finish_mod(unfinished)
                    unfinished = None
                for k, (hi, lo, col_scale) in enumerate(job[2]):
                    m = banks_before(n) + k
                    dve.wait_ge(s["hi"], m + 1)
                    if col_scale is None:
                        nc.vector.tensor_tensor(lo, bank[m % NB][:, :], hi.bitcast(F32),
                                                ALU.subtract).then_inc(s["lo"], 1)
                    else:
                        nc.vector.scalar_tensor_tensor(out=lo, in0=bank[m % NB][:, :], scalar=col_scale,
                                                       in1=hi.bitcast(F32), op0=ALU.mult,
                                                       op1=ALU.subtract).then_inc(s["lo"], 1)
                if n == 1 and first:
                    dve.wait_ge(s["wd"], 1)
                    wd_t = wd_ps[:, 0:KD * H].rearrange("p (k h) -> p k h", k=KD)
                    nc.vector.tensor_copy(t["wd_hi"][:, :, :], wd_t).then_inc(s["wd_hi"], 1)
                    dve.wait_ge(s["wd_hi"], 1)
                    nc.vector.tensor_tensor(t["wd_lo"][:, :, :], wd_t, t["wd_hi"][:, :, :].bitcast(F32), ALU.subtract)
                    vecs = wd_ps[:, KD * H:KD * H + NV]
                    nc.vector.tensor_copy(t["mu"][:, :, :],
                                          vecs[:, 0:2 * KD].rearrange("p (m k) -> p m k", m=2)).then_inc(s["mu"], 1)
                    nc.vector.tensor_copy(t["norm_w"][:, :], vecs[:, 2 * KD:])
                    dve.wait_ge(s["mu"], 1)
                    nc.vector.tensor_scalar(t["one_minus_mu"][:, :, :], t["mu"][:, :, :], -1.0, 1.0, ALU.mult, ALU.add)


KINDS = "gqk"
USES = [(kind, b) for b in range(4) for kind in KINDS] + [("v", 0), ("v", 1)]
USES += [(kind, b) for b in range(4, NP) for kind in KINDS] + [("v", 2), ("v", 3)]
BY_ACT = [u for u in USES if u[0] != "k"]
NU, NA = len(USES), len(BY_ACT)


def attention_pass(nc, t, W, norm, x_v, o_v):
    with ExitStack() as ctx:
        def sb(name, shape, dt=F32):
            return ctx.enter_context(nc.sbuf_tensor(name, shape, dt))

        def ps(name, shape):
            return ctx.enter_context(nc.psum_tensor(name, shape, F32))

        x = norm["x"]
        hT = sb("hT", [P, KD, T])
        h_hi = sb("h_hi", [P, KD, T], F32R)
        h_lo = sb("h_lo", [P, KD, T], F32R)
        q = sb("q", [P, NP, T])
        kg = sb("kg", [P, NP, T])
        k_hi = sb("k_hi", [P, T], F32R)
        k_lo = sb("k_lo", [P, T], F32R)
        q_hi = sb("q_hi", [P, NC, 2, CH], F32R)
        q_lo = sb("q_lo", [P, NC, 2, CH], F32R)
        v = sb("v", [P, NC, HID])
        o = sb("o", [P, 2, NC, P])
        decay = sb("decay", [P, 4, CH])
        prob = sb("prob", [P, 4, CH])
        r_hi = sb("r_hi", [P, NC, 2, CH], F32R)
        r_lo = sb("r_lo", [P, NC, 2, CH], F32R)
        state = sb("state", [P, NP, P])
        mid = sb("mid", [P, P])
        kw = sb("kw", [P, NC, P])
        inter = sb("inter", [P, NC, P])
        gate = sb("gate", [P, 3, T])
        stats, mv, var_eps, rstd = (norm[part][:, 0] for part in ("stats", "mv", "var_eps", "rstd"))
        zt = sb("zt", [H, 5, T])
        g_raw = sb("g_raw", [P, NC * H])
        g_hi = sb("g_hi", [P, NC * H], F32R)
        g_lo = sb("g_lo", [P, NC * H], F32R)
        w_new = sb("w_new", [P, 3, NC * H])
        w_cur = sb("w_cur", [P, 3, NC, H])

        tick = sb("tick", [P, 2])

        psA = ps("psA", [P, 4, CH])
        psS = ps("psS", [P, 4, CH])
        psK = ps("psK", [P, 4, P])
        psO = ps("psO", [P, 4, P])
        psJ = [ps(f"psJ{n}", [P, 512]) for n in range(2)]
        psT = ps("psT", [P, KD, T])
        psZ = psT[0:H, 0, :]
        psG = psT[:, 1, 0:NC * H]
        psC = psT[:, 1, NC * H:4 * NC * H]

        s = signals(nc, ctx, "a", "xT hT h_hi h_lo z zb softin e1 l soft gT g_turned g_raw cum w_new g_hi g cur "
                 "proj by_act k gate1 gate2 r a e mask kq_hi k_lo q_lo score prob kT kw inc mid state pv gla inter o zero")
        s.update(norm["s"])
        store = [ctx.enter_context(nc.semaphore(f"a_store{n}")) for n in range(2)]
        block = ctx.enter_context(nc.Block())

        def evacuated(eng, i, u):
            if u < 0:
                i, u = i - 1, u + NU
                if isinstance(i, int) and i < 0:
                    return
            kind, b = USES[u]
            if kind == "k":
                hold(eng, s["k"], NP * i + b + 1)
            else:
                hold(eng, s["by_act"], NA * i + BY_ACT.index(USES[u]) + 1)

        def proj_done(i, use):
            return NU * i + USES.index(use) + 1

        def act_done(i, use):
            return NA * i + BY_ACT.index(use) + 1

        def sp_tile(sp, i, gla, proj, prep):
            j = i - 1
            if prep:
                hold(sp, s["xT"], KD * (i + 1))
                sp.dma_start(x[:, :, :], x_v[i + 1]).then_inc(s["x"], 16)
            if gla:
                for p in range(NP):
                    sp.wait_ge(s["o"], NP * j + p + 1)
                    sp.dma_start(o_v[j, :, :, p * P:(p + 1) * P], o[:, p % 2, :, :]).then_inc(store[p % 2], 16)

        @block.sync
        def _(sp):
            sp_tile(sp, 0, False, True, True)
            sp_tile(sp, 1, True, True, True)
            with sp.Fori(2, NT - 1) as i:
                sp_tile(sp, i, True, True, True)
            sp_tile(sp, NT - 1, True, True, False)
            sp_tile(sp, NT, True, False, False)
            for n in range(2):
                sp.wait_ge(store[n], 16 * NP // 2 * NT)

        def project(i, kind, b, pe):
            u = USES.index((kind, b))
            bank = psJ[u % 2]
            evacuated(pe, i, u - 2)
            for k in range(KD):
                if u == 0:
                    pe.wait_ge(s["h_lo"], KD * i + k + 1)
                if kind == "v":
                    c, half = b % 2, b // 2
                    hh, hl = (a[:, k, c * CH:(c + 1) * CH] for a in (h_hi, h_lo))
                    wh, wl = (a[:, k, half * 512:(half + 1) * 512] for a in W["v"])
                    last = three_passes(nc, bank[:, :], hh, hl, wh, wl, k == 0, k == KD - 1)
                else:
                    wh, wl = (a[:, k, b * P:(b + 1) * P] for a in W[kind])
                    last = three_passes(nc, bank[:, 0:T], wh, wl, h_hi[:, k, :], h_lo[:, k, :], k == 0, k == KD - 1)
            last.then_inc(s["proj"], 1)

        def turn_x(pe, n):
            pe.wait_ge(s["xn"], NC * (n + 1))
            hold(pe, s["hT"], KD * n)
            hold(pe, s["w_new"], n)
            for k in range(KD):
                for c in range(NC):
                    last = nc.tensor.transpose(psT[:, k, c * CH:(c + 1) * CH], x[:, c, k * P:(k + 1) * P],
                                               t["ident"][:, :])
                last.then_inc(s["xT"], 1)

        def pe_tile(pe, i, gla, proj, prep):
            j = i - 1
            for p in range(NP):
                n = NP * j + p
                if gla:
                    pe.wait_ge(s["r"], n + 1)
                    hold(pe, s["e"], n)
                    nc.tensor.matmul(psA[:, :, :], t["after_r"][:, :], r_hi[:, :, :, :], start=True, stop=False)
                    nc.tensor.matmul(psA[:, :, :], t["after_r"][:, :], r_lo[:, :, :, :], start=False,
                                     stop=True).then_inc(s["a"], 1)
                    pe.wait_ge(s["k_lo"], n + 1)
                    pe.wait_ge(s["q_lo"], n + 1)
                    hold(pe, s["prob"], n)
                    for c in range(NC):
                        cols = slice(c * CH, (c + 1) * CH)
                        last = three_passes(nc, psS[:, 2 * c:2 * c + 2, :], k_hi[:, cols], k_lo[:, cols],
                                            q_hi[:, c, :, :], q_lo[:, c, :, :], True, True)
                    last.then_inc(s["score"], 1)
                    hold(pe, s["mid"], n)
                    hold(pe, s["state"], n)
                    for c in range(NC):
                        last = nc.tensor.transpose(psK[:, c, :], kg[:, p, c * CH:(c + 1) * CH], t["ident"][:, :])
                    last.then_inc(s["kT"], 1)
                if p == 0 and gla:
                    project(j, "v", 2, pe)
                if p > 0 and proj:
                    project(i, "g", p - 1, pe)
                if gla:
                    pe.wait_ge(s["kw"], n + 1)
                    pe.wait_ge(s["by_act"], act_done(j, ("v", 1 + 2 * (p // 4))) if p else act_done(j, ("v", 1)))
                    for c in range(NC):
                        last = nc.tensor.matmul(psK[:, 2 + c, :], kw[:, c, :], v[:, c, p * P:(p + 1) * P],
                                                start=True, stop=True)
                    last.then_inc(s["inc"], 1)
                    pe.wait_ge(s["prob"], n + 1)
                    hold(pe, s["o"], n)
                    for c in range(NC):
                        for h in range(2):
                            nc.tensor.matmul(psO[:, c, h * DH:(h + 1) * DH], prob[:, 2 * c + h, :],
                                             v[:, c, p * P + h * DH:p * P + (h + 1) * DH], start=True, stop=True)
                    nc.tensor.matmul(psO[:, 2, :], q[:, p, 0:CH], state[:, p, :], start=True,
                                     stop=True).then_inc(s["pv"], 1)
                if p == 0 and gla:
                    project(j, "v", 3, pe)
                if p > 0 and proj:
                    project(i, "q", p - 1, pe)
                    if p == 4:
                        pe.wait_ge(s["gT"], i + 1)
                    project(i, "k", p - 1, pe)
                if gla:
                    pe.wait_ge(s["mid"], n + 1)
                    nc.tensor.matmul(psO[:, 3, :], q[:, p, CH:T], mid[:, :], start=True, stop=True).then_inc(s["gla"], 1)
                if p == 1 and proj:
                    for k in range(KD):
                        last = three_passes(nc, psZ, t["wd_hi"][:, k, :], t["wd_lo"][:, k, :], h_hi[:, k, :],
                                            h_lo[:, k, :], k == 0, k == KD - 1)
                    last.then_inc(s["z"], 1)
                if p == 4 and proj:
                    for c in range(NC):
                        last = nc.tensor.transpose(psG[:, c * H:(c + 1) * H], zt[:, 4, c * CH:(c + 1) * CH],
                                                   t["ident"][0:H, 0:H])
                    last.then_inc(s["g_turned"], 1)
                if p == 5 and proj:
                    pe.wait_ge(s["g_raw"], i + 1)
                    for n3, m in enumerate(("upto", "after", "ones")):
                        last = nc.tensor.matmul(psC[:, n3 * NC * H:(n3 + 1) * NC * H], t[m][:, :], g_raw[:, :],
                                                start=True, stop=True)
                    last.then_inc(s["cum"], 1)
                if p == 4 and proj:
                    project(i, "v", 0, pe)
                    project(i, "v", 1, pe)
                if p == 6 and prep:
                    turn_x(pe, i + 1)
            if proj:
                for kind in KINDS:
                    project(i, kind, NP - 1, pe)

        @block.tensor
        def _(pe):
            turn_x(pe, 0)
            pe_tile(pe, 0, False, True, True)
            pe_tile(pe, 1, True, True, True)
            with pe.Fori(2, NT - 1) as i:
                pe_tile(pe, i, True, True, True)
            pe_tile(pe, NT - 1, True, True, False)
            pe_tile(pe, NT, True, False, False)

        def affine_h(act, n):
            hold(act, s["h_lo"], KD * n)
            for k in range(KD):
                act.wait_ge(s["xT"], KD * n + 2 * (k // 2) + 2)
                nc.scalar.activation(hT[:, k, :], psT[:, k, :], ACT.Identity, bias=t["mod"][:, SA, k:k + 1],
                                     scale=t["ca1"][:, k:k + 1]).then_inc(s["hT"], 1)

        def round_h(act, i):
            act.wait_ge(s["hT"], KD * (i + 1))
            hold(act, s["proj"], NU * i)
            for k in range(KD):
                nc.scalar.copy(h_hi[:, k, :], hT[:, k, :]).then_inc(s["h_hi"], 1)

        def copy_v(act, i, b):
            c, half = b % 2, b // 2
            act.wait_ge(s["proj"], proj_done(i, ("v", b)))
            hold(act, s["gla"], NP * (i - 1) + 4 * (half + 1))
            nc.scalar.copy(v[:, c, half * 512:(half + 1) * 512],
                           psJ[USES.index(("v", b)) % 2][:, :]).then_inc(s["by_act"], 1)

        def copy_qg(act, i, b):
            act.wait_ge(s["proj"], proj_done(i, ("g", b)))
            hold(act, s["gate2"], NP * i + b)
            nc.scalar.activation(gate[:, 0, :], psJ[USES.index(("g", b)) % 2][:, 0:T], ACT.Exp,
                                 scale=-1.0).then_inc(s["by_act"], 1)
            act.wait_ge(s["proj"], proj_done(i, ("q", b)))
            hold(act, s["gla"], NP * (i - 1) + b + 1)
            nc.scalar.copy(q[:, b, :], psJ[USES.index(("q", b)) % 2][:, 0:T]).then_inc(s["by_act"], 1)

        def round_pair(act, i, p):
            n = NP * i + p
            hold(act, s["k"], n + 1)
            act.wait_ge(s["by_act"], act_done(i, ("q", p)))
            hold(act, s["score"], n)
            nc.scalar.copy(k_hi[:, :], kg[:, p, :])
            for h in range(2):
                r = slice(h * DH, (h + 1) * DH)
                last = nc.scalar.copy(q_hi[r, :, h, :], q[r, p, :].rearrange("p (c t) -> p c t", c=NC))
            last.then_inc(s["kq_hi"], 1)

        def act_tile(act, i, gla, proj, prep):
            j = i - 1
            for p in range(NP):
                n = NP * j + p
                if gla:
                    act.wait_ge(s["a"], n + 1)
                    hold(act, s["prob"], n)
                    nc.scalar.activation(decay[:, :, :], psA[:, :, :], ACT.Exp).then_inc(s["e"], 1)
                    if p == 1:
                        copy_v(act, j, 3)
                    if p + 1 < NP:
                        round_pair(act, j, p + 1)
                    elif proj:
                        round_pair(act, i, 0)
                if p == 0 and gla:
                    copy_v(act, j, 2)
                if p == 0 and proj:
                    round_h(act, i)
                if p == 3 and proj:
                    act.wait_ge(s["softin"], i + 1)
                    nc.scalar.activation(zt[:, 2, :], zt[:, 1, :], ACT.Exp).then_inc(s["e1"], 1)
                    act.wait_ge(s["e1"], i + 1)
                    nc.scalar.activation(zt[:, 3, :], zt[:, 2, :], ACT.Ln, bias=1.0).then_inc(s["l"], 1)
                if p > 0 and proj:
                    copy_qg(act, i, p - 1)
                if p == 4 and proj:
                    copy_v(act, i, 0)
                    copy_v(act, i, 1)
                if p == 6 and proj:
                    act.wait_ge(s["cum"], i + 1)
                    hold(act, s["cur"], i)
                    nc.scalar.activation(w_new[:, :, :], psC.rearrange("p (a b) -> p a b", a=3),
                                         ACT.Exp).then_inc(s["w_new"], 1)
                if p == 7 and prep:
                    affine_h(act, i + 1)
            if proj:
                copy_qg(act, i, NP - 1)
                if not gla:
                    round_pair(act, i, 0)

        @block.scalar
        def _(act):
            affine_h(act, 0)
            act.wait_ge(s["zero"], 1)
            act_tile(act, 0, False, True, True)
            act_tile(act, 1, True, True, True)
            with act.Fori(2, NT - 1) as i:
                act_tile(act, i, True, True, True)
            act_tile(act, NT - 1, True, True, False)
            act_tile(act, NT, True, False, False)

        def norm_stats(dve, n):
            dve.wait_ge(s["x"], 16 * (n + 1))
            for c in range(NC):
                last = nc.vector.bn_stats(stats[:, c, :], x[:, c, :])
            last.then_inc(s["stats"], 1)
            dve.wait_ge(s["stats"], n + 1)
            nc.vector.memset(tick[:, 0:1], 0.0)
            for c in range(NC):
                last = nc.vector.bn_aggr(mv[:, c, :], stats[:, c, :])
            last.then_inc(s["mv"], 1)
            dve.wait_ge(s["mv"], n + 1)
            nc.vector.tensor_scalar(var_eps[:, :], mv[:, :, 1], LN_EPS, None, ALU.add).then_inc(s["var_eps"], 1)

        def norm_x(dve, n):
            dve.wait_ge(s["rstd"], n + 1)
            for c in range(NC):
                nc.vector.tensor_scalar(x[:, c, :], x[:, c, :], mv[:, c, 0:1], rstd[:, c:c + 1], ALU.subtract,
                                        ALU.mult).then_inc(s["xn"], 1)

        def rest_h(dve, i, k):
            dve.wait_ge(s["h_hi"], KD * i + k + 1)
            nc.vector.tensor_tensor(h_lo[:, k, :], hT[:, k, :], h_hi[:, k, :].bitcast(F32),
                                    ALU.subtract).then_inc(s["h_lo"], 1)

        def gate_start(dve, i, b):
            dve.wait_ge(s["by_act"], act_done(i, ("g", b)))
            nc.vector.tensor_scalar(gate[:, 1, :], gate[:, 0, :], 1.0, None, ALU.add).then_inc(s["gate1"], 1)
            dve.wait_ge(s["gate1"], NP * i + b + 1)
            nc.vector.reciprocal(gate[:, 2, :], gate[:, 1, :]).then_inc(s["gate2"], 1)

        def gate_end(dve, i, b):
            dve.wait_ge(s["gate2"], NP * i + b + 1)
            dve.wait_ge(s["proj"], proj_done(i, ("k", b)))
            hold(dve, s["gla"], NP * (i - 1) + b + 1)
            nc.vector.tensor_tensor(kg[:, b, :], psJ[USES.index(("k", b)) % 2][:, 0:T], gate[:, 2, :],
                                    ALU.mult).then_inc(s["k"], 1)

        def rest_q(dve, i, p):
            dve.wait_ge(s["kq_hi"], NP * i + p + 1)
            for h in range(2):
                r = slice(h * DH, (h + 1) * DH)
                last = nc.vector.tensor_tensor(q_lo[r, :, h, :], q[r, p, :].rearrange("p (c t) -> p c t", c=NC),
                                               q_hi[r, :, h, :].bitcast(F32), ALU.subtract)
            last.then_inc(s["q_lo"], 1)

        def dve_tile(dve, i, gla, proj, prep):
            j = i - 1
            for p in range(NP):
                n = NP * j + p
                if gla:
                    if p == 0:
                        dve.wait_ge(s["cur"], i)
                    dve.wait_ge(s["kT"], n + 1)
                    hold(dve, s["inc"], n)
                    nc.vector.tensor_tensor(
                        kw[:, :, :].rearrange("p c (h d) -> p c h d", h=2),
                        psK[:, 0:2, :].rearrange("p c (h d) -> p c h d", h=2),
                        w_cur[:, 1, :, 2 * p:2 * p + 2].unsqueeze(3).to_broadcast([P, NC, 2, DH]),
                        ALU.mult).then_inc(s["kw"], 1)
                    dve.wait_ge(s["mask"], n + 1)
                    dve.wait_ge(s["score"], n + 1)
                    hold(dve, s["pv"], n)
                    nc.vector.tensor_tensor(prob[:, :, :], decay[:, :, :], psS[:, :, :], ALU.mult).then_inc(s["prob"], 1)
                    dve.wait_ge(s["inc"], n + 1)
                    hold(dve, s["gla"], n)
                    for h in range(2):
                        r = slice(h * DH, (h + 1) * DH)
                        last = nc.vector.scalar_tensor_tensor(
                            out=mid[r, r], in0=state[r, p, r], scalar=w_cur[r, 2, 0, 2 * p + h:2 * p + h + 1],
                            in1=psK[r, 2, r], op0=ALU.mult, op1=ALU.add)
                    last.then_inc(s["mid"], 1)
                    if p + 1 < NP:
                        rest_q(dve, j, p + 1)
                    elif proj:
                        rest_q(dve, i, 0)
                if p > 0 and proj:
                    gate_start(dve, i, p - 1)
                if gla:
                    dve.wait_ge(s["mid"], n + 1)
                    dve.wait_ge(s["pv"], n + 1)
                    for h in range(2):
                        r = slice(h * DH, (h + 1) * DH)
                        last = nc.vector.scalar_tensor_tensor(
                            out=state[r, p, r], in0=mid[r, r], scalar=w_cur[r, 2, 1, 2 * p + h:2 * p + h + 1],
                            in1=psK[r, 3, r], op0=ALU.mult, op1=ALU.add)
                    last.then_inc(s["state"], 1)
                if p == 0 and proj:
                    for k in range(2 if gla else KD):
                        rest_h(dve, i, k)
                if p == 2 and proj:
                    dve.wait_ge(s["z"], i + 1)
                    nc.vector.tensor_scalar(zt[:, 0, :], psZ, t["bd"][:, 0:1], None, ALU.add).then_inc(s["zb"], 1)
                    dve.wait_ge(s["zb"], i + 1)
                    nc.vector.scalar_tensor_tensor(out=zt[:, 1, :], in0=zt[:, 0, :], scalar=-1.0, in1=zt[:, 0, :],
                                                   op0=ALU.mult, op1=ALU.min).then_inc(s["softin"], 1)
                if p == 3 and proj:
                    dve.wait_ge(s["l"], i + 1)
                    nc.vector.scalar_tensor_tensor(out=zt[:, 1, :], in0=zt[:, 0, :], scalar=0.0, in1=zt[:, 3, :],
                                                   op0=ALU.max, op1=ALU.add).then_inc(s["soft"], 1)
                    dve.wait_ge(s["soft"], i + 1)
                    nc.vector.tensor_scalar(zt[:, 4, :], zt[:, 1, :], -1.0, None, ALU.mult).then_inc(s["gT"], 1)
                if p == 5 and proj:
                    dve.wait_ge(s["g_turned"], i + 1)
                    nc.vector.tensor_copy(g_raw[:, :], psG).then_inc(s["g_raw"], 1)
                if p == 7 and proj:
                    hold(dve, s["r"], NP * i if gla else 0)
                    dve.wait_ge(s["g_raw"], i + 1)
                    nc.vector.tensor_copy(g_hi[:, :], g_raw[:, :]).then_inc(s["g_hi"], 1)
                    dve.wait_ge(s["g_hi"], i + 1)
                    nc.vector.tensor_tensor(g_lo[:, :], g_raw[:, :], g_hi[:, :].bitcast(F32),
                                            ALU.subtract).then_inc(s["g"], 1)
                if p == 4 and prep:
                    norm_stats(dve, i + 1)
                if p == 5 and prep:
                    norm_x(dve, i + 1)
                if p > 0 and proj:
                    gate_end(dve, i, p - 1)
                if gla:
                    dve.wait_ge(s["gla"], n + 1)
                    nc.vector.tensor_tensor(
                        inter[:, :, :].rearrange("p c (h d) -> p c h d", h=2),
                        psO[:, 2:4, :].rearrange("p c (h d) -> p c h d", h=2),
                        w_cur[:, 0, :, 2 * p:2 * p + 2].unsqueeze(3).to_broadcast([P, NC, 2, DH]),
                        ALU.mult).then_inc(s["inter"], 1)
                    if p == 0 and proj:
                        rest_h(dve, i, 2)
                    dve.wait_ge(s["inter"], n + 1)
                    hold(dve, store[p % 2], 16 * (NP // 2 * j + p // 2))
                    nc.vector.tensor_tensor(o[:, p % 2, :, :], inter[:, :, :], psO[:, 0:2, :], ALU.add).then_inc(s["o"], 1)
                    if p == 0 and proj:
                        rest_h(dve, i, 3)
            if proj:
                dve.wait_ge(s["w_new"], i + 1)
                nc.vector.tensor_copy(w_cur[:, :, :, :].rearrange("p a c h -> p (a c h)"),
                                      w_new[:, :, :].rearrange("p a b -> p (a b)")).then_inc(s["cur"], 1)
                gate_start(dve, i, NP - 1)
                gate_end(dve, i, NP - 1)
                if not gla:
                    rest_q(dve, i, 0)

        @block.vector
        def _(dve):
            nc.vector.memset(state[:, :, :], 0.0)
            nc.vector.memset(mid[:, :], 0.0)
            nc.vector.memset(q_lo[:, :, :, :].bitcast(F32), 0.0)
            nc.vector.memset(q_hi[:, :, :, :].bitcast(F32), 0.0).then_inc(s["zero"], 1)
            dve.wait_ge(s["zero"], 1)
            dve_tile(dve, 0, False, True, True)
            dve_tile(dve, 1, True, True, True)
            with dve.Fori(2, NT - 1) as i:
                dve_tile(dve, i, True, True, True)
            dve_tile(dve, NT - 1, True, True, False)
            dve_tile(dve, NT, True, False, False)

        def rsqrt(pool, n):
            pool.wait_ge(s["var_eps"], n + 1)
            nc.gpsimd.tensor_tensor(rstd[:, :], var_eps[:, :], t["minus_half"][:, 0:NC], ALU.pow).then_inc(s["rstd"], 1)

        def spread_g(pool, i, p):
            if p == 0:
                pool.wait_ge(s["g"], i + 1)
            hold(pool, s["a"], NP * i + p)
            for dst, g in ((r_hi, g_hi), (r_lo, g_lo)):
                gg = g[:, :].bitcast(F32).rearrange("p (c h) -> p c h", c=NC)[:, :, 2 * p:2 * p + 2]
                last = nc.gpsimd.tensor_tensor(dst[:, :, :, :], gg.unsqueeze(3).to_broadcast([P, NC, 2, CH]),
                                               t["upto"][:, :].unsqueeze(1).unsqueeze(1).to_broadcast([P, NC, 2, CH]),
                                               ALU.mult)
            last.then_inc(s["r"], 1)

        def rest_k(pool, i, p):
            pool.wait_ge(s["kq_hi"], NP * i + p + 1)
            nc.gpsimd.tensor_tensor(k_lo[:, :], kg[:, p, :], k_hi[:, :].bitcast(F32), ALU.subtract).then_inc(s["k_lo"], 1)

        def pool_tile(pool, i, gla, proj, prep):
            j = i - 1
            for p in range(NP):
                if gla:
                    pool.wait_ge(s["e"], NP * j + p + 1)
                    nc.gpsimd.tensor_tensor(tick[:, 1:2], t["zeros"][:, :], t["zeros"][:, :],
                                            ALU.mult)
                    nc.gpsimd.affine_select(out=decay[:, :, :], in_=decay[:, :, :], compare_op=ALU.is_ge, fill=0.0,
                                            base=0, pattern=[[0, 4], [1, CH]], channel_multiplier=-1).then_inc(s["mask"], 1)
                    if p + 1 < NP:
                        spread_g(pool, j, p + 1)
                        rest_k(pool, j, p + 1)
                    elif proj:
                        spread_g(pool, i, 0)
                        rest_k(pool, i, 0)
                if p == 4 and prep:
                    rsqrt(pool, i + 1)
            if proj and not gla:
                spread_g(pool, i, 0)
                rest_k(pool, i, 0)

        @block.gpsimd
        def _(pool):
            pool_tile(pool, 0, False, True, True)
            pool_tile(pool, 1, True, True, True)
            with pool.Fori(2, NT - 1) as i:
                pool_tile(pool, i, True, True, True)
            pool_tile(pool, NT - 1, True, True, False)
            pool_tile(pool, NT, True, False, False)


def output_pass(nc, t, W, norm, x_v, o_v, out_v):
    with ExitStack() as ctx:
        def sb(name, shape, dt=F32):
            return ctx.enter_context(nc.sbuf_tensor(name, shape, dt))

        def ps(name, shape):
            return ctx.enter_context(nc.psum_tensor(name, shape, F32))

        xn = norm["x"]
        hT = sb("hT2", [P, KD, T])
        h_hi = sb("h_hi2", [P, KD, T], F32R)
        h_lo = sb("h_lo2", [P, KD, T], F32R)
        o = sb("o_rows", [P, NC, HID])
        og = sb("og", [P, 2, 512])
        z_hi = sb("z_hi", [P, NP, T], F32R)
        z_lo = sb("z_lo", [P, NP, T], F32R)
        x1 = sb("x1", [P, NC, DM])
        x1_old = sb("x1_old", [P, NC, DM])
        x2n = sb("x2n", [P, NC, DM])
        h2 = sb("h2", [P, KD, T + 1])
        mix = sb("mix", [P, KD, T])
        prev = sb("prev", [P, KD, T])
        ra_hi = sb("ra_hi", [P, KD, T], F32R)
        ra_lo = sb("ra_lo", [P, KD, T], F32R)
        xk_hi = sb("xk_hi", [P, KD, T], F32R)
        xk_lo = sb("xk_lo", [P, KD, T], F32R)
        r = sb("r_gate", [P, NC, DM])
        relu = sb("relu", [P, 2, 2, T])
        ss = sb("ss", [P, NC])
        stats, mv, var_eps, rstd = (norm[part] for part in ("stats", "mv", "var_eps", "rstd"))

        tick = sb("tick2", [P, 1])

        psT = ps("psT2", [P, KD, T])
        psG = [ps(f"psG{n}", [P, 512]) for n in range(2)]
        psR = [ps(f"psR{n}", [P, 512]) for n in range(2)]
        psW = [ps(f"psW{n}", [P, 512]) for n in range(2)]
        psZ = psG + psR
        psK = psW + psG

        s = signals(nc, ctx, "b", "xb ol xT hT h_hi h_lo og sg sq ve3 rstd3 z tz zh zl wo x1 "
                 "st2 mv2 ve2 rstd2 xn2 xT2 h2 prev mixr xr_hi xr prevk mixk xk_hi xk last rr rs kt relu k2 ka_hi ka "
                 "kv fin1 fin keep store zero")
        s.update({"xa": norm["s"]["x"], "st1": norm["s"]["stats"], "mv1": norm["s"]["mv"],
                  "ve1": norm["s"]["var_eps"], "rstd1": norm["s"]["rstd"], "xn": norm["s"]["xn"]})
        block = ctx.enter_context(nc.Block())

        def sp_tile(sp, i, att, ffn, prep):
            j = i - 1
            if prep:
                sp.wait_ge(s["xT"], KD * (i + 1))
                sp.dma_start(xn[:, :, :], x_v[i + 1]).then_inc(s["xa"], 16)
            if att:
                hold(sp, s["keep"], i)
                sp.dma_start(x1[:, :, :], x_v[i]).then_inc(s["xb"], 16)
            if prep:
                sp.wait_ge(s["tz"], 4 * (i + 1))
                sp.dma_start(o[:, :, :], o_v[i + 1]).then_inc(s["ol"], 16)
            if ffn:
                for c in range(NC):
                    sp.wait_ge(s["fin"], NC * j + c + 1)
                    sp.dma_start(out_v[j, :, c, :], r[:, c, :]).then_inc(s["store"], 16)

        @block.sync
        def _(sp):
            sp.dma_start(o[:, :, :], o_v[0]).then_inc(s["ol"], 16)
            sp_tile(sp, 0, True, False, True)
            sp_tile(sp, 1, True, True, True)
            with sp.Fori(2, NT - 1) as i:
                sp_tile(sp, i, True, True, True)
            sp_tile(sp, NT - 1, True, True, False)
            sp_tile(sp, NT, False, True, False)
            sp.wait_ge(s["store"], 16 * NC * NT)

        def turn(pe, src, sem):
            for k in range(KD):
                for c in range(NC):
                    last = nc.tensor.transpose(psT[:, k, c * CH:(c + 1) * CH], src[:, c, k * P:(k + 1) * P],
                                               t["ident"][:, :])
                last.then_inc(sem, 1)

        def rows_product(bank, a_hi, a_lo, w, c, half, blocks, ready=()):
            for k in range(blocks):
                for at, eng, sem, value in ready:
                    if at == k:
                        eng.wait_ge(sem, value)
                ah, al = (a[:, k, c * CH:(c + 1) * CH] for a in (a_hi, a_lo))
                wh, wl = (a[:, k, half * 512:(half + 1) * 512] for a in w)
                last = three_passes(nc, bank[:, :], ah, al, wh, wl, k == 0, k == blocks - 1)
            return last

        def pe_tile(pe, i, att, ffn, prep):
            j = i - 1

            def turn_z(n):
                c, half = n // 2, n % 2
                pe.wait_ge(s["z"], 4 * i + n + 1)
                if n < 2:
                    pe.wait_ge(s["sg"], 4 * i + 3 + n)
                if n == 2:
                    hold(pe, s["fin1"], NC * j)
                for b in range(4):
                    last = nc.tensor.transpose(psZ[n][:, b * CH:(b + 1) * CH],
                                               o[:, c, (4 * half + b) * P:(4 * half + b + 1) * P], t["ident"][:, :])
                last.then_inc(s["tz"], 1)

            if att:
                pe.wait_ge(s["h_lo"], i + 1)
                for n in range(4):
                    if n < 2:
                        hold(pe, s["relu"], KD * (i - 1))
                    else:
                        pe.wait_ge(s["sg"], 4 * i + n - 1)
                    rows_product(psG[n % 2], h_hi, h_lo, W["og"], n // 2, n % 2, KD).then_inc(s["og"], 1)
            if att:
                turn_z(0)
            if ffn:
                pe.wait_ge(s["xn2"], NC * (j + 1))
                hold(pe, s["hT"], KD * (i + 1 if att else i))
                hold(pe, s["h2"], KD * j)
                turn(pe, x2n, s["xT2"])
            if att:
                for n in range(1, 4):
                    turn_z(n)
                hold(pe, s["relu"], KD * j)
                for c in range(NC):
                    ready = [(4 * half, pe, s["zl"], 4 * i + 2 * c + half + 1) for half in range(2)]
                    rows_product(psW[c], z_hi, z_lo, W["o"], c, 0, NP, ready).then_inc(s["wo"], 1)
            if ffn:
                pe.wait_ge(s["xr"], j + 1)
                if att:
                    pe.wait_ge(s["zl"], 4 * (i + 1))
                hold(pe, s["fin1"], NC * j)
                for c in range(NC):
                    rows_product(psR[c], ra_hi, ra_lo, W["r"], c, 0, KD).then_inc(s["rr"], 1)
            if prep:
                pe.wait_ge(s["xn"], NC * (i + 2))
                hold(pe, s["h2"], KD * (j + 1) if ffn else 0)
                turn(pe, xn, s["xT"])
            if ffn:
                pe.wait_ge(s["xk"], j + 1)
                pe.wait_ge(s["x1"], NC * (i + 1) if att else NC * i)
                hold(pe, s["relu"], KD * j)
                for n in range(KD):
                    for k in range(KD):
                        wh, wl = (a[:, k, n * P:(n + 1) * P] for a in W["k2"])
                        last = three_passes(nc, psK[n][:, 0:T], wh, wl, xk_hi[:, k, :], xk_lo[:, k, :], k == 0,
                                            k == KD - 1)
                    last.then_inc(s["kt"], 1)
                pe.wait_ge(s["rs"], NC * (j + 1))
                for c in range(NC):
                    ready = [(k, pe, s["ka"], KD * j + k + 1) for k in range(KD)]
                    rows_product(psR[c], ra_hi, ra_lo, W["v2"], c, 0, KD, ready if c == 0 else ()).then_inc(s["kv"], 1)

        @block.tensor
        def _(pe):
            pe.wait_ge(s["xn"], NC)
            turn(pe, xn, s["xT"])
            pe_tile(pe, 0, True, False, True)
            pe_tile(pe, 1, True, True, True)
            with pe.Fori(2, NT - 1) as i:
                pe_tile(pe, i, True, True, True)
            pe_tile(pe, NT - 1, True, True, False)
            pe_tile(pe, NT, False, True, False)

        def affine_h(act, n, blocks):
            hold(act, s["h_lo"], n)
            for k in blocks:
                act.wait_ge(s["xT"], KD * n + 2 * (k // 2) + 2)
                nc.scalar.activation(hT[:, k, :], psT[:, k, :], ACT.Identity, bias=t["mod"][:, SA, k:k + 1],
                                     scale=t["ca1"][:, k:k + 1]).then_inc(s["hT"], 1)

        def act_tile(act, i, att, ffn, prep):
            j = i - 1

            def copy_z(n):
                c, half = n // 2, n % 2
                act.wait_ge(s["tz"], 4 * i + n + 1)
                nc.scalar.copy(z_hi[:, 4 * half:4 * half + 4, c * CH:(c + 1) * CH],
                               psZ[n][:, :].rearrange("p (b t) -> p b t", b=4)).then_inc(s["zh"], 1)

            if att:
                act.wait_ge(s["ol"], 16 * (i + 1))
                hold(act, s["ve3"], i)
                hold(act, s["z"], 4 * i)
                for c in range(NC):
                    hold(act, s["sq"], NC * i + c)
                    nc.scalar.activation(og[:, :, :], o[:, c, :].rearrange("p (b d) -> p b d", b=2), ACT.Square,
                                         accum_out=ss[:, c:c + 1]).then_inc(s["sq"], 1)
                act.wait_ge(s["sq"], NC * (i + 1))
                for n in range(4):
                    act.wait_ge(s["og"], 4 * i + n + 1)
                    if n > 1:
                        act.wait_ge(s["z"], 4 * i + n - 1)
                    nc.scalar.activation(og[:, n % 2, :], psG[n % 2][:, :], ACT.Sigmoid).then_inc(s["sg"], 1)
                hold(act, s["wo"], NC * i)
                copy_z(0)
                copy_z(1)
            if ffn:
                hold(act, s["last"], j + 1)
                for k in range(KD):
                    act.wait_ge(s["xT2"], KD * j + 2 * (k // 2) + 2)
                    nc.scalar.activation(h2[:, k, 1:T + 1], psT[:, k, :], ACT.Identity, bias=t["mod"][:, SB, k:k + 1],
                                         scale=t["cb1"][:, k:k + 1]).then_inc(s["h2"], 1)
            if att:
                copy_z(2)
                copy_z(3)
            if ffn:
                hold(act, s["store"], 16 * NC * j)
                for c in range(NC):
                    act.wait_ge(s["rr"], NC * j + c + 1)
                    nc.scalar.activation(r[:, c, :], psR[c][:, :], ACT.Sigmoid).then_inc(s["rs"], 1)
            if prep:
                affine_h(act, i + 1, (0, 1) if ffn else range(KD))
            if ffn:
                for n in range(KD):
                    act.wait_ge(s["kt"], KD * j + n + 1)
                    hold(act, s["ka"], KD * j + n - 1 if n else KD * j)
                    nc.scalar.activation(relu[:, n % 2, 0, :], psK[n][:, 0:T], ACT.Relu).then_inc(s["relu"], 1)
                    act.wait_ge(s["relu"], KD * j + n + 1)
                    nc.scalar.activation(relu[:, n % 2, 1, :], relu[:, n % 2, 0, :], ACT.Square).then_inc(s["k2"], 1)
                    if prep and n in (1, 2):
                        affine_h(act, i + 1, (n + 1,))

        @block.scalar
        def _(act):
            affine_h(act, 0, range(KD))
            act.wait_ge(s["zero"], 1)
            act_tile(act, 0, True, False, True)
            act_tile(act, 1, True, True, True)
            with act.Fori(2, NT - 1) as i:
                act_tile(act, i, True, True, True)
            act_tile(act, NT - 1, True, True, False)
            act_tile(act, NT, False, True, False)

        def row_stats(dve, which, src, n, st, m, ve):
            for c in range(NC):
                last = nc.vector.bn_stats(stats[:, which, c, :], src[:, c, :])
            last.then_inc(st, 1)
            dve.wait_ge(st, n + 1)
            nc.vector.memset(tick[:, 0:1], 0.0)
            for c in range(NC):
                last = nc.vector.bn_aggr(mv[:, which, c, :], stats[:, which, c, :])
            last.then_inc(m, 1)
            dve.wait_ge(m, n + 1)
            nc.vector.tensor_scalar(var_eps[:, which, :], mv[:, which, :, 1], LN_EPS, None, ALU.add).then_inc(ve, 1)

        def split_h(dve, n):
            dve.wait_ge(s["hT"], KD * (n + 1))
            hold(dve, s["og"], 4 * n)
            nc.vector.tensor_copy(h_hi[:, :, :], hT[:, :, :]).then_inc(s["h_hi"], 1)
            dve.wait_ge(s["h_hi"], n + 1)
            nc.vector.tensor_tensor(h_lo[:, :, :], hT[:, :, :], h_hi[:, :, :].bitcast(F32),
                                    ALU.subtract).then_inc(s["h_lo"], 1)

        def norm_first(dve, n):
            dve.wait_ge(s["rstd1"], n + 1)
            for c in range(NC):
                nc.vector.tensor_scalar(xn[:, c, :], xn[:, c, :], mv[:, 0, c, 0:1], rstd[:, 0, c:c + 1], ALU.subtract,
                                        ALU.mult).then_inc(s["xn"], 1)

        def norm_second(dve, n):
            dve.wait_ge(s["rstd2"], n + 1)
            hold(dve, s["xT2"], KD * n)
            for c in range(NC):
                nc.vector.tensor_scalar(x2n[:, c, :], x1[:, c, :], mv[:, 1, c, 0:1], rstd[:, 1, c:c + 1],
                                        ALU.subtract, ALU.mult).then_inc(s["xn2"], 1)

        def shift_mix(dve, j, m, hi, lo, s_prev, s_mix, s_hi, s_lo):
            for k in range(KD):
                last = nc.vector.tensor_scalar(prev[:, k, :], h2[:, k, 0:T], t["one_minus_mu"][:, m, k:k + 1], None,
                                               ALU.mult)
            last.then_inc(s_prev, 1)
            dve.wait_ge(s_prev, j + 1)
            for k in range(KD):
                last = nc.vector.scalar_tensor_tensor(out=mix[:, k, :], in0=h2[:, k, 1:T + 1],
                                                      scalar=t["mu"][:, m, k:k + 1], in1=prev[:, k, :],
                                                      op0=ALU.mult, op1=ALU.add)
            last.then_inc(s_mix, 1)
            dve.wait_ge(s_mix, j + 1)
            nc.vector.tensor_copy(hi[:, :, :], mix[:, :, :]).then_inc(s_hi, 1)
            dve.wait_ge(s_hi, j + 1)
            nc.vector.tensor_tensor(lo[:, :, :], mix[:, :, :], hi[:, :, :].bitcast(F32), ALU.subtract).then_inc(s_lo, 1)

        def dve_tile(dve, i, att, ffn, prep):
            j = i - 1
            if prep:
                dve.wait_ge(s["xa"], 16 * (i + 2))
                row_stats(dve, 0, xn, i + 1, s["st1"], s["mv1"], s["ve1"])
            if att:
                dve.wait_ge(s["sq"], NC * (i + 1))
                nc.vector.tensor_scalar(var_eps[:, 2, :], ss[:, :], 1.0 / HID, RMS_EPS, ALU.mult,
                                        ALU.add).then_inc(s["ve3"], 1)
                for n in range(4):
                    c, half = n // 2, n % 2
                    dve.wait_ge(s["sg"], 4 * i + n + 1)
                    rows = o[:, c, half * 512:(half + 1) * 512]
                    nc.vector.tensor_tensor(rows, rows, og[:, n % 2, :], ALU.mult).then_inc(s["z"], 1)
                hold(dve, s["wo"], NC * i)
                for n in range(4):
                    c, half = n // 2, n % 2
                    dve.wait_ge(s["zh"], 4 * i + n + 1)
                    d = (slice(None), slice(4 * half, 4 * half + 4), slice(c * CH, (c + 1) * CH))
                    nc.vector.tensor_tensor(z_lo[d], psZ[n][:, :].rearrange("p (b t) -> p b t", b=4),
                                            z_hi[d].bitcast(F32), ALU.subtract).then_inc(s["zl"], 1)
            if ffn:
                dve.wait_ge(s["h2"], KD * (j + 1))
                hold(dve, s["kv"], NC * j)
                shift_mix(dve, j, 0, ra_hi, ra_lo, s["prev"], s["mixr"], s["xr_hi"], s["xr"])
                hold(dve, s["kt"], KD * j)
                dve.wait_ge(s["xr"], j + 1)
                shift_mix(dve, j, 1, xk_hi, xk_lo, s["prevk"], s["mixk"], s["xk_hi"], s["xk"])
                dve.wait_ge(s["xk"], j + 1)
                nc.vector.tensor_copy(h2[:, :, 0:1], h2[:, :, T:T + 1]).then_inc(s["last"], 1)
            if prep:
                norm_first(dve, i + 1)
            if att:
                dve.wait_ge(s["rstd3"], i + 1)
                dve.wait_ge(s["xb"], 16 * (i + 1))
                for c in range(NC):
                    dve.wait_ge(s["wo"], NC * i + c + 1)
                    nc.vector.scalar_tensor_tensor(out=x1[:, c, :], in0=psW[c][:, :], scalar=rstd[:, 2, c:c + 1],
                                                   in1=x1[:, c, :], op0=ALU.mult, op1=ALU.add).then_inc(s["x1"], 1)
                dve.wait_ge(s["x1"], NC * (i + 1))
                row_stats(dve, 1, x1, i, s["st2"], s["mv2"], s["ve2"])
            if ffn:
                dve.wait_ge(s["rr"], NC * (j + 1))
                for n in range(KD):
                    dve.wait_ge(s["k2"], KD * j + n + 1)
                    nc.vector.tensor_copy(ra_hi[:, n, :], relu[:, n % 2, 1, :]).then_inc(s["ka_hi"], 1)
                    dve.wait_ge(s["ka_hi"], KD * j + n + 1)
                    nc.vector.tensor_tensor(ra_lo[:, n, :], relu[:, n % 2, 1, :], ra_hi[:, n, :].bitcast(F32),
                                            ALU.subtract).then_inc(s["ka"], 1)
            if prep:
                split_h(dve, i + 1)
            if att:
                norm_second(dve, i)
            if ffn:
                for c in range(NC):
                    dve.wait_ge(s["kv"], NC * j + c + 1)
                    nc.vector.tensor_tensor(r[:, c, :], psR[c][:, :], r[:, c, :], ALU.mult).then_inc(s["fin1"], 1)
                    dve.wait_ge(s["fin1"], NC * j + c + 1)
                    nc.vector.tensor_tensor(r[:, c, :], x1_old[:, c, :], r[:, c, :], ALU.add).then_inc(s["fin"], 1)
            if att:
                hold(dve, s["fin"], NC * i)
                nc.vector.tensor_copy(x1_old[:, :, :], x1[:, :, :]).then_inc(s["keep"], 1)

        @block.vector
        def _(dve):
            nc.vector.memset(h2[:, :, 0:1], 0.0).then_inc(s["zero"], 1)
            dve.wait_ge(s["zero"], 1)
            nc.vector.memset(tick[:, 0:1], 0.0).then_inc(s["last"], 1)
            split_h(dve, 0)
            dve_tile(dve, 0, True, False, True)
            dve_tile(dve, 1, True, True, True)
            with dve.Fori(2, NT - 1) as i:
                dve_tile(dve, i, True, True, True)
            dve_tile(dve, NT - 1, True, True, False)
            dve_tile(dve, NT, False, True, False)

        def rsqrt(pool, which, n, ready, done):
            pool.wait_ge(ready, n + 1)
            nc.gpsimd.tensor_tensor(rstd[:, which, :], var_eps[:, which, :], t["minus_half"][:, 0:NC],
                                    ALU.pow).then_inc(done, 1)

        def pool_tile(pool, i, att, ffn, prep):
            if prep:
                rsqrt(pool, 0, i + 1, s["ve1"], s["rstd1"])
            if att:
                rsqrt(pool, 2, i, s["ve3"], s["rstd3"])
                rsqrt(pool, 1, i, s["ve2"], s["rstd2"])

        @block.gpsimd
        def _(pool):
            pool_tile(pool, 0, True, False, True)
            pool_tile(pool, 1, True, True, True)
            with pool.Fori(2, NT - 1) as i:
                pool_tile(pool, i, True, True, True)
            pool_tile(pool, NT - 1, True, True, False)


def adaln_gla_block(nc, x, wq, wk, wv, wo, wg, wog, wd, bd, norm_w, w_r, w_k, w_v, mu_r, mu_k, c, wmod, out):
    o_rows = nc.dram_tensor("o_rows_dram", (TOK, HID), F32).ap()
    x_v = x.rearrange("a (i c p) d -> (a i) p c d", c=NC, p=CH)
    out_v = out.rearrange("a (i c p) d -> (a i) p c d", c=NC, p=CH)
    o_v = o_rows.rearrange("(i c p) d -> i p c d", c=NC, p=CH)
    with ExitStack() as ctx:
        t = {}
        for name, shape, dt in (
            ("ones", [P, P], F32), ("ident", [P, P], F32), ("upto", [P, P], F32), ("after", [P, P], F32),
            ("after_r", [P, P], F32R), ("zeros", [P, 1], F32), ("minus_half", [P, 4], F32), ("bd", [H, 1], F32),
            ("mu", [P, 2, KD], F32), ("one_minus_mu", [P, 2, KD], F32), ("norm_w", [P, NP], F32),
            ("silu_c", [P, KD], F32), ("mod", [P, 6, KD], F32), ("ca1", [P, KD], F32), ("cb1", [P, KD], F32),
            ("ga", [P, KD], F32), ("gb", [P, KD], F32), ("wd_hi", [P, KD, H], F32R), ("wd_lo", [P, KD, H], F32R),
        ):
            t[name] = ctx.enter_context(nc.sbuf_tensor(f"c_{name}", shape, dt))
        small = {"c": c, "wd": wd, "bd": bd, "mu_r": mu_r, "mu_k": mu_k, "norm_w": norm_w}
        wmod_v = wmod.rearrange("(p t) (v n) -> v p t n", t=KD, v=6)

        def pair(ctx2, name, blocks, width):
            return [ctx2.enter_context(nc.sbuf_tensor(f"w_{name}_{part}", [P, blocks, width], F32R))
                    for part in ("hi", "lo")]

        def rows(w, n):
            return w.rearrange("(n r p) d -> n p r d", r=4, p=P)[n]

        with ExitStack() as first:
            W = {name: pair(first, name, KD, HID) for name in "qgkv"}
            jobs = []
            for name, w in (("q", wq), ("g", wg), ("k", wk), ("v", wv)):
                for n in range(2):
                    cols = [(*(a[:, k, n * 512:(n + 1) * 512] for a in W[name]), None) for k in range(KD)]
                    jobs.append((rows(w, n), None, cols))
                if name == "g":
                    jobs += [(wmod_v[v], v) for v in (SA, CA)]
            norm = norm_parts(nc, first, "an", 1)
            prepare(nc, t, jobs, "p", norm, x_v[0], small)
            attention_pass(nc, t, W, norm, x_v, o_v)
        with ExitStack() as second:
            W = {"og": pair(second, "og", KD, HID), "o": pair(second, "o", NP, DM)}
            for name in ("r", "k2", "v2"):
                W[name] = pair(second, name, KD, DM)
            cols = {name: [(*(a[:, k, :] for a in W[name]), None) for k in range(KD)] for name in ("r", "k2", "v2")}
            og, o = [], []
            for n in range(2):
                og.append((rows(wog, n), None, [(*(a[:, k, n * 512:(n + 1) * 512] for a in W["og"]), None)
                                                for k in range(KD)]))
                o.append((wo.rearrange("(r p) (n d) -> n p r d", p=P, n=2)[n], t["ga"],
                          [(*(a[:, 4 * n + k, :] for a in W["o"]), t["norm_w"][:, 4 * n + k:4 * n + k + 1])
                           for k in range(4)]))
            mod = {v: (wmod_v[v], v) for v in (GA, GB, SB, CB)}
            jobs = [mod[GA], mod[GB], og[0], o[0], og[1], o[1], mod[SB], mod[CB],
                    (rows(w_v, 0), t["gb"], cols["v2"]), (rows(w_r, 0), None, cols["r"]), (rows(w_k, 0), None, cols["k2"])]
            norm = norm_parts(nc, second, "bn", 3)
            prepare(nc, t, jobs, "s", norm, x_v[0])
            output_pass(nc, t, W, norm, x_v, o_v, out_v)


_INS = ["L0_attn_x", "L0_attn_Wq", "L0_attn_Wk", "L0_attn_Wv", "L0_attn_Wo", "L0_attn_Wg", "L0_attn_Wog", "L0_attn_Wd",
        "L0_attn_bd", "L0_attn_norm_w", "L0_ffn_W_r", "L0_ffn_W_k", "L0_ffn_W_v", "L0_ffn_mu_r", "L0_ffn_mu_k", "L0_c",
        "L0_wmod"]


def kernel(**inputs):
    import numpy as _np
    import concourse.bacc as _bacc
    from concourse import mybir as _mybir
    from concourse.bass_utils import run_bass_kernel_spmd as _run

    nc = _bacc.Bacc("TRN2", target_bir_lowering=False, num_devices=1)
    arrays, args = {}, []
    for name in _INS:
        a = _np.ascontiguousarray(inputs[name])
        arrays[f"in_{name}_dram"] = a
        args.append(nc.dram_tensor(f"in_{name}_dram", a.shape, _mybir.dt.from_np(a.dtype), kind="ExternalInput").ap())
    out = nc.dram_tensor("out_0_dram", (1, TOK, DM), _mybir.dt.float32, kind="ExternalOutput").ap()
    adaln_gla_block(nc, *args, out)
    r = _run(nc, [arrays], core_ids=[0])
    return r.results[0]["out_0_dram"]
```
